# Optimizing a Trainium2 kernel written in Bass

```python
import numpy as np
import jax
import jax.numpy as jnp

def _softmax(x, axis=-1):
    return jax.nn.softmax(x, axis=axis)

def _gelu(x):
    return jax.nn.gelu(x, approximate=True)

def _silu(x):
    return jax.nn.silu(x)

def _sigmoid(x):
    return jax.nn.sigmoid(x)

def _layernorm(x, axis=-1, eps=1e-05):
    m = jnp.mean(x, axis=axis, keepdims=True)
    v = jnp.var(x, axis=axis, keepdims=True)
    return (x - m) / jnp.sqrt(v + eps)

def _scatter_add(tgt, idx, src, axis=0):
    return tgt.at[idx].add(src)

def _segment_sum(src, seg, n):
    return jax.ops.segment_sum(src, seg, n)
kernel_name = 'mk_sandwich_d2_jaxref_r8_561d0c'

def setup_inputs(seed: int=0):
    np.random.seed(seed)
    _w = jnp.asarray

    def _L0_attn_setup():
        import jax, jax.numpy as jnp
        import numpy as np
        import math
        EMBED_DIM = 128
        NUM_HEADS = 16
        HEAD_DIM = EMBED_DIM // NUM_HEADS
        BLOCK = 64
        SCALE = 1.0 / math.sqrt(HEAD_DIM)

        def _flash_attn(Q, K, V):
            B, H, S, hd = Q.shape
            nkb = S // BLOCK
            Kb = K.reshape(B, H, nkb, BLOCK, hd).transpose(2, 0, 1, 3, 4)
            Vb = V.reshape(B, H, nkb, BLOCK, hd).transpose(2, 0, 1, 3, 4)
            out0 = jnp.zeros_like(Q)
            m0 = jnp.full((B, H, S, 1), -jnp.inf, dtype=Q.dtype)
            l0 = jnp.zeros((B, H, S, 1), dtype=Q.dtype)

            def body(carry, kv):
                out, m, l = carry
                K_blk, V_blk = kv
                scores = jnp.einsum('bhqd,bhkd->bhqk', Q, K_blk) * SCALE
                M_ij = scores.max(axis=-1, keepdims=True)
                m_new = jnp.maximum(m, M_ij)
                corr = jnp.exp(m - m_new)
                exp_scores = jnp.exp(scores - m_new)
                chunk_sum = exp_scores.sum(axis=-1, keepdims=True)
                l_new = chunk_sum * corr + chunk_sum
                out_new = out * corr + jnp.einsum('bhqk,bhkd->bhqd', exp_scores, V_blk)
                return ((out_new, m_new, l_new), None)
            (out, m, l), _ = jax.lax.scan(body, (out0, m0, l0), (Kb, Vb))
            return out / l
        key = jax.random.key(seed)
        ks = jax.random.split(key, 6)
        B, S, E = (4, 256, EMBED_DIM)
        std = 1.0 / math.sqrt(E)
        return {'x': jax.random.normal(ks[0], (B, S, E), dtype=jnp.float32), 'q_w': jax.random.normal(ks[1], (E, E), dtype=jnp.float32) * std, 'k_w': jax.random.normal(ks[2], (E, E), dtype=jnp.float32) * std, 'v_w': jax.random.normal(ks[3], (E, E), dtype=jnp.float32) * std, 'out_w': jax.random.normal(ks[4], (E, E), dtype=jnp.float32) * std, 'out_b': jnp.zeros((E,), dtype=jnp.float32)}
    _L0_attn_in = _L0_attn_setup()

    def _L0_ffn_setup():
        import jax, jax.numpy as jnp
        import numpy as np
        D_IN, D_HID = (128, 512)

        def _ternary(key, shape):
            return jax.random.randint(key, shape, -1, 2).astype(jnp.float32)

        def _tlin(x, w, s):
            return jnp.einsum('bsi,oi->bso', x, w) * s
        key = jax.random.key(seed)
        ks = jax.random.split(key, 12)
        inv = lambda fan: 1.0 / np.sqrt(fan).astype(np.float32)
        return {'x': jax.random.normal(ks[0], (4, 256, D_IN), dtype=jnp.float32), 'w1_w': _ternary(ks[1], (D_HID, D_IN)), 'w1_s': jax.random.uniform(ks[2], (D_HID,), dtype=jnp.float32) * inv(D_IN), 'w2_w': _ternary(ks[3], (D_HID, D_IN)), 'w2_s': jax.random.uniform(ks[4], (D_HID,), dtype=jnp.float32) * inv(D_IN), 'h1_w': _ternary(ks[5], (D_HID, D_HID)), 'h1_s': jax.random.uniform(ks[6], (D_HID,), dtype=jnp.float32) * inv(D_HID), 'h2_w': _ternary(ks[7], (D_HID, D_HID)), 'h2_s': jax.random.uniform(ks[8], (D_HID,), dtype=jnp.float32) * inv(D_HID), 'w3_w': _ternary(ks[9], (D_IN, D_HID)), 'w3_s': jax.random.uniform(ks[10], (D_IN,), dtype=jnp.float32) * inv(D_HID)}
    _L0_ffn_in = _L0_ffn_setup()

    def _L1_attn_setup():
        import jax, jax.numpy as jnp
        import numpy as np
        B, S, D, H = (4, 512, 128, 8)
        HD = D // H
        key = jax.random.key(seed)
        k1, k2, k3 = jax.random.split(key, 3)
        x = jax.random.normal(k1, (B, S, D), dtype=jnp.float32)
        w_qkv = jax.random.normal(k2, (D, 3 * D), dtype=jnp.float32) * (1.0 / np.sqrt(D))
        w_out = jax.random.normal(k3, (D, D), dtype=jnp.float32) * (1.0 / np.sqrt(D))
        return {'x': x, 'w_qkv': w_qkv, 'w_out': w_out}
    _L1_attn_in = _L1_attn_setup()

    def _L1_ffn_setup():
        import jax, jax.numpy as jnp
        import numpy as np
        B, S, H, F, E = (1, 256, 128, 256, 8)

        def _swiglu(x, wg, wu, wd):
            return jax.nn.silu(x @ wg.T) * (x @ wu.T) @ wd.T
        key = jax.random.key(seed)
        ks = jax.random.split(key, 8)
        sc = 1.0 / np.sqrt(H)
        scf = 1.0 / np.sqrt(F)
        return {'hidden_states': jax.random.normal(ks[0], (B, S, H), jnp.float32), 'gate_w': jax.random.normal(ks[1], (E, H), jnp.float32) * sc, 'shared_gate': jax.random.normal(ks[2], (F, H), jnp.float32) * sc, 'shared_up': jax.random.normal(ks[3], (F, H), jnp.float32) * sc, 'shared_down': jax.random.normal(ks[4], (H, F), jnp.float32) * scf, 'r_gate': jax.random.normal(ks[5], (E, F, H), jnp.float32) * sc, 'r_up': jax.random.normal(ks[6], (E, F, H), jnp.float32) * sc, 'r_down': jax.random.normal(ks[7], (E, H, F), jnp.float32) * scf}
    _L1_ffn_in = _L1_ffn_setup()
    _d = {'L0_attn_x': _L0_attn_in['x'], 'L0_attn_q_w': _L0_attn_in['q_w'], 'L0_attn_k_w': _L0_attn_in['k_w'], 'L0_attn_v_w': _L0_attn_in['v_w'], 'L0_attn_out_w': _L0_attn_in['out_w'], 'L0_attn_out_b': _L0_attn_in['out_b'], 'L0_ffn_w1_w': _L0_ffn_in['w1_w'], 'L0_ffn_w1_s': _L0_ffn_in['w1_s'], 'L0_ffn_w2_w': _L0_ffn_in['w2_w'], 'L0_ffn_w2_s': _L0_ffn_in['w2_s'], 'L0_ffn_h1_w': _L0_ffn_in['h1_w'], 'L0_ffn_h1_s': _L0_ffn_in['h1_s'], 'L0_ffn_h2_w': _L0_ffn_in['h2_w'], 'L0_ffn_h2_s': _L0_ffn_in['h2_s'], 'L0_ffn_w3_w': _L0_ffn_in['w3_w'], 'L0_ffn_w3_s': _L0_ffn_in['w3_s'], 'L1_attn_w_qkv': _L1_attn_in['w_qkv'], 'L1_attn_w_out': _L1_attn_in['w_out'], 'L1_ffn_gate_w': _L1_ffn_in['gate_w'], 'L1_ffn_shared_gate': _L1_ffn_in['shared_gate'], 'L1_ffn_shared_up': _L1_ffn_in['shared_up'], 'L1_ffn_shared_down': _L1_ffn_in['shared_down'], 'L1_ffn_r_gate': _L1_ffn_in['r_gate'], 'L1_ffn_r_up': _L1_ffn_in['r_up'], 'L1_ffn_r_down': _L1_ffn_in['r_down']}
    _x0 = _d['L0_attn_x']
    _d['L0_attn_x'] = jax.random.normal(jax.random.fold_in(jax.random.key(seed), 1), (16, 512, 128), dtype=_x0.dtype)
    del _x0
    return _d

def reference(L0_attn_x, L0_attn_q_w, L0_attn_k_w, L0_attn_v_w, L0_attn_out_w, L0_attn_out_b, L0_ffn_w1_w, L0_ffn_w1_s, L0_ffn_w2_w, L0_ffn_w2_s, L0_ffn_h1_w, L0_ffn_h1_s, L0_ffn_h2_w, L0_ffn_h2_s, L0_ffn_w3_w, L0_ffn_w3_s, L1_attn_w_qkv, L1_attn_w_out, L1_ffn_gate_w, L1_ffn_shared_gate, L1_ffn_shared_up, L1_ffn_shared_down, L1_ffn_r_gate, L1_ffn_r_up, L1_ffn_r_down):

    def _L0_attn_ref(x, q_w, k_w, v_w, out_w, out_b):
        import jax, jax.numpy as jnp
        import numpy as np
        import math
        EMBED_DIM = 128
        NUM_HEADS = 16
        HEAD_DIM = EMBED_DIM // NUM_HEADS
        BLOCK = 64
        SCALE = 1.0 / math.sqrt(HEAD_DIM)

        def _flash_attn(Q, K, V):
            B, H, S, hd = Q.shape
            nkb = S // BLOCK
            Kb = K.reshape(B, H, nkb, BLOCK, hd).transpose(2, 0, 1, 3, 4)
            Vb = V.reshape(B, H, nkb, BLOCK, hd).transpose(2, 0, 1, 3, 4)
            out0 = jnp.zeros_like(Q)
            m0 = jnp.full((B, H, S, 1), -jnp.inf, dtype=Q.dtype)
            l0 = jnp.zeros((B, H, S, 1), dtype=Q.dtype)

            def body(carry, kv):
                out, m, l = carry
                K_blk, V_blk = kv
                scores = jnp.einsum('bhqd,bhkd->bhqk', Q, K_blk) * SCALE
                M_ij = scores.max(axis=-1, keepdims=True)
                m_new = jnp.maximum(m, M_ij)
                corr = jnp.exp(m - m_new)
                exp_scores = jnp.exp(scores - m_new)
                chunk_sum = exp_scores.sum(axis=-1, keepdims=True)
                l_new = chunk_sum * corr + chunk_sum
                out_new = out * corr + jnp.einsum('bhqk,bhkd->bhqd', exp_scores, V_blk)
                return ((out_new, m_new, l_new), None)
            (out, m, l), _ = jax.lax.scan(body, (out0, m0, l0), (Kb, Vb))
            return out / l
        B, S, E = x.shape
        H, hd = (NUM_HEADS, HEAD_DIM)

        def split_heads(t):
            return t.reshape(B, S, H, hd).transpose(0, 2, 1, 3)
        Q = split_heads(x @ q_w.T)
        K = split_heads(x @ k_w.T)
        V = split_heads(x @ v_w.T)
        out = _flash_attn(Q, K, V)
        out = out.transpose(0, 2, 1, 3).reshape(B, S, E)
        return out @ out_w.T + out_b

    def _L0_ffn_ref(x, w1_w, w1_s, w2_w, w2_s, h1_w, h1_s, h2_w, h2_s, w3_w, w3_s):
        import jax, jax.numpy as jnp
        import numpy as np
        D_IN, D_HID = (128, 512)

        def _ternary(key, shape):
            return jax.random.randint(key, shape, -1, 2).astype(jnp.float32)

        def _tlin(x, w, s):
            return jnp.einsum('bsi,oi->bso', x, w) * s
        h = jax.nn.silu(_tlin(x, w1_w, w1_s)) * _tlin(x, w2_w, w2_s)
        h = jax.nn.gelu(_tlin(h, h1_w, h1_s), approximate=False)
        h = jax.nn.gelu(_tlin(h, h2_w, h2_s), approximate=False)
        return _tlin(h, w3_w, w3_s)

    def _L1_attn_ref(x, w_qkv, w_out):
        import jax, jax.numpy as jnp
        import numpy as np
        B, S, D, H = (4, 512, 128, 8)
        HD = D // H
        b, s, d = x.shape
        qkv = x @ w_qkv
        q, k, v = jnp.split(qkv, 3, axis=-1)
        q = q.reshape(b, s, H, HD)
        k = k.reshape(b, s, H, HD)
        v = v.reshape(b, s, H, HD)
        fq = jnp.fft.fft(q, axis=-1)
        fk = jnp.fft.fft(k, axis=-1)
        fv = jnp.fft.fft(v, axis=-1)
        kv = fk * fv
        kv = jnp.cumsum(kv, axis=1)
        vals = jnp.fft.ifft(kv * jnp.conj(fq), axis=-1).real.astype(x.dtype)
        vals = vals.reshape(b, s, d)
        return vals @ w_out

    def _L1_ffn_ref(hidden_states, gate_w, shared_gate, shared_up, shared_down, r_gate, r_up, r_down):
        import jax, jax.numpy as jnp
        import numpy as np
        B, S, H, F, E = (1, 256, 128, 256, 8)

        def _swiglu(x, wg, wu, wd):
            return jax.nn.silu(x @ wg.T) * (x @ wu.T) @ wd.T
        b, s, h = hidden_states.shape
        x = hidden_states.reshape(-1, h)
        shared_out = _swiglu(x, shared_gate, shared_up, shared_down)
        logits = x @ gate_w.T
        top_id = jnp.argmax(logits, axis=-1)
        score = jax.nn.sigmoid(jnp.max(logits, axis=-1))
        xs = x * score[:, None]

        def body(acc, ws):
            wg, wu, wd, e = ws
            xe = jnp.where((top_id == e)[:, None], xs, 0.0)
            return (acc + _swiglu(xe, wg, wu, wd), None)
        acc0 = jnp.zeros_like(x)
        routed_out, _ = jax.lax.scan(body, acc0, (r_gate, r_up, r_down, jnp.arange(E)))
        return (shared_out + routed_out).reshape(b, s, h)
    x = L0_attn_x
    x = x + _layernorm(_L0_attn_ref(_layernorm(x, axis=-1), L0_attn_q_w, L0_attn_k_w, L0_attn_v_w, L0_attn_out_w, L0_attn_out_b), axis=-1)
    x = x + _layernorm(_L0_ffn_ref(_layernorm(x, axis=-1), L0_ffn_w1_w, L0_ffn_w1_s, L0_ffn_w2_w, L0_ffn_w2_s, L0_ffn_h1_w, L0_ffn_h1_s, L0_ffn_h2_w, L0_ffn_h2_s, L0_ffn_w3_w, L0_ffn_w3_s), axis=-1)
    x = x + _layernorm(_L1_attn_ref(_layernorm(x, axis=-1), L1_attn_w_qkv, L1_attn_w_out), axis=-1)
    x = x + _layernorm(_L1_ffn_ref(_layernorm(x, axis=-1), L1_ffn_gate_w, L1_ffn_shared_gate, L1_ffn_shared_up, L1_ffn_shared_down, L1_ffn_r_gate, L1_ffn_r_up, L1_ffn_r_down), axis=-1)
    return x

_drawn_inputs = setup_inputs


def setup_inputs(seed=0):
    import zlib

    import numpy as np

    out = dict(_drawn_inputs(seed))
    spreads = {'L0_attn_out_b': (0.0, 0.1)}
    factors = {}
    for name, (base, spread) in spreads.items():
        noise = np.random.default_rng([zlib.crc32(name.encode()), seed]).standard_normal(out[name].shape)
        drawn = base * np.exp(spread * noise) if base else spread * noise
        out[name] = jnp.asarray(drawn.astype(out[name].dtype))
    for name, factor in factors.items():
        out[name] = (out[name] * factor).astype(out[name].dtype)
    return out
```

```python
from contextlib import ExitStack

import concourse.bass as bass
from concourse import mybir

P = 128
F32 = mybir.dt.float32
BF16 = mybir.dt.bfloat16
I32 = mybir.dt.int32
U32 = mybir.dt.uint32
ALU = mybir.AluOpType
ACT = mybir.ActivationFunctionType
AX_X = mybir.AxisListType.X
ds = bass.ds

EPS = 1e-5
HD = 8
NPART = 3
ROWS = NPART * NPART * HD
KROWS = ROWS + NPART
BLK = 64
LN_STEPS = 13
NE = 8


def late(c, k):
    return not isinstance(c, int) or c >= k


def run_stages(eng, n, stages):
    most = max(lag for lag, _ in stages)
    peel = most + 2 + most % 2
    for c in range(peel):
        for lag, stage in stages:
            if 0 <= c - lag < n:
                stage(c - lag, (c - lag) % 2)
    with eng.Fori(peel // 2, n // 2) as u:
        r = u * 2
        for s in range(2):
            for lag, stage in stages:
                k = s - lag
                stage(r + k if k > 0 else r - (-k) if k < 0 else r, k % 2)
    for c in range(n, n + most):
        for lag, stage in stages:
            if c - lag < n:
                stage(c - lag, (c - lag) % 2)


def block_kernel(nc, io, out):
    B, S, E = io["L0_attn_x"].shape
    NCH = B
    NT = S // P
    TILES = NCH * NT
    H0 = E // HD
    HG = 4
    NG = H0 // HG
    SCALE = 1.0 / float(HD) ** 0.5
    NB = S // BLK
    DH = io["L0_ffn_h1_w"].shape[0]
    FB = DH // P
    F1 = io["L1_ffn_shared_gate"].shape[1]
    FB1 = F1 // P
    ST_TILES = TILES + NE
    assert (E, S, NT, FB, FB1) == (P, 512, 4, 4, 2)

    q_scr = nc.dram_tensor("q_scr", (B, H0, 5, HD, S), BF16).ap()
    k_scr = nc.dram_tensor("k_scr", (B, H0, NPART, HD, S), BF16).ap()
    xs_scr = nc.dram_tensor("xs_scr", (ST_TILES * P, E), F32).ap()
    y_scr = nc.dram_tensor("y_scr", (ST_TILES * P, E), F32).ap()
    x_dram = io["L0_attn_x"]

    top = ExitStack()
    with top:
        def sem(name):
            return top.enter_context(nc.semaphore(name))

        def sb(name, shape, dt=F32, ctx=top):
            return ctx.enter_context(nc.sbuf_tensor(name, shape, dt))

        PS = top.enter_context(nc.psum_tensor("PS", [P, 8, 512], F32))
        X = sb("X", [P, TILES * E])
        AO = sb("AO", [P, TILES * E])
        idf = sb("idf", [P, P])
        idb = sb("idb", [P, P], BF16)
        neg_half = sb("neg_half", [P, NT])
        const_in = sem("const_in")
        held = sem("held")
        ones_set = sem("ones_set")

        def settled(eng):
            eng.sem_inc(held, 1)

        def ln_bufs(name, ctx):
            return dict(st=sb(name + "_st", [P, NT, 6], F32, ctx), mv=sb(name + "_mv", [P, NT, 2], F32, ctx),
                        ve=sb(name + "_ve", [P, NT], F32, ctx), rs=sb(name + "_rs", [P, NT], F32, ctx),
                        steps=sem(name + "_steps"), rstd=sem(name + "_rstd"))

        def layernorm(dve, c, ln, src, dst, last=None):
            steps, base = ln["steps"], c * LN_STEPS
            settled(dve)
            for t in range(NT):
                dve.bn_stats(ln["st"][:, t, :], src(t)).then_inc(steps, 1)
            dve.wait_ge(steps, base + 4)
            settled(dve)
            for t in range(NT):
                dve.bn_aggr(ln["mv"][:, t, :], ln["st"][:, t, :]).then_inc(steps, 1)
            dve.wait_ge(steps, base + 8)
            dve.tensor_scalar(ln["ve"][:], ln["mv"][:, :, 1], EPS, None, ALU.add).then_inc(steps, 1)
            dve.wait_ge(ln["rstd"], c + 1)
            for t in range(NT):
                dve.tensor_scalar(dst(t), src(t), ln["mv"][:, t, 0:1], ln["rs"][:, t:t + 1],
                                  ALU.subtract, ALU.mult).then_inc(steps, 1)

        def rstd(ln):
            def stage(pool, c):
                pool.wait_ge(ln["steps"], c * LN_STEPS + 9)
                pool.tensor_tensor(ln["rs"][:], ln["ve"][:], neg_half[:], ALU.pow).then_inc(ln["rstd"], 1)
            return stage

        def tile_of(buf, c, t):
            return buf[:, ds(c * (NT * E) + t * E, E)]

        def chunk_of(buf, c):
            return buf[:, ds(c * (NT * E), NT * E)]

        att = ExitStack()
        V = sb("V", [P, TILES * E], F32, att)
        p1 = ExitStack()
        wq = sb("wq", [P, P], F32, p1)
        wk = sb("wk", [P, P], F32, p1)
        wv = sb("wv", [P, P], F32, p1)
        zero = sb("zero", [P, 1024], F32, p1)
        xn1 = sb("xn1", [P, 2, S], F32, p1)
        xT1 = sb("xT1", [P, 2, S], F32, p1)
        parts = sb("parts", [P, 2, NPART, 2 * S], BF16, p1)
        resid = sb("resid", [P, 2, 2 * S], F32, p1)
        ln1 = ln_bufs("ln1", p1)
        x_in = [sem("x_in0"), sem("x_in1")]
        zero_out = sem("zero_out")
        turned1 = sem("turned1")
        xT1_set = sem("xT1_set")
        qk_done = sem("qk_done")
        v_done = sem("v_done")
        part1_set = sem("part1_set")
        v_set = sem("v_set")
        split_steps = sem("split_steps")
        part3_set = sem("part3_set")
        parts_out = [sem("parts_out0"), sem("parts_out1")]
        PARTS_DMA = 8 * 16

        with nc.Block() as block:
            @block.sync
            def _(sp):
                sp.dma_start(idf[:], io["ident"]).then_inc(const_in, 16)
                sp.dma_start(wq[:], io["L0_attn_q_w"]).then_inc(const_in, 16)
                sp.dma_start(wk[:], io["L0_attn_k_w"]).then_inc(const_in, 16)
                sp.dma_start(wv[:], io["L0_attn_v_w"]).then_inc(const_in, 16)

                def load(c, s):
                    if late(c, 2):
                        sp.wait_ge(x_in[s], (c - s) * 8)
                    sp.dma_start(chunk_of(X, c).rearrange("p (t e) -> p t e", t=NT),
                                 x_dram[ds(c, 1)].rearrange("b (t p) e -> p (b t) e", p=P)).then_inc(x_in[s], 16)

                def store_parts(c, s):
                    sp.wait_ge(part3_set, c + 1)
                    sp.wait_ge(split_steps, 2 * c + 2)
                    for j in range(5):
                        sp.dma_start(q_scr[ds(c, 1), :, j].rearrange("b h d t -> (b h) d t"),
                                     parts[:, s, j % NPART, 0:S]).then_inc(parts_out[s], 16)
                    for j in range(NPART):
                        sp.dma_start(k_scr[ds(c, 1), :, j].rearrange("b h d t -> (b h) d t"),
                                     parts[:, s, j, S:2 * S]).then_inc(parts_out[s], 16)
                run_stages(sp, NCH, [(0, load), (2, store_parts)])
                for s in range(2):
                    sp.wait_ge(parts_out[s], NCH // 2 * PARTS_DMA)

            @block.tensor
            def _(pe):
                pe.wait_ge(const_in, 64)

                def turn(c, s):
                    pe.wait_ge(ln1["steps"], c * LN_STEPS + LN_STEPS)
                    if late(c, 2):
                        pe.wait_ge(xT1_set, c - 1)
                    for t in range(NT):
                        mm = pe.transpose(PS[:, s, t * P:(t + 1) * P], xn1[:, s, t * P:(t + 1) * P], idf[:])
                    mm.then_inc(turned1, 1)

                def project(c, s):
                    pe.wait_ge(xT1_set, c + 1)
                    if late(c, 1):
                        pe.wait_ge(split_steps, 2 * c)
                    pe.matmul(PS[:, 2, :], wq[:], xT1[:, s, :], start=True, stop=True)
                    pe.matmul(PS[:, 3, :], wk[:], xT1[:, s, :], start=True, stop=True).then_inc(qk_done, 1)
                    if late(c, 2):
                        pe.wait_ge(v_set, c - 1)
                    for t in range(NT):
                        mm = pe.matmul(PS[:, 4 + s, t * P:(t + 1) * P], xT1[:, s, t * P:(t + 1) * P], wv[:],
                                       start=True, stop=True)
                    mm.then_inc(v_done, 1)

                run_stages(pe, NCH, [(0, turn), (1, project)])

            @block.scalar
            def _(act):
                def copy_xT(c, s):
                    act.wait_ge(turned1, c + 1)
                    if late(c, 2):
                        act.wait_ge(v_done, c - 1)
                    act.copy(xT1[:, s, :], PS[:, s, :]).then_inc(xT1_set, 1)

                def cast(c, s):
                    act.wait_ge(qk_done, c + 1)
                    if late(c, 2):
                        act.wait_ge(parts_out[s], (c - s) * (PARTS_DMA // 2))
                        act.wait_ge(part3_set, c - 1)
                    act.copy(parts[:, s, 0, :], PS[:, 2:4, :].rearrange("p a b -> p (a b)")).then_inc(part1_set, 1)
                    act.wait_ge(v_done, c + 1)
                    act.copy(chunk_of(V, c), PS[:, 4 + s, :]).then_inc(v_set, 1)

                run_stages(act, NCH, [(0, copy_xT), (1, cast)])

            @block.gpsimd
            def _(pool):
                pool.wait_ge(ones_set, 4)
                flat = xs_scr.rearrange("(n p a) e -> n p (a e)", p=P, a=8)
                for n in range(ST_TILES // 8):
                    pool.dma_start(flat[n], zero[:]).then_inc(zero_out, 16)

                def third(c, s):
                    pool.wait_ge(split_steps, 2 * c + 2)
                    if late(c, 2):
                        pool.wait_ge(parts_out[s], (c - s) * (PARTS_DMA // 2))
                    pool.tensor_tensor(parts[:, s, 2, :], resid[:, s, :], parts[:, s, 1, :],
                                       ALU.subtract).then_inc(part3_set, 1)
                run_stages(pool, NCH, [(0, lambda c, s: rstd(ln1)(pool, c)), (1, third)])
                pool.wait_ge(zero_out, 16 * (ST_TILES // 8))

            @block.vector
            def _(dve):
                dve.memset(zero[:], 0.0).then_inc(ones_set, 1)
                dve.memset(neg_half[:], -0.5).then_inc(ones_set, 1)
                dve.memset(PS[:, 6:8, :], 0.0).then_inc(ones_set, 1)
                dve.wait_ge(const_in, 64)
                dve.tensor_copy(idb[:], idf[:]).then_inc(ones_set, 1)

                def norm(c, s):
                    dve.wait_ge(x_in[s], (c - s) * 8 + 16)
                    if late(c, 2):
                        dve.wait_ge(turned1, c - 1)
                    layernorm(dve, c, ln1, lambda t: tile_of(X, c, t), lambda t: xn1[:, s, t * P:(t + 1) * P])

                def split(c, s):
                    dve.wait_ge(part1_set, c + 1)
                    if late(c, 2):
                        dve.wait_ge(part3_set, c - 1)
                        dve.wait_ge(parts_out[s], (c - s) * (PARTS_DMA // 2))
                    dve.tensor_tensor(resid[:, s, :], PS[:, 2:4, :].rearrange("p a b -> p (a b)"),
                                      parts[:, s, 0, :], ALU.subtract).then_inc(split_steps, 1)
                    dve.wait_ge(split_steps, 2 * c + 1)
                    dve.tensor_copy(parts[:, s, 1, :], resid[:, s, :]).then_inc(split_steps, 1)

                run_stages(dve, NCH, [(0, norm), (1, split)])
        p1.close()

        p2 = ExitStack()
        QR = sb("QR", [KROWS, NG, HG, S], BF16, p2)
        KR = sb("KR", [KROWS, NG, HG, S], BF16, p2)
        EX = sb("EX", [P, 2, HG, S], F32, p2)
        VS = sb("VS", [P, NG, NT, HG, HD + 1], F32, p2)
        OT = sb("OT", [P, S], F32, p2)
        bmax = sb("bmax", [P, 2, NT * HG, NB], F32, p2)
        m_prev = sb("m_prev", [P, NT * HG], F32, p2)
        m_all = sb("m_all", [P, NT * HG], F32, p2)
        m_res = sb("m_res", [P, NT * HG], F32, p2)
        m_diff = sb("m_diff", [P, 2, NT * HG], F32, p2)
        m_part = sb("m_part", [P, 2, NPART, NT * HG], BF16, p2)
        m_row = sb("m_row", [NPART * NT * HG, 2, P], BF16, p2)
        corr = sb("corr", [P, NG, NT * HG], F32, p2)
        den = sb("den", [P, NT * HG], F32, p2)
        rden = sb("rden", [P, NT * HG], F32, p2)
        load_in = [sem(f"load_in{i}") for i in range(NG)]
        mrow_in = [sem("mrow_in0"), sem("mrow_in1")]
        kones = sem("kones")
        vs_preset = sem("vs_preset")
        vs_set = sem("vs_set")
        pair_done = sem("pair_done")
        pair_max = sem("pair_max")
        st_done = sem("st_done")
        ex_set = sem("ex_set")
        pv_done = sem("pv_done")
        max_steps = sem("max_steps")
        mt_done = sem("mt_done")
        mrow_set = sem("mrow_set")
        corr_set = sem("corr_set")
        ot_set = sem("ot_set")
        ot_turned = sem("ot_turned")
        nrm_steps = sem("nrm_steps")
        MAX_STEPS = 7
        GROUPS = NCH * NG

        def run_groups(eng, step, tail):
            for i in range(NG):
                step(0, i, i, lambda k, i=i: i >= k)
            with eng.Fori(1, NCH) as c:
                for i in range(NG):
                    step(c, i, c * NG + i, lambda k: True)
            for g in range(GROUPS, GROUPS + tail):
                step(None, g % NG, g, lambda k, g=g: g - k < GROUPS)

        def at(c, i, g, k):
            if c is None or isinstance(c, int):
                return (g - k) // NG, (g - k) % NG
            return (c - 1 if i - k < 0 else c), (i - k) % NG

        with nc.Block() as block:
            @block.sync
            def _(sp):
                sp.wait_ge(kones, 1)

                def load(c, i, g):
                    for a in range(NPART):
                        rows = slice(a * NPART * HD, (a + 1) * NPART * HD)
                        sp.dma_start(QR[rows, i, :, :],
                                     q_scr[ds(c, 1), i * HG:(i + 1) * HG, a:a + NPART]
                                     .rearrange("b h j d t -> (j d) (b h) t")).then_inc(load_in[i], 16)
                        sp.dma_start(KR[rows, i, :, :],
                                     k_scr[ds(c, 1), i * HG:(i + 1) * HG]
                                     .rearrange("b h j d t -> (j d) (b h) t")).then_inc(load_in[i], 16)

                def load_max(c, i, g, k):
                    _, j = at(c, i, g, k)
                    sp.wait_ge(mrow_set, g - k + 1)
                    sp.dma_start(QR[ROWS:KROWS, j].rearrange("r h q -> r (h q)"),
                                 m_row[:, j % 2, :]).then_inc(mrow_in[j % 2], 16)

                def step(c, i, g, has):
                    if has(0):
                        if has(4):
                            sp.wait_ge(st_done, (g - 3) * 16)
                        load(c, i, g)
                    if has(2):
                        load_max(c, i, g, 2)
                run_groups(sp, step, 2)

            @block.tensor
            def _(pe):
                def score_half(c, i, g, n):
                    t, h = n // HG, n % HG
                    pair = n // 2
                    if n == 0:
                        pe.wait_ge(load_in[i], c * 96 + 96)
                    if n % 2 == 0 and not (isinstance(g, int) and g == 0 and pair < 2):
                        pe.wait_ge(pair_max, g * 8 + pair - 1)
                    mm = pe.matmul(PS[:, 2 * (pair % 2) + n % 2, :], QR[0:ROWS, i, h, t * P:(t + 1) * P],
                                   KR[0:ROWS, i, h, :], start=True, stop=True)
                    if n % 2 == 1:
                        mm.then_inc(pair_done, 1)

                def score_T(j, g, n):
                    kt, h = n // HG, n % HG
                    if n == 0:
                        pe.wait_ge(mrow_in[j % 2], (g - j % 2) * 8 + 16)
                    if not (isinstance(g, int) and g == 0 and n < 2):
                        pe.wait_ge(ex_set, g * 16 + n - 1)
                    pe.matmul(PS[:, 4 + n % 2, :], KR[:, j, h, kt * P:(kt + 1) * P], QR[:, j, h, :],
                              start=True, stop=True).then_inc(st_done, 1)

                def pv(j, g, kt):
                    pe.wait_ge(ex_set, g * 16 + 4 * kt + 4)
                    if kt == 0:
                        pe.wait_ge(vs_set, g + 1)
                    if kt == 0 and not (isinstance(g, int) and g == 0):
                        pe.wait_ge(ot_set, g)
                    for h in range(HG):
                        mm = pe.matmul(PS[32 * h:32 * h + HD + 1, 6, :], VS[:, j, kt, h, :],
                                       EX[:, kt % 2, h, :], start=(kt == 0), stop=(kt == NT - 1))
                    mm.then_inc(pv_done, 1)

                def turn_max(i, g):
                    pe.wait_ge(max_steps, (g + 1) * MAX_STEPS)
                    if not (isinstance(g, int) and g < 3):
                        pe.wait_ge(nrm_steps, (g - 2) * 3)
                    settled(pe)
                    pe.transpose(PS[0:NPART * NT * HG, 7, 0:P // 2].bitcast(BF16),
                                 m_part[:, i % 2].rearrange("p a b -> p (a b)"), idb[:]).then_inc(mt_done, 1)

                def turn_out(g):
                    pe.wait_ge(ot_set, g + 1)
                    pe.wait_ge(mrow_set, min(g + 3, GROUPS) if isinstance(g, int) else g + 3)
                    if isinstance(g, int) and g + 3 > GROUPS:
                        pe.wait_ge(nrm_steps, g * 3)
                    for t in range(NT):
                        mm = pe.transpose(PS[:, 7, t * P:(t + 1) * P], OT[:, t * P:(t + 1) * P], idf[:])
                    mm.then_inc(ot_turned, 1)

                def step(c, i, g, has):
                    for q in range(NT):
                        for n in range(4 * q, 4 * q + 4):
                            if has(0):
                                score_half(c, i, g, n)
                            if has(2):
                                score_T((i - 2) % NG, g - 2, n)
                        if q == 0 and has(3):
                            pv((i - 3) % NG, g - 3, NT - 1)
                        if q > 0 and has(2):
                            pv((i - 2) % NG, g - 2, q - 1)
                        if q == 1 and has(1):
                            turn_max((i - 1) % NG, g - 1)
                        if q == 2 and has(3):
                            turn_out(g - 3)
                run_groups(pe, step, 3)

            @block.scalar
            def _(act):
                def exps(g, n):
                    act.wait_ge(st_done, g * 16 + n + 1)
                    kt, h = n // HG, n % HG
                    if h == 0 and not (isinstance(g, int) and g == 0 and kt < 2):
                        act.wait_ge(pv_done, g * 4 + kt - 1)
                    act.activation(EX[:, kt % 2, h, :], PS[:, 4 + n % 2, :], ACT.Exp,
                                   scale=SCALE).then_inc(ex_set, 1)

                def copy_out(g):
                    act.wait_ge(pv_done, g * 4 + 4)
                    if not (isinstance(g, int) and g == 0):
                        act.wait_ge(ot_turned, g)
                    act.copy(OT[:], PS[:, 6, :]).then_inc(ot_set, 1)

                def correction(i, g):
                    act.wait_ge(max_steps, (g + 1) * MAX_STEPS)
                    if not (isinstance(g, int) and g < NG):
                        act.wait_ge(nrm_steps, (g - 3) * 3)
                    act.activation(corr[:, i, :], m_diff[:, i % 2, :], ACT.Exp, scale=SCALE).then_inc(corr_set, 1)

                def copy_rows(i, g):
                    act.wait_ge(mt_done, g + 1)
                    if not (isinstance(g, int) and g < 2):
                        act.wait_ge(mrow_in[i % 2], (g - i % 2) * 8)
                    act.copy(m_row[:, i % 2, :],
                             PS[0:NPART * NT * HG, 7, 0:P // 2].bitcast(BF16)).then_inc(mrow_set, 1)

                def step(c, i, g, has):
                    for q in range(NT):
                        if has(2):
                            for n in range(4 * q, 4 * q + 4):
                                exps(g - 2, n)
                        if q == 0 and has(3):
                            copy_out(g - 3)
                        if q == 1 and has(1):
                            correction((i - 1) % NG, g - 1)
                            copy_rows((i - 1) % NG, g - 1)
                run_groups(act, step, 3)

            @block.gpsimd
            def _(pool):
                pool.wait_ge(vs_preset, 2)

                def stage_values(c, i, g):
                    if not (isinstance(g, int) and g < NG):
                        pool.wait_ge(pv_done, (g - NG + 1) * 4)
                    src = chunk_of(V, c).rearrange("p (t x) -> p t x", t=NT)[:, :, i * HG * HD:(i + 1) * HG * HD]
                    pool.tensor_copy(VS[:, i, :, :, 0:HD],
                                     src.rearrange("p t (h d) -> p t h d", d=HD)).then_inc(vs_set, 1)

                def step(c, i, g, has):
                    if has(0):
                        stage_values(c, i, g)
                run_groups(pool, step, 0)

            @block.vector
            def _(dve):
                dve.memset(KR[BLK:KROWS], 1.0).then_inc(kones, 1)
                dve.memset(VS[:], 0.0).then_inc(vs_preset, 1)
                dve.wait_ge(vs_preset, 1)
                dve.memset(VS[BLK:P, :, NT - 1, :, HD], 1.0).then_inc(vs_preset, 1)

                def pair_reduce(i, g, u):
                    t, v = u // 2, u % 2
                    dve.wait_ge(pair_done, g * 8 + u + 1)
                    rows = bmax[:, i % 2].rearrange("p (h t) b -> p h t b", t=NT)
                    dve.tensor_reduce(rows[:, 2 * v:2 * v + 2, t, :],
                                      PS[:, 2 * (u % 2):2 * (u % 2) + 2, :].rearrange("p h (b k) -> p h b k", k=BLK),
                                      AX_X, ALU.max).then_inc(pair_max, 1)

                def max_chain(i, g):
                    base = g * MAX_STEPS
                    s = i % 2
                    dve.wait_ge(pair_max, g * 8 + 8)
                    dve.tensor_reduce(m_prev[:], bmax[:, s, :, 0:NB - 1], AX_X, ALU.max).then_inc(max_steps, 1)
                    dve.wait_ge(max_steps, base + 1)
                    dve.tensor_tensor(m_all[:], m_prev[:], bmax[:, s, :, NB - 1], ALU.max).then_inc(max_steps, 1)
                    dve.wait_ge(max_steps, base + 2)
                    if not (isinstance(g, int) and g < 2):
                        dve.wait_ge(mt_done, g - 1)
                        dve.wait_ge(corr_set, g - 1)
                    dve.tensor_scalar(m_part[:, s, 0, :], m_all[:], -1.0, None, ALU.mult).then_inc(max_steps, 1)
                    dve.tensor_tensor(m_diff[:, s, :], m_prev[:], m_all[:], ALU.subtract).then_inc(max_steps, 1)
                    dve.wait_ge(max_steps, base + 4)
                    dve.scalar_tensor_tensor(m_res[:], m_all[:], -1.0, m_part[:, s, 0, :],
                                             ALU.mult, ALU.subtract).then_inc(max_steps, 1)
                    dve.wait_ge(max_steps, base + 5)
                    dve.tensor_copy(m_part[:, s, 1, :], m_res[:]).then_inc(max_steps, 1)
                    dve.wait_ge(max_steps, base + 6)
                    dve.tensor_tensor(m_part[:, s, 2, :], m_res[:], m_part[:, s, 1, :],
                                      ALU.subtract).then_inc(max_steps, 1)

                def normalise(c, j, g):
                    dve.wait_ge(ot_turned, g + 1)
                    dve.wait_ge(corr_set, g + 1)
                    o = PS[:, 7, :].rearrange("p (k d) -> p k d", d=32)
                    sums = o[:, :, HD].rearrange("p (t h) -> p h t", t=NT)
                    dve.scalar_tensor_tensor(den[:].rearrange("p (h t) -> p h t", t=NT),
                                             corr[:, j, :].rearrange("p (h t) -> p h t", t=NT), 1.0, sums,
                                             ALU.add, ALU.mult).then_inc(nrm_steps, 1)
                    dve.wait_ge(nrm_steps, g * 3 + 1)
                    dve.reciprocal(rden[:], den[:]).then_inc(nrm_steps, 1)
                    dve.wait_ge(nrm_steps, g * 3 + 2)
                    dst = chunk_of(AO, c).rearrange("p (t x) -> p t x", t=NT)[:, :, j * HG * HD:(j + 1) * HG * HD]
                    dve.tensor_tensor(dst.rearrange("p t (h d) -> p t h d", d=HD),
                                      o[:, :, 0:HD].rearrange("p (t h) d -> p t h d", t=NT),
                                      rden[:].rearrange("p (h t) -> p t h", t=NT).unsqueeze(3)
                                      .broadcast_to([P, NT, HG, HD]), ALU.mult).then_inc(nrm_steps, 1)

                def step(c, i, g, has):
                    for u in range(8):
                        if has(0):
                            pair_reduce(i, g, u)
                        if u == 6 and has(3):
                            b, j = at(c, i, g, 3)
                            normalise(b, j, g - 3)
                    if has(0):
                        max_chain(i, g)
                run_groups(dve, step, 3)
        p2.close()
        att.close()

        XT = sb("XT", [P, TILES * E])
        p3 = ExitStack()
        wo = sb("wo", [P, P], F32, p3)
        bias = sb("bias", [P, P], F32, p3)
        AOs = sb("AOs", [P, 2, S], F32, p3)
        aT = sb("aT", [P, 2, S], F32, p3)
        y3 = sb("y3", [P, 2, S], F32, p3)
        xn2 = sb("xn2", [P, 2, S], F32, p3)
        lnA = ln_bufs("lnA", p3)
        ln2 = ln_bufs("ln2", p3)
        w3_in = sem("w3_in")
        ao_staged = sem("ao_staged")
        ao_turned = sem("ao_turned")
        aT_set = sem("aT_set")
        proj_done = sem("proj_done")
        y3_set = sem("y3_set")
        x3_set = sem("x3_set")
        turned2 = sem("turned2")
        xT2_set = sem("xT2_set")

        def tiles4(buf, s):
            return lambda t: buf[:, s, t * P:(t + 1) * P]

        with nc.Block() as block:
            @block.sync
            def _(sp):
                sp.dma_start(wo[:], io["L0_attn_out_w"]).then_inc(w3_in, 16)
                sp.dma_start(bias[:], io["L0_attn_out_b"].to_broadcast([P, P])).then_inc(w3_in, 16)

            @block.gpsimd
            def _(pool):
                def stage_rows(c, s):
                    if late(c, 2):
                        pool.wait_ge(ao_turned, c - 1)
                    pool.tensor_copy(AOs[:, s, :], chunk_of(AO, c)).then_inc(ao_staged, 1)
                run_stages(pool, NCH, [(0, stage_rows), (1, lambda c, s: rstd(lnA)(pool, c)),
                                       (1, lambda c, s: rstd(ln2)(pool, c))])

            @block.tensor
            def _(pe):
                def turn_rows(c, s):
                    pe.wait_ge(ao_staged, c + 1)
                    if late(c, 2):
                        pe.wait_ge(aT_set, c - 1)
                    for t in range(NT):
                        mm = pe.transpose(PS[:, s, t * P:(t + 1) * P], AOs[:, s, t * P:(t + 1) * P], idf[:])
                    mm.then_inc(ao_turned, 1)

                def project(c, s):
                    if isinstance(c, int) and c == 0:
                        pe.wait_ge(w3_in, 32)
                    pe.wait_ge(aT_set, c + 1)
                    if late(c, 2):
                        pe.wait_ge(y3_set, c - 1)
                    for t in range(NT):
                        mm = pe.matmul(PS[:, 2 + s, t * P:(t + 1) * P], aT[:, s, t * P:(t + 1) * P], wo[:],
                                       start=True, stop=True)
                    mm.then_inc(proj_done, 1)

                def turn_norm(c, s):
                    pe.wait_ge(ln2["steps"], c * LN_STEPS + LN_STEPS)
                    if late(c, 2):
                        pe.wait_ge(xT2_set, c - 1)
                    for t in range(NT):
                        mm = pe.transpose(PS[:, 4 + s, t * P:(t + 1) * P], xn2[:, s, t * P:(t + 1) * P], idf[:])
                    mm.then_inc(turned2, 1)
                run_stages(pe, NCH, [(0, turn_rows), (1, project), (2, turn_norm)])

            @block.scalar
            def _(act):
                def copy_aT(c, s):
                    act.wait_ge(ao_turned, c + 1)
                    if late(c, 2):
                        act.wait_ge(proj_done, c - 1)
                    act.copy(aT[:, s, :], PS[:, s, :]).then_inc(aT_set, 1)

                def copy_xT(c, s):
                    act.wait_ge(turned2, c + 1)
                    act.copy(chunk_of(XT, c), PS[:, 4 + s, :]).then_inc(xT2_set, 1)
                run_stages(act, NCH, [(0, copy_aT), (2, copy_xT)])

            @block.vector
            def _(dve):
                dve.wait_ge(w3_in, 32)

                def residual(c, s):
                    dve.wait_ge(proj_done, c + 1)
                    dve.tensor_tensor(y3[:, s, :].rearrange("p (t e) -> p t e", t=NT),
                                      PS[:, 2 + s, :].rearrange("p (t e) -> p t e", t=NT),
                                      bias[:].unsqueeze(1).broadcast_to([P, NT, E]), ALU.add).then_inc(y3_set, 1)
                    dve.wait_ge(y3_set, c + 1)
                    layernorm(dve, c, lnA, tiles4(y3, s), tiles4(y3, s))
                    dve.wait_ge(lnA["steps"], c * LN_STEPS + LN_STEPS)
                    dve.tensor_tensor(chunk_of(X, c), chunk_of(X, c), y3[:, s, :], ALU.add).then_inc(x3_set, 1)
                    dve.wait_ge(x3_set, c + 1)
                    if late(c, 2):
                        dve.wait_ge(turned2, c - 1)
                    layernorm(dve, c, ln2, lambda t: tile_of(X, c, t), tiles4(xn2, s))
                run_stages(dve, NCH, [(1, residual)])
        p3.close()

        p4 = ExitStack()
        w1 = sb("w1", [P, DH], F32, p4)
        w2 = sb("w2", [P, DH], F32, p4)
        hw = [sb("h1w", [P, FB, DH], F32, p4), sb("h2w", [P, FB, DH], F32, p4)]
        w3 = sb("w3", [P, FB, P], F32, p4)
        scales = sb("scales", [P, 4, FB], F32, p4)
        w3s = sb("w3s", [P, P], F32, p4)
        sil = sb("sil", [P, 2, S], F32, p4)
        hA = sb("hA", [P, 2, FB, S], F32, p4)
        hB = sb("hB", [P, 2, FB, S], F32, p4)
        y4 = sb("y4", [P, 2, S], F32, p4)
        xn3 = sb("xn3", [P, 2, S], F32, p4)
        lnB = ln_bufs("lnB", p4)
        ln3 = ln_bufs("ln3", p4)
        w4_in = sem("w4_in")
        in_done = sem("in_done")
        hid_done = sem("hid_done")
        mlp_done = sem("mlp_done")
        act_out = sem("act_out")
        h_set = sem("h_set")
        y4_set = sem("y4_set")
        x4_set = sem("x4_set")
        turned3 = sem("turned3")
        xT3_set = sem("xT3_set")
        PAIRS = NCH // 2

        def run_pairs(eng, step):
            step(0, True, False)
            step(1, True, True)
            with eng.Fori(2, PAIRS) as p:
                step(p, True, True)
            step(PAIRS, False, True)

        with nc.Block() as block:
            @block.sync
            def _(sp):
                sp.dma_start(w1[:], io["L0_ffn_w1_w"]).then_inc(w4_in, 16)
                sp.dma_start(w2[:], io["L0_ffn_w2_w"]).then_inc(w4_in, 16)
                for n, name in enumerate(("L0_ffn_w1_s", "L0_ffn_w2_s", "L0_ffn_h1_s", "L0_ffn_h2_s")):
                    sp.dma_start(scales[:, n, :], io[name]).then_inc(w4_in, 16)
                sp.dma_start(hw[0][:], io["L0_ffn_h1_w"].rearrange("(k p) o -> p k o", p=P)).then_inc(w4_in, 16)
                sp.dma_start(hw[1][:], io["L0_ffn_h2_w"].rearrange("(k p) o -> p k o", p=P)).then_inc(w4_in, 16)
                sp.dma_start(w3[:], io["L0_ffn_w3_w"].rearrange("(k p) o -> p k o", p=P)).then_inc(w4_in, 16)
                sp.dma_start(w3s[:], io["L0_ffn_w3_s"].to_broadcast([P, P])).then_inc(w4_in, 16)

            @block.tensor
            def _(pe):
                pe.wait_ge(w4_in, 160)

                def first(p):
                    return isinstance(p, int) and p == 0

                def layer_in(p, s):
                    xT = chunk_of(XT, 2 * p + s)
                    for f in range(FB):
                        n = 4 * s + f
                        if n >= 2:
                            pe.wait_ge(act_out, 24 * p + n - 1)
                            pe.wait_ge(h_set, 8 * p + n - 1)
                        elif not first(p):
                            pe.wait_ge(act_out, 24 * p - 2 + 2 * n)
                        for k, w in enumerate((w1, w2)):
                            pe.matmul(PS[:, 2 * (n % 2) + k, :], w[:, f * P:(f + 1) * P], xT,
                                      start=True, stop=True).then_inc(in_done, 1)

                def layer_hid(p, s, layer):
                    src = (hA, hB)[layer]
                    n = 2 * layer + s
                    pe.wait_ge(act_out, 24 * p + (4 * s + 4 if layer == 0 else 8 + 4 * s + 4))
                    if layer == 0:
                        pe.wait_ge(h_set, 8 * p + 4 * s + 4)
                    for f in range(FB):
                        if n == 0:
                            pe.wait_ge((act_out, h_set)[f % 2], (24 if f % 2 == 0 else 8) * p + 7 + f // 2)
                        else:
                            pe.wait_ge(act_out, 24 * p + 8 + 4 * (n - 1) + f + 1)
                        for k in range(FB):
                            mm = pe.matmul(PS[:, f, :], hw[layer][:, k, f * P:(f + 1) * P], src[:, s, k, :],
                                           start=(k == 0), stop=(k == FB - 1))
                        mm.then_inc(hid_done, 1)

                def layer_out(p, s):
                    pe.wait_ge(act_out, 24 * p + 16 + 4 * s + 4)
                    if not first(p):
                        pe.wait_ge(y4_set, 2 * p - 1 + s)
                    for t in range(NT):
                        for k in range(FB):
                            mm = pe.matmul(PS[:, 4 + s, t * P:(t + 1) * P], hA[:, s, k, t * P:(t + 1) * P],
                                           w3[:, k, :], start=(k == 0), stop=(k == FB - 1))
                    mm.then_inc(mlp_done, 1)

                def turn(p, s):
                    pe.wait_ge(ln3["steps"], (2 * p + s + 1) * LN_STEPS)
                    if not first(p):
                        pe.wait_ge(xT3_set, 2 * p - 1 + s)
                    for t in range(NT):
                        mm = pe.transpose(PS[:, 6 + s, t * P:(t + 1) * P], xn3[:, s, t * P:(t + 1) * P], idf[:])
                    mm.then_inc(turned3, 1)

                def step(p, now, before):
                    if now:
                        layer_in(p, 0)
                        layer_in(p, 1)
                        layer_hid(p, 0, 0)
                        layer_hid(p, 1, 0)
                        layer_hid(p, 0, 1)
                    if before:
                        turn(p - 1, 0)
                        turn(p - 1, 1)
                    if now:
                        layer_hid(p, 1, 1)
                        layer_out(p, 0)
                        layer_out(p, 1)
                run_pairs(pe, step)

            @block.gpsimd
            def _(pool):
                def step(p, now, before):
                    if before:
                        for s in range(2):
                            rstd(lnB)(pool, (p - 1) * 2 + s)
                            rstd(ln3)(pool, (p - 1) * 2 + s)
                run_pairs(pool, step)

            @block.scalar
            def _(act):
                act.wait_ge(w4_in, 160)

                def silus(p, s):
                    for f in range(FB):
                        n = 4 * s + f
                        act.wait_ge(in_done, 16 * p + 2 * n + 1)
                        if not (isinstance(p, int) and p == 0 and n < 2):
                            act.wait_ge(h_set, 8 * p + n - 1)
                        act.activation(sil[:, n % 2, :], PS[:, 2 * (n % 2), :], ACT.Silu,
                                       scale=scales[:, 0, f:f + 1]).then_inc(act_out, 1)

                def gelus(p, s, layer):
                    dst = (hB, hA)[layer]
                    for f in range(FB):
                        act.wait_ge(hid_done, 16 * p + 8 * layer + 4 * s + f + 1)
                        if f == 0 and not (isinstance(p, int) and p == 0 and layer == 0):
                            act.wait_ge(hid_done, 16 * p + 4 * s + (4 if layer else -4))
                        act.activation(dst[:, s, f, :], PS[:, f, :], ACT.Gelu,
                                       scale=scales[:, 2 + layer, f:f + 1]).then_inc(act_out, 1)

                def copy_xT(p, s):
                    act.wait_ge(turned3, 2 * p + s + 1)
                    act.copy(chunk_of(XT, 2 * p + s), PS[:, 6 + s, :]).then_inc(xT3_set, 1)

                def step(p, now, before):
                    if now:
                        silus(p, 0)
                        silus(p, 1)
                        gelus(p, 0, 0)
                        gelus(p, 1, 0)
                        gelus(p, 0, 1)
                    if before:
                        copy_xT(p - 1, 0)
                        copy_xT(p - 1, 1)
                    if now:
                        gelus(p, 1, 1)
                run_pairs(act, step)

            @block.vector
            def _(dve):
                dve.wait_ge(w4_in, 160)

                def gate(p, s):
                    if not (isinstance(p, int) and p == 0):
                        dve.wait_ge(mlp_done, 2 * p - 1 + s)
                    for f in range(FB):
                        n = 4 * s + f
                        dve.wait_ge(in_done, 16 * p + 2 * n + 2)
                        dve.wait_ge(act_out, 24 * p + n + 1)
                        dve.scalar_tensor_tensor(hA[:, s, f, :], PS[:, 2 * (n % 2) + 1, :], scales[:, 1, f:f + 1],
                                                 sil[:, n % 2, :], ALU.mult, ALU.mult).then_inc(h_set, 1)

                def residual(p, s):
                    c = 2 * p + s
                    dve.wait_ge(mlp_done, c + 1)
                    dve.tensor_tensor(y4[:, s, :].rearrange("p (t e) -> p t e", t=NT),
                                      PS[:, 4 + s, :].rearrange("p (t e) -> p t e", t=NT),
                                      w3s[:].unsqueeze(1).broadcast_to([P, NT, E]), ALU.mult).then_inc(y4_set, 1)
                    dve.wait_ge(y4_set, c + 1)
                    layernorm(dve, c, lnB, tiles4(y4, s), tiles4(y4, s))
                    dve.wait_ge(lnB["steps"], c * LN_STEPS + LN_STEPS)
                    dve.tensor_tensor(chunk_of(X, c), chunk_of(X, c), y4[:, s, :], ALU.add).then_inc(x4_set, 1)
                    dve.wait_ge(x4_set, c + 1)
                    if not (isinstance(p, int) and p == 0):
                        dve.wait_ge(turned3, c - 1)
                    layernorm(dve, c, ln3, lambda t: tile_of(X, c, t), tiles4(xn3, s))

                def step(p, now, before):
                    if now:
                        gate(p, 0)
                        gate(p, 1)
                    if before:
                        residual(p - 1, 0)
                        residual(p - 1, 1)
                run_pairs(dve, step)
        p4.close()

        p5 = ExitStack()
        wqkvT = sb("wqkvT", [P, 3, P], F32, p5)
        wout1 = sb("wout1", [P, P], F32, p5)
        dft = sb("dft", [P, 6, P], F32, p5)
        fold = sb("fold", [P, 8, P], F32, p5)
        gate_w = sb("gate_w", [P, NE], F32, p5)
        ones5 = sb("ones5", [P, S], F32, p5)
        kA = sb("kA", [P, 2, S], F32, p5)
        qq = sb("qq", [P, 2, 2, S], F32, p5)
        p12 = sb("p12", [P, 2, 2, S], F32, p5)
        csum = sb("csum", [P, 2, S], F32, p5)
        p34 = sb("p34", [P, 2, 2, S], F32, p5)
        y5 = sb("y5", [P, 2, S], F32, p5)
        xn4 = sb("xn4", [P, 2, S], F32, p5)
        xT4 = sb("xT4", [P, 2, S], F32, p5)
        lnC = ln_bufs("lnC", p5)
        ln4 = ln_bufs("ln4", p5)
        w5_in = sem("w5_in")
        folds_done = sem("folds_done")
        fold_set = sem("fold_set")
        ones5_set = sem("ones5_set")
        k_done = sem("k_done")
        q_done = sem("q_done")
        v5_done = sem("v5_done")
        kv_done = sem("kv_done")
        out5_done = sem("out5_done")
        turned4 = sem("turned4")
        logits_done = sem("logits_done")
        kA_set = sem("kA_set")
        qq_set = sem("qq_set")
        xT4_set = sem("xT4_set")
        p12_set = sem("p12_set")
        scan_set = sem("scan_set")
        p34_set = sem("p34_set")
        x5_set = sem("x5_set")
        xn4_kept = sem("xn4_kept")
        LB = 7

        with nc.Block() as block:
            @block.sync
            def _(sp):
                sp.dma_start(wqkvT[:], io["L1_attn_w_qkv"].rearrange("(k p) i -> p k i", p=P)).then_inc(w5_in, 16)
                sp.dma_start(wout1[:], io["L1_attn_w_out"]).then_inc(w5_in, 16)
                sp.dma_start(dft[:], io["dft"].rearrange("k p i -> p k i")).then_inc(w5_in, 16)
                sp.dma_start(gate_w[:], io["L1_ffn_gate_w"]).then_inc(w5_in, 16)

            @block.tensor
            def _(pe):
                pe.wait_ge(w5_in, 64)
                for n, (w, d) in enumerate(((1, 0), (2, 0), (2, 1), (0, 0), (0, 1))):
                    pe.matmul(PS[:, n // 4, (n % 4) * P:(n % 4 + 1) * P], wqkvT[:, w, :], dft[:, d, :],
                              start=True, stop=True)
                for n in (5, 6):
                    mm = pe.matmul(PS[:, n // 4, (n % 4) * P:(n % 4 + 1) * P], dft[:, n - 1, :], wout1[:],
                                   start=True, stop=True)
                mm.then_inc(folds_done, 1)
                pe.wait_ge(fold_set, 1)

                def project(c, s):
                    xT = chunk_of(XT, c)
                    if late(c, 1):
                        pe.wait_ge(kA_set, c)
                    if late(c, 4):
                        pe.wait_ge(xT4_set, 2 * c - 6)
                    pe.matmul(PS[:, 0, :], fold[:, 0, :], xT, start=True, stop=True).then_inc(k_done, 1)
                    if late(c, 1):
                        pe.wait_ge(qq_set, c)
                    pe.matmul(PS[:, 3, :], fold[:, 3, :], xT, start=True, stop=True)
                    pe.matmul(PS[:, 4, :], fold[:, 4, :], xT, start=True, stop=True).then_inc(q_done, 1)
                    if late(c, 1):
                        pe.wait_ge(p12_set, 2 * c)
                    pe.matmul(PS[:, 1, :], fold[:, 1, :], xT, start=True, stop=True)
                    pe.matmul(PS[:, 2, :], fold[:, 2, :], xT, start=True, stop=True).then_inc(v5_done, 1)

                def combine(c, s):
                    pe.wait_ge(p12_set, 2 * c + 2)
                    if late(c, 1):
                        pe.wait_ge(scan_set, c)
                    pe.matmul(PS[:, 5, :], dft[:, 2, :], p12[:, s, 0, :], start=True, stop=False)
                    pe.matmul(PS[:, 5, :], dft[:, 3, :], p12[:, s, 1, :], start=False, stop=True).then_inc(kv_done, 1)

                def output(c, s):
                    pe.wait_ge(p34_set, 2 * c + 2)
                    if late(c, 1):
                        pe.wait_ge(lnC["steps"], c * LN_STEPS)
                    for t in range(NT):
                        for k in range(2):
                            mm = pe.matmul(PS[:, 6, t * P:(t + 1) * P], p34[:, s, k, t * P:(t + 1) * P],
                                           fold[:, 5 + k, :], start=(k == 0), stop=(k == 1))
                    mm.then_inc(out5_done, 1)

                def turn(c, s):
                    pe.wait_ge(ln4["steps"], c * LN_STEPS + LN_STEPS)
                    pe.wait_ge(kA_set, min(c + 4, NCH) if isinstance(c, int) else c + 4)
                    if isinstance(c, int) and c + 4 > NCH:
                        pe.wait_ge(xT4_set, 2 * c)
                    for t in range(NT):
                        mm = pe.transpose(PS[:, 0, t * P:(t + 1) * P], xn4[:, s, t * P:(t + 1) * P], idf[:])
                    mm.then_inc(turned4, 1)

                def logits(c, s):
                    pe.wait_ge(xT4_set, 2 * c + 2)
                    for t in range(NT):
                        mm = pe.matmul(PS[:, LB, ds(c * (NT * NE) + t * NE, NE)], xT4[:, s, t * P:(t + 1) * P],
                                       gate_w[:], start=True, stop=True)
                    mm.then_inc(logits_done, 1)
                run_stages(pe, NCH, [(0, project), (1, combine), (2, output), (3, turn), (4, logits)])

            @block.scalar
            def _(act):
                act.wait_ge(folds_done, 1)
                act.copy(fold[:, 0:7, :], PS[:, 0:2, :].rearrange("p a (b e) -> p (a b) e", e=P)[:, 0:7, :])\
                   .then_inc(fold_set, 1)

                def copies(c, s):
                    act.wait_ge(k_done, c + 1)
                    if late(c, 2):
                        act.wait_ge(p12_set, 2 * c - 2)
                    act.copy(kA[:, s, :], PS[:, 0, :]).then_inc(kA_set, 1)
                    act.wait_ge(q_done, c + 1)
                    if late(c, 2):
                        act.wait_ge(p34_set, 2 * c - 2)
                    act.copy(qq[:, s], PS[:, 3:5, :]).then_inc(qq_set, 1)

                def copy_xT(c, s):
                    act.wait_ge(turned4, c + 1)
                    if late(c, 2):
                        act.wait_ge(logits_done, c - 1)
                    act.copy(xT4[:, s, :], PS[:, 0, :]).then_inc(xT4_set, 1)
                    act.copy(chunk_of(XT, c), PS[:, 0, :]).then_inc(xT4_set, 1)
                run_stages(act, NCH, [(0, copies), (3, copy_xT)])

            @block.gpsimd
            def _(pool):
                def spectra(c, s):
                    pool.wait_ge(scan_set, c + 1)
                    pool.wait_ge(qq_set, c + 1)
                    if late(c, 2):
                        pool.wait_ge(out5_done, c - 1)
                    for k in range(2):
                        pool.tensor_tensor(p34[:, s, k, :], qq[:, s, k, :], csum[:, s, :],
                                           ALU.mult).then_inc(p34_set, 1)

                def keep(c, s):
                    pool.wait_ge(ln4["steps"], c * LN_STEPS + LN_STEPS)
                    pool.tensor_copy(chunk_of(AO, c), xn4[:, s, :]).then_inc(xn4_kept, 1)
                run_stages(pool, NCH, [(3, keep), (1, spectra), (2, lambda c, s: rstd(lnC)(pool, c)),
                                       (2, lambda c, s: rstd(ln4)(pool, c))])

            @block.vector
            def _(dve):
                dve.memset(ones5[:], 1.0).then_inc(ones5_set, 1)
                dve.wait_ge(ones5_set, 1)

                def products(c, s):
                    dve.wait_ge(kA_set, c + 1)
                    dve.wait_ge(v5_done, c + 1)
                    if late(c, 2):
                        dve.wait_ge(kv_done, c - 1)
                    for k in range(2):
                        dve.tensor_tensor(p12[:, s, k, :], PS[:, 1 + k, :], kA[:, s, :], ALU.mult).then_inc(p12_set, 1)

                def scan(c, s):
                    dve.wait_ge(kv_done, c + 1)
                    if late(c, 2):
                        dve.wait_ge(p34_set, 2 * c - 2)
                    dve.tensor_tensor_scan(csum[:, s, :], ones5[:], PS[:, 5, :], 0.0, ALU.mult,
                                           ALU.add).then_inc(scan_set, 1)

                def residual(c, s):
                    dve.wait_ge(out5_done, c + 1)
                    layernorm(dve, c, lnC, lambda t: PS[:, 6, t * P:(t + 1) * P], tiles4(y5, s))
                    dve.wait_ge(lnC["steps"], c * LN_STEPS + LN_STEPS)
                    dve.tensor_tensor(chunk_of(X, c), chunk_of(X, c), y5[:, s, :], ALU.add).then_inc(x5_set, 1)
                    dve.wait_ge(x5_set, c + 1)
                    if late(c, 2):
                        dve.wait_ge(turned4, c - 1)
                        dve.wait_ge(xn4_kept, c - 1)
                    layernorm(dve, c, ln4, lambda t: tile_of(X, c, t), tiles4(xn4, s))
                run_stages(dve, NCH, [(0, products), (1, scan), (2, residual)])
        p5.close()

        SH = sb("SH", [P, TILES * E])
        TE = TILES * NE
        pos_u = sb("pos_u", [P, TILES], U32)
        score = sb("score", [P, TILES])
        tile_e = sb("tile_e", [P, ST_TILES], I32)
        p6 = ExitStack()
        lg = sb("lg", [P, TILES, NE], F32, p6)
        mx = sb("mx", [P, TILES], F32, p6)
        cand = sb("cand", [P, TILES, NE], F32, p6)
        best = sb("best", [P, TILES], F32, p6)
        oh = sb("oh", [P, NE, TILES], F32, p6)
        ohb = sb("ohb", [P, NE * TILES], BF16, p6)
        tri = sb("tri", [P, P], F32, p6)
        trib = sb("trib", [P, P], BF16, p6)
        onesb = sb("onesb", [P, P], BF16, p6)
        onesr = sb("onesr", [P, TE], F32, p6)
        cls = sb("cls", [P, NE], F32, p6)
        starts = sb("starts", [P, ST_TILES], F32, p6)
        incl = sb("incl", [P, TE], F32, p6)
        where = sb("where", [P, TE], F32, p6)
        cnt = sb("cnt", [P, 6, NE], F32, p6)
        cnti = sb("cnti", [P, 2, NE], I32, p6)
        posf = sb("posf", [P, TILES], F32, p6)
        texp = sb("texp", [P, ST_TILES], F32, p6)
        w6_in = sem("w6_in")
        r6 = sem("route_steps")
        mx_set = sem("mx_set")
        score_set = sem("score_set")
        ranks_done = sem("ranks_done")

        with nc.Block() as block:
            @block.sync
            def _(sp):
                sp.dma_start(tri[:], io["tri"]).then_inc(w6_in, 16)
                sp.dma_start(cls[:], io["cls"].to_broadcast([P, NE])).then_inc(w6_in, 16)
                sp.dma_start(starts[:], io["starts"].to_broadcast([P, ST_TILES])).then_inc(w6_in, 16)

            @block.scalar
            def _(act):
                act.wait_ge(mx_set, 1)
                act.activation(score[:], mx[:], ACT.Sigmoid).then_inc(score_set, 1)

            @block.tensor
            def _(pe):
                pe.wait_ge(r6, 9)
                pe.matmul(PS[:, 0, :], trib[:], ohb[:], start=True, stop=True)
                pe.matmul(PS[:, 1, :], onesb[:], ohb[:], start=True, stop=True).then_inc(ranks_done, 1)

            @block.vector
            def _(dve):
                n = [0]

                def then(ins):
                    n[0] += 1
                    ins.then_inc(r6, 1)
                    dve.wait_ge(r6, n[0])

                def b_te(col):
                    return col.unsqueeze(2).broadcast_to([P, TILES, NE])

                cls_te = cls[:].unsqueeze(1).broadcast_to([P, TILES, NE])
                oh_te = oh[:].rearrange("p e t -> p t e")
                dve.wait_ge(w6_in, 48)
                then(dve.tensor_copy(lg[:], PS[:, LB, :].rearrange("p (t e) -> p t e", e=NE)))
                dve.tensor_reduce(mx[:], lg[:], AX_X, ALU.max).then_inc(mx_set, 1)
                dve.wait_ge(mx_set, 1)
                then(dve.tensor_tensor(cand[:], lg[:], b_te(mx[:]), ALU.is_equal))
                then(dve.tensor_tensor(cand[:], cand[:], cls_te, ALU.mult))
                then(dve.tensor_reduce(best[:], cand[:], AX_X, ALU.max))
                then(dve.tensor_tensor(oh_te, b_te(best[:]), cls_te, ALU.is_equal))
                then(dve.tensor_copy(ohb[:], oh[:].rearrange("p e t -> p (e t)")))
                then(dve.tensor_copy(trib[:], tri[:]))
                then(dve.memset(onesb[:], 1.0))
                then(dve.memset(onesr[:], 1.0))
                dve.wait_ge(ranks_done, 1)
                then(dve.tensor_tensor_scan(incl[:], onesr[:], PS[:, 1, :], 0.0, ALU.mult, ALU.add))
                then(dve.tensor_tensor(where[:], incl[:], PS[:, 1, :], ALU.subtract))
                then(dve.tensor_tensor(where[:], where[:], PS[:, 0, :], ALU.add))
                ends = incl[:].rearrange("p (e t) -> p e t", e=NE)[:, :, TILES - 1]
                count, padded, pad_ends, shift, pad_ceil = (cnt[:, k, :] for k in range(5))
                then(dve.tensor_copy(count, ends))
                then(dve.tensor_tensor(count[:, 1:NE], ends[:, 1:NE], ends[:, 0:NE - 1], ALU.subtract))
                then(dve.tensor_scalar(pad_ceil, count, float(P - 1), None, ALU.add))
                then(dve.tensor_copy(cnti[:, 0, :], pad_ceil))
                then(dve.tensor_scalar(cnti[:, 1, :], cnti[:, 0, :], 7, 7, ALU.arith_shift_right,
                                       ALU.logical_shift_left))
                then(dve.tensor_copy(padded, cnti[:, 1, :]))
                then(dve.tensor_tensor_scan(pad_ends, onesr[:, 0:NE], padded, 0.0, ALU.mult, ALU.add))
                then(dve.tensor_tensor(shift, pad_ends, padded, ALU.subtract))
                then(dve.tensor_tensor(shift, shift, ends, ALU.subtract))
                then(dve.tensor_tensor(shift, shift, count, ALU.add))
                w_et = where[:].rearrange("p (e t) -> p e t", e=NE)
                then(dve.tensor_tensor(w_et, w_et, shift.unsqueeze(2).broadcast_to([P, NE, TILES]), ALU.add))
                then(dve.tensor_tensor(w_et, w_et, oh[:], ALU.mult))
                then(dve.tensor_reduce(posf[:], where[:].rearrange("p (e t) -> p t e", e=NE), AX_X, ALU.add))
                then(dve.tensor_copy(pos_u[:], posf[:]))
                then(dve.memset(texp[:], 0.0))
                for e in range(NE - 1):
                    then(dve.scalar_tensor_tensor(texp[:], starts[:], pad_ends[:, e:e + 1], texp[:],
                                                  ALU.is_ge, ALU.add))
                then(dve.tensor_copy(tile_e[:], texp[:]))
        p6.close()

        wgu = sb("wgu", [P, NE * 2 * F1])
        wdn = sb("wdn", [P, NE * FB1 * E])
        w8_in = sem("w8_in")
        p7 = ExitStack()
        sgu = sb("sgu", [P, 2, F1], F32, p7)
        sdn = sb("sdn", [P, FB1, P], F32, p7)
        sg = sb("sg", [P, 2, FB1, S], F32, p7)
        sh = sb("sh", [P, 2, FB1, S], F32, p7)
        xs = sb("xs", [P, 2, NT, E], F32, p7)
        idx = sb("idx", [P, 2, NT], U32, p7)
        w7_in = sem("w7_in")
        gu_done = sem("gu_done")
        sg_set = sem("sg_set")
        sh_set = sem("sh_set")
        dn_done = sem("dn_done")
        SH_set = sem("SH_set")
        xs_set = sem("xs_set")
        xs_out = [sem("xs_out0"), sem("xs_out1")]

        with nc.Block() as block:
            @block.sync
            def _(sp):
                sp.dma_start(sgu[:, 0, :], io["L1_ffn_shared_gate"]).then_inc(w7_in, 16)
                sp.dma_start(sgu[:, 1, :], io["L1_ffn_shared_up"]).then_inc(w7_in, 16)
                sp.dma_start(sdn[:], io["L1_ffn_shared_down"].rearrange("(k p) o -> p k o", p=P)).then_inc(w7_in, 16)
                g = wgu[:].rearrange("p (e u f) -> p e u f", e=NE, u=2)
                sp.dma_start(g[:, :, 0, :], io["L1_ffn_r_gate"].rearrange("e p f -> p e f")).then_inc(w8_in, 16)
                sp.dma_start(g[:, :, 1, :], io["L1_ffn_r_up"].rearrange("e p f -> p e f")).then_inc(w8_in, 16)
                sp.dma_start(wdn[:].rearrange("p (e k o) -> p e k o", e=NE, k=FB1),
                             io["L1_ffn_r_down"].rearrange("e (k p) o -> p e k o", p=P)).then_inc(w8_in, 16)

            @block.tensor
            def _(pe):
                pe.wait_ge(w7_in, 48)

                def expand(c, s):
                    for f in range(FB1):
                        if late(c, 1):
                            pe.wait_ge(sh_set, 2 * c + f - 1)
                        for u in range(2):
                            mm = pe.matmul(PS[:, 2 * f + u, :], sgu[:, u, f * P:(f + 1) * P], chunk_of(XT, c),
                                           start=True, stop=True)
                        mm.then_inc(gu_done, 1)

                def reduce(c, s):
                    pe.wait_ge(sh_set, 2 * c + 2)
                    if late(c, 2):
                        pe.wait_ge(SH_set, c - 1)
                    for t in range(NT):
                        for f in range(FB1):
                            mm = pe.matmul(PS[:, 4 + s, t * P:(t + 1) * P], sh[:, s, f, t * P:(t + 1) * P],
                                           sdn[:, f, :], start=(f == 0), stop=(f == FB1 - 1))
                    mm.then_inc(dn_done, 1)
                run_stages(pe, NCH, [(0, expand), (1, reduce)])

            @block.scalar
            def _(act):
                def silus(c, s):
                    for f in range(FB1):
                        act.wait_ge(gu_done, 2 * c + f + 1)
                        if late(c, 2):
                            act.wait_ge(sh_set, 2 * c - 2)
                        act.activation(sg[:, s, f, :], PS[:, 2 * f, :], ACT.Silu).then_inc(sg_set, 1)

                def keep(c, s):
                    act.wait_ge(dn_done, c + 1)
                    act.copy(chunk_of(SH, c), PS[:, 4 + s, :]).then_inc(SH_set, 1)
                run_stages(act, NCH, [(0, silus), (1, keep)])

            @block.gpsimd
            def _(pool):
                def scatter(c, s):
                    pool.wait_ge(xs_set, 5 * c + 5)
                    settled(pool)
                    for t in range(NT):
                        pool.indirect_dma_start(out=xs_scr, out_offset=bass.IndirectOffsetOnAxis(idx[:, s, t:t + 1], 0),
                                                in_=xs[:, s, t, :], in_offset=None).then_inc(xs_out[s], 16)
                run_stages(pool, NCH, [(0, scatter)])
                for s in range(2):
                    pool.wait_ge(xs_out[s], NCH // 2 * NT * 16)

            @block.vector
            def _(dve):
                def scale(c, s):
                    if late(c, 2):
                        dve.wait_ge(xs_out[s], (c - s) * 32)
                    for t in range(NT):
                        dve.tensor_scalar(xs[:, s, t, :], tile_of(AO, c, t), score[:, ds(c * NT + t, 1)], None,
                                          ALU.mult).then_inc(xs_set, 1)
                    dve.tensor_copy(idx[:, s, :], pos_u[:, ds(c * NT, NT)]).then_inc(xs_set, 1)

                def gate(c, s):
                    if late(c, 2):
                        dve.wait_ge(dn_done, c - 1)
                    for f in range(FB1):
                        dve.wait_ge(gu_done, 2 * c + f + 1)
                        dve.wait_ge(sg_set, 2 * c + f + 1)
                        dve.tensor_tensor(sh[:, s, f, :], PS[:, 2 * f + 1, :], sg[:, s, f, :],
                                          ALU.mult).then_inc(sh_set, 1)
                run_stages(dve, NCH, [(0, scale), (0, gate)])
        p7.close()

        p8 = ExitStack()
        xt = sb("xt", [P, 2, E], F32, p8)
        xtT = sb("xtT", [P, 2, P], F32, p8)
        g8 = sb("g8", [P, 2, F1], F32, p8)
        h8 = sb("h8", [P, 2, F1], F32, p8)
        h8T = sb("h8T", [P, 2, FB1 * P], F32, p8)
        y8 = sb("y8", [P, 2, E], F32, p8)
        xt_in = [sem("xt_in0"), sem("xt_in1")]
        xt_turned = sem("xt_turned")
        xtT_set = sem("xtT_set")
        gu8_done = sem("gu8_done")
        g8_set = sem("g8_set")
        h8_set = sem("h8_set")
        h8_turned = sem("h8_turned")
        h8T_set = sem("h8T_set")
        y8_done = sem("y8_done")
        y8_set = sem("y8_set")
        y8_out = [sem("y8_out0"), sem("y8_out1")]
        xs_tiles = xs_scr.rearrange("(n p) e -> n p e", p=P)
        y_tiles = y_scr.rearrange("(n p) e -> n p e", p=P)

        with nc.Block() as block:
            @block.sync
            def _(sp):
                def load(j, s):
                    if late(j, 2):
                        sp.wait_ge(xt_turned, j - 1)
                    sp.dma_start(xt[:, s, :], xs_tiles[ds(j, 1)].rearrange("n p e -> p (n e)")).then_inc(xt_in[s], 16)

                def store(j, s):
                    sp.wait_ge(y8_set, j + 1)
                    sp.dma_start(y_tiles[ds(j, 1)].rearrange("n p e -> p (n e)"), y8[:, s, :]).then_inc(y8_out[s], 16)
                run_stages(sp, ST_TILES, [(0, load), (4, store)])
                for s in range(2):
                    sp.wait_ge(y8_out[s], 16 * (ST_TILES // 2))

            @block.tensor
            def _(pe):
                pe.wait_ge(w8_in, 48)

                def turn_x(j, s):
                    pe.wait_ge(xt_in[s], (j - s) * 8 + 16)
                    if late(j, 2):
                        pe.wait_ge(xtT_set, j - 1)
                    pe.transpose(PS[:, s, 0:P], xt[:, s, :], idf[:]).then_inc(xt_turned, 1)

                def expand(j, s):
                    e = pe.value_load(tile_e[0:1, ds(j, 1)], min_val=0, max_val=NE - 1)
                    pe.wait_ge(xtT_set, j + 1)
                    if late(j, 2):
                        pe.wait_ge(h8_set, j - 1)
                    pe.matmul(PS[:, 2 + s, :], xtT[:, s, :], wgu[:, ds(e * (2 * F1), 2 * F1)],
                              start=True, stop=True).then_inc(gu8_done, 1)

                def turn_h(j, s):
                    pe.wait_ge(h8_set, j + 1)
                    if late(j, 2):
                        pe.wait_ge(h8T_set, j - 1)
                    for f in range(FB1):
                        mm = pe.transpose(PS[:, 4 + s, f * P:(f + 1) * P], h8[:, s, f * P:(f + 1) * P], idf[:])
                    mm.then_inc(h8_turned, 1)

                def reduce(j, s):
                    e = pe.value_load(tile_e[0:1, ds(j, 1)], min_val=0, max_val=NE - 1)
                    pe.wait_ge(h8T_set, j + 1)
                    if late(j, 2):
                        pe.wait_ge(y8_set, j - 1)
                    for f in range(FB1):
                        mm = pe.matmul(PS[:, 6 + s, 0:E], h8T[:, s, f * P:(f + 1) * P],
                                       wdn[:, ds(e * (FB1 * E) + f * E, E)], start=(f == 0), stop=(f == FB1 - 1))
                    mm.then_inc(y8_done, 1)
                run_stages(pe, ST_TILES, [(0, turn_x), (1, expand), (2, turn_h), (3, reduce)])

            @block.scalar
            def _(act):
                def copy_xT(j, s):
                    act.wait_ge(xt_turned, j + 1)
                    if late(j, 2):
                        act.wait_ge(gu8_done, j - 1)
                    act.copy(xtT[:, s, :], PS[:, s, 0:P]).then_inc(xtT_set, 1)

                def silu(j, s):
                    act.wait_ge(gu8_done, j + 1)
                    if late(j, 2):
                        act.wait_ge(h8_set, j - 1)
                    act.activation(g8[:, s, :], PS[:, 2 + s, 0:F1], ACT.Silu).then_inc(g8_set, 1)

                def copy_y(j, s):
                    act.wait_ge(y8_done, j + 1)
                    if late(j, 2):
                        act.wait_ge(y8_out[s], (j - s) * 8)
                    act.copy(y8[:, s, :], PS[:, 6 + s, 0:E]).then_inc(y8_set, 1)
                run_stages(act, ST_TILES, [(0, copy_xT), (1, silu), (3, copy_y)])

            @block.vector
            def _(dve):
                def gate(j, s):
                    dve.wait_ge(g8_set, j + 1)
                    if late(j, 2):
                        dve.wait_ge(h8_turned, j - 1)
                    dve.tensor_tensor(h8[:, s, :], PS[:, 2 + s, F1:2 * F1], g8[:, s, :], ALU.mult).then_inc(h8_set, 1)

                def copy_hT(j, s):
                    dve.wait_ge(h8_turned, j + 1)
                    if late(j, 2):
                        dve.wait_ge(y8_done, j - 1)
                    dve.tensor_copy(h8T[:, s, :], PS[:, 4 + s, 0:FB1 * P]).then_inc(h8T_set, 1)
                run_stages(dve, ST_TILES, [(1, gate), (2, copy_hT)])
        p8.close()

        p9 = ExitStack()
        idx9 = sb("idx9", [P, 2, NT], U32, p9)
        y9 = sb("y9", [P, 2, S], F32, p9)
        o9 = sb("o9", [P, 2, S], F32, p9)
        ln9 = ln_bufs("ln9", p9)
        idx9_set = sem("idx9_set")
        y9_in = [sem("y9_in0"), sem("y9_in1")]
        sum_set = sem("sum_set")
        o9_set = sem("o9_set")
        o9_out = [sem("o9_out0"), sem("o9_out1")]

        with nc.Block() as block:
            @block.gpsimd
            def _(pool):
                def gather(c, s):
                    if late(c, 2):
                        pool.wait_ge(o9_set, c - 1)
                    pool.tensor_copy(idx9[:, s, :], pos_u[:, ds(c * NT, NT)]).then_inc(idx9_set, 1)
                    pool.wait_ge(idx9_set, c + 1)
                    settled(pool)
                    for t in range(NT):
                        pool.indirect_dma_start(out=y9[:, s, t * P:(t + 1) * P], out_offset=None, in_=y_scr,
                                                in_offset=bass.IndirectOffsetOnAxis(idx9[:, s, t:t + 1], 0))\
                            .then_inc(y9_in[s], 16)
                run_stages(pool, NCH, [(0, gather), (1, lambda c, s: rstd(ln9)(pool, c))])

            @block.vector
            def _(dve):
                def finish(c, s):
                    dve.wait_ge(y9_in[s], (c - s) * 32 + 64)
                    dve.tensor_tensor(y9[:, s, :], y9[:, s, :], chunk_of(SH, c), ALU.add).then_inc(sum_set, 1)
                    dve.wait_ge(sum_set, c + 1)
                    layernorm(dve, c, ln9, tiles4(y9, s), tiles4(y9, s))
                    dve.wait_ge(ln9["steps"], c * LN_STEPS + LN_STEPS)
                    if late(c, 2):
                        dve.wait_ge(o9_out[s], (c - s) * 8)
                    dve.tensor_tensor(o9[:, s, :], chunk_of(X, c), y9[:, s, :], ALU.add).then_inc(o9_set, 1)
                run_stages(dve, NCH, [(0, finish)])

            @block.sync
            def _(sp):
                def store(c, s):
                    sp.wait_ge(o9_set, c + 1)
                    sp.dma_start(out[ds(c, 1)].rearrange("b (t p) e -> p (b t) e", p=P),
                                 o9[:, s, :].rearrange("p (t e) -> p t e", t=NT)).then_inc(o9_out[s], 16)
                run_stages(sp, NCH, [(0, store)])
                for s in range(2):
                    sp.wait_ge(o9_out[s], 8 * NCH)
        p9.close()


def _constants():
    import numpy as np

    n, f = np.arange(16), np.arange(9)
    ang = 2 * np.pi * np.outer(n, f) / 16
    fwd = np.zeros((16, 16))
    fwd[:, :9] = np.cos(ang)
    fwd[:, 9:] = -np.sin(ang)[:, 1:8]
    swp = np.zeros((16, 16))
    swp[:, 1:8] = fwd[:, 9:]
    swp[:, 9:] = fwd[:, 1:8]
    c1, c2 = np.zeros((16, 16)), np.zeros((16, 16))
    g1, g2 = np.zeros((16, 16)), np.zeros((16, 16))
    for k in range(9):
        w = 1.0 if k in (0, 8) else 2.0
        c1[k, k] = 1
        g1[k] = w * np.cos(ang[:, k]) / 16
        if w == 2:
            c1[8 + k, k] = -1
            c2[k, 8 + k] = c2[8 + k, 8 + k] = 1
            g1[8 + k] = g1[k]
            g2[k] = 2 * np.sin(ang[:, k]) / 16
            g2[8 + k] = -g2[k]
    heads = np.eye(8)
    mats = [fwd, swp, c1, c2, g1.T, g2.T]
    return {
        "ident": np.eye(128, dtype=np.float32),
        "tri": np.triu(np.ones((128, 128), np.float32), 1),
        "dft": np.stack([np.kron(heads, m) for m in mats]).astype(np.float32),
        "cls": (8 - np.arange(8, dtype=np.float32)).reshape(1, 8),
        "starts": (128 * np.arange(72, dtype=np.float32)).reshape(1, 72),
    }


def _layout(inputs):
    import numpy as np

    a = {k: np.asarray(v) for k, v in inputs.items()}
    turned = ["L0_attn_q_w", "L0_attn_k_w", "L0_attn_v_w", "L0_attn_out_w", "L0_ffn_w1_w", "L0_ffn_w2_w",
              "L0_ffn_h1_w", "L0_ffn_h2_w", "L0_ffn_w3_w", "L1_attn_w_qkv", "L1_ffn_gate_w",
              "L1_ffn_shared_gate", "L1_ffn_shared_up", "L1_ffn_shared_down"]
    for k in turned:
        a[k] = a[k].T
    for k in ("L1_ffn_r_gate", "L1_ffn_r_up", "L1_ffn_r_down"):
        a[k] = a[k].transpose(0, 2, 1)
    for k in ("L0_ffn_w1_s", "L0_ffn_w2_s", "L0_ffn_h1_s", "L0_ffn_h2_s"):
        a[k] = a[k].reshape(-1, 128).T
    for k in ("L0_attn_out_b", "L0_ffn_w3_s"):
        a[k] = a[k].reshape(1, -1)
    return a


def kernel(**inputs):
    import numpy as _np
    import concourse.bacc as _bacc
    from concourse import mybir as _mybir
    from concourse.bass_utils import run_bass_kernel_spmd as _run

    nc = _bacc.Bacc("TRN2", target_bir_lowering=False, num_devices=1)
    arrays, aps = {}, {}
    for name, a in {**_layout(inputs), **_constants()}.items():
        a = _np.ascontiguousarray(a)
        arrays[f"in_{name}"] = a
        aps[name] = nc.dram_tensor(f"in_{name}", a.shape, _mybir.dt.from_np(a.dtype), kind="ExternalInput").ap()
    out = nc.dram_tensor("out_0", aps["L0_attn_x"].shape, _mybir.dt.from_np(_np.dtype("float32")),
                         kind="ExternalOutput").ap()
    block_kernel(nc, aps, out)
    r = _run(nc, [arrays], core_ids=[0])
    return r.results[0]["out_0"]
```

```python
from contextlib import ExitStack

import concourse.bass as bass
from concourse import mybir

P = 128
F32 = mybir.dt.float32
BF16 = mybir.dt.bfloat16
I32 = mybir.dt.int32
U32 = mybir.dt.uint32
ALU = mybir.AluOpType
ACT = mybir.ActivationFunctionType
AX_X = mybir.AxisListType.X
ds = bass.ds

EPS = 1e-5
HD = 8
NPART = 3
ROWS = NPART * NPART * HD
KROWS = ROWS + NPART
BLK = 64
LN_STEPS = 13
NE = 8


def late(c, k):
    return not isinstance(c, int) or c >= k


def run_stages(eng, n, stages):
    most = max(lag for lag, _ in stages)
    peel = most + 2 + most % 2
    for c in range(peel):
        for lag, stage in stages:
            if 0 <= c - lag < n:
                stage(c - lag, (c - lag) % 2)
    if n > peel:
        with eng.Fori(peel // 2, n // 2) as u:
            r = u * 2
            for s in range(2):
                for lag, stage in stages:
                    k = s - lag
                    stage(r + k if k > 0 else r - (-k) if k < 0 else r, k % 2)
    for c in range(max(n, peel), n + most):
        for lag, stage in stages:
            if c - lag < n:
                stage(c - lag, (c - lag) % 2)


def block_kernel(nc, io, out):
    B, S, E = io["L0_attn_x"].shape
    NCH = B
    NT = S // P
    TILES = NCH * NT
    H0 = E // HD
    HG = 4
    NG = H0 // HG
    SCALE = 1.0 / float(HD) ** 0.5
    NB = S // BLK
    DH = io["L0_ffn_h1_w"].shape[0]
    FB = DH // P
    F1 = io["L1_ffn_shared_gate"].shape[1]
    FB1 = F1 // P
    ST_TILES = TILES + NE
    assert (E, S, NT, FB, FB1) == (P, 512, 4, 4, 2)

    q_scr = nc.dram_tensor("q_scr", (B, H0, 5, HD, S), BF16).ap()
    k_scr = nc.dram_tensor("k_scr", (B, H0, NPART, HD, S), BF16).ap()
    xs_scr = nc.dram_tensor("xs_scr", (ST_TILES * P, E), F32).ap()
    y_scr = nc.dram_tensor("y_scr", (ST_TILES * P, E), F32).ap()
    x_dram = io["L0_attn_x"]

    top = ExitStack()
    with top:
        def sem(name):
            return top.enter_context(nc.semaphore(name))

        def sb(name, shape, dt=F32, ctx=top):
            return ctx.enter_context(nc.sbuf_tensor(name, shape, dt))

        PS = top.enter_context(nc.psum_tensor("PS", [P, 8, 512], F32))
        X = sb("X", [P, TILES * E])
        XT = sb("XT", [P, TILES * E])
        zero = sb("zero", [P, 1024])
        idf = sb("idf", [P, P])
        idb = sb("idb", [P, P], BF16)
        neg_half = sb("neg_half", [P, NT])
        const_in = sem("const_in")
        held = sem("held")
        ones_set = sem("ones_set")

        def settled(eng):
            eng.sem_inc(held, 1)

        def ln_bufs(name, ctx):
            return dict(st=sb(name + "_st", [P, NT, 6], F32, ctx), mv=sb(name + "_mv", [P, NT, 2], F32, ctx),
                        ve=sb(name + "_ve", [P, NT], F32, ctx), rs=sb(name + "_rs", [P, NT], F32, ctx),
                        steps=sem(name + "_steps"), rstd=sem(name + "_rstd"))

        def layernorm(dve, c, ln, src, dst):
            ln_stats(dve, c, ln, src)
            ln_aggregate(dve, c, ln)
            ln_rows(dve, c, ln, src, dst)

        def ln_stats(dve, c, ln, src):
            settled(dve)
            for t in range(NT):
                dve.bn_stats(ln["st"][:, t, :], src(t)).then_inc(ln["steps"], 1)

        def ln_aggregate(dve, c, ln):
            steps, base = ln["steps"], c * LN_STEPS
            dve.wait_ge(steps, base + 4)
            settled(dve)
            for t in range(NT):
                dve.bn_aggr(ln["mv"][:, t, :], ln["st"][:, t, :]).then_inc(steps, 1)
            dve.wait_ge(steps, base + 8)
            dve.tensor_scalar(ln["ve"][:], ln["mv"][:, :, 1], EPS, None, ALU.add).then_inc(steps, 1)

        def ln_rows(dve, c, ln, src, dst):
            steps = ln["steps"]
            dve.wait_ge(ln["rstd"], c + 1)
            for t in range(NT):
                dve.tensor_scalar(dst(t), src(t), ln["mv"][:, t, 0:1], ln["rs"][:, t:t + 1],
                                  ALU.subtract, ALU.mult).then_inc(steps, 1)

        def rstd(ln):
            def stage(pool, c):
                pool.wait_ge(ln["steps"], c * LN_STEPS + 9)
                pool.tensor_tensor(ln["rs"][:], ln["ve"][:], neg_half[:], ALU.pow).then_inc(ln["rstd"], 1)
            return stage

        def tile_of(buf, c, t):
            return buf[:, ds(c * (NT * E) + t * E, E)]

        def chunk_of(buf, c):
            return buf[:, ds(c * (NT * E), NT * E)]

        att = ExitStack()
        V = sb("V", [P, TILES * E], F32, att)
        wq = sb("wq", [P, P], F32, att)
        wk = sb("wk", [P, P], F32, att)
        wv = sb("wv", [P, P], F32, att)
        p1 = ExitStack()
        xn1 = sb("xn1", [P, 2, S], F32, p1)
        xT1 = sb("xT1", [P, 2, S], F32, p1)
        parts = sb("parts", [P, 2, NPART, 2 * S], BF16, p1)
        resid = sb("resid", [P, 2, 2 * S], F32, p1)
        ln1 = ln_bufs("ln1", p1)
        x_in = [sem("x_in0"), sem("x_in1")]
        zero_out = sem("zero_out")
        turned1 = sem("turned1")
        xT1_set = sem("xT1_set")
        qk_done = sem("qk_done")
        v_done = sem("v_done")
        part1_set = sem("part1_set")
        v_set = sem("v_set")
        split_steps = sem("split_steps")
        part3_set = sem("part3_set")
        parts_out = [sem("parts_out0"), sem("parts_out1")]
        PARTS_DMA = 8 * 16
        AHEAD = 2

        with nc.Block() as block:
            @block.sync
            def _(sp):
                sp.dma_start(idf[:], io["ident"]).then_inc(const_in, 16)
                sp.dma_start(wq[:], io["L0_attn_q_w"]).then_inc(const_in, 16)
                sp.dma_start(wk[:], io["L0_attn_k_w"]).then_inc(const_in, 16)
                sp.dma_start(wv[:], io["L0_attn_v_w"]).then_inc(const_in, 16)

                def load(c, s):
                    if late(c, 2):
                        sp.wait_ge(x_in[s], (c - s) * 8)
                    sp.dma_start(chunk_of(X, c).rearrange("p (t e) -> p t e", t=NT),
                                 x_dram[ds(c, 1)].rearrange("b (t p) e -> p (b t) e", p=P)).then_inc(x_in[s], 16)

                def store_parts(c, s):
                    sp.wait_ge(part3_set, c + 1)
                    sp.wait_ge(split_steps, 2 * c + 2)
                    for j in range(5):
                        sp.dma_start(q_scr[ds(c, 1), :, j].rearrange("b h d t -> (b h) d t"),
                                     parts[:, s, j % NPART, 0:S]).then_inc(parts_out[s], 16)
                    for j in range(NPART):
                        sp.dma_start(k_scr[ds(c, 1), :, j].rearrange("b h d t -> (b h) d t"),
                                     parts[:, s, j, S:2 * S]).then_inc(parts_out[s], 16)
                for c in range(AHEAD):
                    load(c, c)
                for c in range(AHEAD):
                    store_parts(c, c)
                for s in range(2):
                    sp.wait_ge(parts_out[s], PARTS_DMA)

            @block.tensor
            def _(pe):
                pe.wait_ge(const_in, 64)

                def turn(c, s):
                    pe.wait_ge(ln1["steps"], c * LN_STEPS + LN_STEPS)
                    if late(c, 2):
                        pe.wait_ge(xT1_set, c - 1)
                    for t in range(NT):
                        mm = pe.transpose(PS[:, s, t * P:(t + 1) * P], xn1[:, s, t * P:(t + 1) * P], idf[:])
                    mm.then_inc(turned1, 1)

                def project(c, s):
                    pe.wait_ge(xT1_set, c + 1)
                    if late(c, 1):
                        pe.wait_ge(split_steps, 2 * c)
                    pe.matmul(PS[:, 2, :], wq[:], xT1[:, s, :], start=True, stop=True)
                    pe.matmul(PS[:, 3, :], wk[:], xT1[:, s, :], start=True, stop=True).then_inc(qk_done, 1)
                    if late(c, 2):
                        pe.wait_ge(v_set, c - 1)
                    for t in range(NT):
                        mm = pe.matmul(PS[:, 4 + s, t * P:(t + 1) * P], xT1[:, s, t * P:(t + 1) * P], wv[:],
                                       start=True, stop=True)
                    mm.then_inc(v_done, 1)

                run_stages(pe, AHEAD, [(0, turn), (1, project)])

            @block.scalar
            def _(act):
                def copy_xT(c, s):
                    act.wait_ge(turned1, c + 1)
                    if late(c, 2):
                        act.wait_ge(v_done, c - 1)
                    act.copy(xT1[:, s, :], PS[:, s, :]).then_inc(xT1_set, 1)

                def cast(c, s):
                    act.wait_ge(qk_done, c + 1)
                    if late(c, 2):
                        act.wait_ge(parts_out[s], (c - s) * (PARTS_DMA // 2))
                        act.wait_ge(part3_set, c - 1)
                    act.copy(parts[:, s, 0, :], PS[:, 2:4, :].rearrange("p a b -> p (a b)")).then_inc(part1_set, 1)
                    act.wait_ge(v_done, c + 1)
                    act.copy(chunk_of(V, c), PS[:, 4 + s, :]).then_inc(v_set, 1)

                run_stages(act, AHEAD, [(0, copy_xT), (1, cast)])

            @block.gpsimd
            def _(pool):
                pool.wait_ge(ones_set, 4)
                flat = xs_scr.rearrange("(n p a) e -> n p (a e)", p=P, a=8)
                for n in range(ST_TILES // 8):
                    pool.dma_start(flat[n], zero[:]).then_inc(zero_out, 16)

                def third(c, s):
                    pool.wait_ge(split_steps, 2 * c + 2)
                    if late(c, 2):
                        pool.wait_ge(parts_out[s], (c - s) * (PARTS_DMA // 2))
                    pool.tensor_tensor(parts[:, s, 2, :], resid[:, s, :], parts[:, s, 1, :],
                                       ALU.subtract).then_inc(part3_set, 1)
                run_stages(pool, AHEAD, [(0, lambda c, s: rstd(ln1)(pool, c)), (1, third)])

            @block.vector
            def _(dve):
                dve.memset(zero[:], 0.0).then_inc(ones_set, 1)
                dve.memset(neg_half[:], -0.5).then_inc(ones_set, 1)
                dve.memset(PS[:, 6:8, :], 0.0).then_inc(ones_set, 1)
                dve.wait_ge(const_in, 64)
                dve.tensor_copy(idb[:], idf[:]).then_inc(ones_set, 1)

                def norm(c, s):
                    dve.wait_ge(x_in[s], (c - s) * 8 + 16)
                    if late(c, 2):
                        dve.wait_ge(turned1, c - 1)
                    layernorm(dve, c, ln1, lambda t: tile_of(X, c, t), lambda t: xn1[:, s, t * P:(t + 1) * P])

                def split(c, s):
                    dve.wait_ge(part1_set, c + 1)
                    if late(c, 2):
                        dve.wait_ge(part3_set, c - 1)
                        dve.wait_ge(parts_out[s], (c - s) * (PARTS_DMA // 2))
                    dve.tensor_tensor(resid[:, s, :], PS[:, 2:4, :].rearrange("p a b -> p (a b)"),
                                      parts[:, s, 0, :], ALU.subtract).then_inc(split_steps, 1)
                    dve.wait_ge(split_steps, 2 * c + 1)
                    dve.tensor_copy(parts[:, s, 1, :], resid[:, s, :]).then_inc(split_steps, 1)

                run_stages(dve, AHEAD, [(0, norm), (1, split)])
        p1.close()

        p2 = ExitStack()
        QR = sb("QR", [KROWS, NG, HG, S], BF16, p2)
        KR = sb("KR", [KROWS, NG, HG, S], BF16, p2)
        EX = sb("EX", [P, 2, HG, S], F32, p2)
        VS = sb("VS", [P, NG, NT, HG, HD + 1], F32, p2)
        OT = sb("OT", [P, S], F32, p2)
        OTT = sb("OTT", [P, S], F32, p2)
        bmax = sb("bmax", [P, 2, NT * HG, NB], F32, p2)
        m_prev = sb("m_prev", [P, NT * HG], F32, p2)
        m_all = sb("m_all", [P, NT * HG], F32, p2)
        m_res = sb("m_res", [P, NT * HG], F32, p2)
        m_diff = sb("m_diff", [P, 2, NT * HG], F32, p2)
        m_part = sb("m_part", [P, 2, NPART, NT * HG], BF16, p2)
        m_row = sb("m_row", [NPART * NT * HG, 2, P], BF16, p2)
        corr = sb("corr", [P, NG, NT * HG], F32, p2)
        den = sb("den", [P, NT * HG], F32, p2)
        rden = sb("rden", [P, NT * HG], F32, p2)
        xnB = sb("xnB", [P, S], F32, p2)
        xTB = sb("xTB", [P, S], F32, p2)
        qkf = sb("qkf", [P, S], F32, p2)
        residB = sb("residB", [P, S], F32, p2)
        partsB = sb("partsB", [P, 2, NPART, S], BF16, p2)
        wo = sb("wo", [P, P], F32, p2)
        bias = sb("bias", [P, P], F32, p2)
        AOs = sb("AOs", [P, S], F32, p2)
        aT = sb("aT", [P, S], F32, p2)
        y3 = sb("y3", [P, S], F32, p2)
        xn2 = sb("xn2", [P, S], F32, p2)
        ln1b = ln_bufs("ln1b", p2)
        lnA = ln_bufs("lnA", p2)
        ln2 = ln_bufs("ln2", p2)
        load_in = [sem(f"load_in{i}") for i in range(NG)]
        mrow_in = [sem("mrow_in0"), sem("mrow_in1")]
        xB_in = sem("xB_in")
        w3_in = sem("w3_in")
        q_out = sem("q_out")
        k_out = sem("k_out")
        kones = sem("kones")
        vs_preset = sem("vs_preset")
        vs_set = sem("vs_set")
        pair_done = sem("pair_done")
        pair_max = sem("pair_max")
        st_done = sem("st_done")
        ex_set = sem("ex_set")
        pv_done = sem("pv_done")
        max_prev = sem("max_prev")
        max_all = sem("max_all")
        m_split = sem("m_split")
        mrow_set = sem("mrow_set")
        corr_set = sem("corr_set")
        ot_set = sem("ot_set")
        nrm_steps = sem("nrm_steps")
        split_B = sem("split_B")
        part1_B = sem("part1_B")
        y3_set = sem("y3_set")
        x3_set = sem("x3_set")
        use_done = sem("use_done")
        use_read = sem("use_read")
        M_SPLIT = 5
        GROUPS = NCH * NG
        TAIL = 7

        def kind_of(b, i, q):
            g = b * NG + i
            if q == 0:
                if i == 0:
                    return "value" if AHEAD <= b + 1 < NCH else None
                return ("turn", "query", "key")[i - 1] if b + 2 < NCH else None
            if q == 1:
                return "maxima" if 0 <= g - 1 < GROUPS else None
            if q == 2:
                return "outputs" if 0 <= g - 3 < GROUPS else None
            if i == 3:
                return "rows" if 0 <= b - 1 < NCH else None
            if i == 1:
                return None
            return ("project", "", "norm")[i] if 0 <= b - 2 < NCH else None

        uses = [(b, i, q) for b in range(NCH + 2) for i in range(NG) for q in range(NT) if kind_of(b, i, q)]
        PER_CHUNK = 4 * NG - 1
        STEADY = 3
        ENDING = NCH - 2

        def use(b, i, q):
            if isinstance(b, int):
                return uses.index((b, i, q))
            return b * PER_CHUNK + (uses.index((STEADY, i, q)) - STEADY * PER_CHUNK)

        def kind(b, i, q):
            return kind_of(b if isinstance(b, int) else STEADY, i, q)

        def run_groups(eng, step, tail):
            def at(b, i):
                g = b * NG + i
                step(b, i, g, lambda k: 0 <= g - k < GROUPS)
            for b in range(STEADY):
                for i in range(NG):
                    at(b, i)
            with eng.Fori(STEADY, ENDING) as b:
                for i in range(NG):
                    step(b, i, b * NG + i, lambda k: True)
            for g in range(ENDING * NG, GROUPS + tail):
                at(g // NG, g % NG)

        def behind(b, i, k):
            return (b - 1 if i - k < 0 else b), (i - k) % NG

        def some(n):
            return not (isinstance(n, int) and n <= 0)

        def exists(b):
            return not isinstance(b, int) or 0 <= b < NCH

        with nc.Block() as block:
            @block.sync
            def _(sp):
                sp.dma_start(wo[:], io["L0_attn_out_w"]).then_inc(w3_in, 16)
                sp.dma_start(bias[:], io["L0_attn_out_b"].to_broadcast([P, P])).then_inc(w3_in, 16)
                sp.wait_ge(kones, 1)

                def load(b, i):
                    for a in range(NPART):
                        rows = slice(a * NPART * HD, (a + 1) * NPART * HD)
                        sp.dma_start(QR[rows, i, :, :],
                                     q_scr[ds(b, 1), i * HG:(i + 1) * HG, a:a + NPART]
                                     .rearrange("b h j d t -> (j d) (b h) t")).then_inc(load_in[i], 16)
                        sp.dma_start(KR[rows, i, :, :],
                                     k_scr[ds(b, 1), i * HG:(i + 1) * HG]
                                     .rearrange("b h j d t -> (j d) (b h) t")).then_inc(load_in[i], 16)

                def load_max(i, g):
                    sp.wait_ge(mrow_set, g + 1)
                    sp.dma_start(QR[ROWS:KROWS, i].rearrange("r h q -> r (h q)"),
                                 m_row[:, i % 2, :]).then_inc(mrow_in[i % 2], 16)

                def load_x(b):
                    if some(b):
                        sp.wait_ge(xB_in, b * 16)
                        settled(sp)
                    sp.dma_start(chunk_of(X, b + 2).rearrange("p (t e) -> p t e", t=NT),
                                 x_dram[ds(b + 2, 1)].rearrange("b (t p) e -> p (b t) e", p=P)).then_inc(xB_in, 16)

                def store_q(d):
                    sp.wait_ge(split_B, (d - AHEAD) * 6 + 3)
                    settled(sp)
                    for j in range(5):
                        sp.dma_start(q_scr[ds(d, 1), :, j].rearrange("b h d t -> (b h) d t"),
                                     partsB[:, 0, j % NPART, :]).then_inc(q_out, 16)

                def store_k(d):
                    sp.wait_ge(split_B, (d - AHEAD) * 6 + 6)
                    settled(sp)
                    for j in range(NPART):
                        sp.dma_start(k_scr[ds(d, 1), :, j].rearrange("b h d t -> (b h) d t"),
                                     partsB[:, 1, j, :]).then_inc(k_out, 16)

                def step(b, i, g, has):
                    if i == 0 and exists(b + 2):
                        load_x(b)
                    if has(0):
                        if has(4):
                            sp.wait_ge(st_done, (g - 3) * 16)
                            settled(sp)
                        if i == 0 and some(b - 1):
                            sp.wait_ge(q_out, (b - 1) * (5 * 16))
                            settled(sp)
                            sp.wait_ge(k_out, (b - 1) * (3 * 16))
                            settled(sp)
                        load(b, i)
                    if has(2):
                        load_max((i - 2) % NG, g - 2)
                    if i < 2 and some(b) and exists(b + 1):
                        (store_q, store_k)[i](b + 1)
                run_groups(sp, step, 2)

            @block.tensor
            def _(pe):
                pe.wait_ge(w3_in, 32)

                def score_half(b, i, g, n):
                    t, h = n // HG, n % HG
                    pair = n // 2
                    if n == 0:
                        pe.wait_ge(load_in[i], b * 96 + 96)
                    if n % 2 == 0 and some(g * 8 + pair - 1):
                        pe.wait_ge(pair_max, g * 8 + pair - 1)
                    mm = pe.matmul(PS[:, 2 * (pair % 2) + n % 2, :], QR[0:ROWS, i, h, t * P:(t + 1) * P],
                                   KR[0:ROWS, i, h, :], start=True, stop=True)
                    if n % 2 == 1:
                        mm.then_inc(pair_done, 1)

                def score_T(j, g, n):
                    kt, h = n // HG, n % HG
                    if n == 0:
                        pe.wait_ge(mrow_in[j % 2], (g - j % 2) * 8 + 16)
                    if some(g * 16 + n - 1):
                        pe.wait_ge(ex_set, g * 16 + n - 1)
                    pe.matmul(PS[:, 4 + n % 2, :], KR[:, j, h, kt * P:(kt + 1) * P], QR[:, j, h, :],
                              start=True, stop=True).then_inc(st_done, 1)

                def pv(j, g, kt):
                    pe.wait_ge(ex_set, g * 16 + 4 * kt + 4)
                    if kt == 0:
                        pe.wait_ge(vs_set, g + 1)
                    if kt == 0 and some(g):
                        pe.wait_ge(ot_set, g)
                    for h in range(HG):
                        mm = pe.matmul(PS[32 * h:32 * h + HD + 1, 6, :], VS[:, j, kt, h, :],
                                       EX[:, kt % 2, h, :], start=(kt == 0), stop=(kt == NT - 1))
                    mm.then_inc(pv_done, 1)

                def free_bank(b, i, q):
                    if some(use(b, i, q)):
                        pe.wait_ge(use_read, use(b, i, q))

                def turn(src):
                    for t in range(NT):
                        mm = pe.transpose(PS[:, 7, t * P:(t + 1) * P], src[:, t * P:(t + 1) * P], idf[:])
                    mm.then_inc(use_done, 1)

                def by_rows(src, w):
                    for t in range(NT):
                        mm = pe.matmul(PS[:, 7, t * P:(t + 1) * P], src[:, t * P:(t + 1) * P], w[:],
                                       start=True, stop=True)
                    mm.then_inc(use_done, 1)

                def bank7(b, i, g, q):
                    k = kind(b, i, q)
                    if k is None:
                        return
                    if k == "turn":
                        pe.wait_ge(ln1b["steps"], b * LN_STEPS + LN_STEPS)
                    if k == "maxima":
                        pe.wait_ge(m_split, g * M_SPLIT)
                    if k == "outputs":
                        pe.wait_ge(ot_set, g - 2)
                    if k == "rows":
                        pe.wait_ge(nrm_steps, b * (3 * NG))
                    if k == "norm":
                        pe.wait_ge(ln2["steps"], (b - 2) * LN_STEPS + LN_STEPS)
                    free_bank(b, i, q)
                    if k == "turn":
                        turn(xnB)
                    elif k == "query":
                        pe.matmul(PS[:, 7, :], wq[:], xTB[:], start=True, stop=True).then_inc(use_done, 1)
                    elif k == "key":
                        pe.matmul(PS[:, 7, :], wk[:], xTB[:], start=True, stop=True).then_inc(use_done, 1)
                    elif k == "value":
                        by_rows(xTB, wv)
                    elif k == "maxima":
                        settled(pe)
                        pe.transpose(PS[0:NPART * NT * HG, 7, 0:P // 2].bitcast(BF16),
                                     m_part[:, (i - 1) % 2].rearrange("p a b -> p (a b)"),
                                     idb[:]).then_inc(use_done, 1)
                    elif k == "outputs":
                        turn(OT)
                    elif k == "rows":
                        turn(AOs)
                    elif k == "project":
                        by_rows(aT, wo)
                    elif k == "norm":
                        turn(xn2)

                ORDER = "TssTvTssT"

                def step(b, i, g, has):
                    for q in range(NT):
                        n_half = n_T = 4 * q
                        for what in ORDER:
                            if what == "s":
                                if has(0):
                                    score_half(b, i, g, n_half)
                                n_half += 1
                            elif what == "T":
                                if has(2):
                                    score_T((i - 2) % NG, g - 2, n_T)
                                n_T += 1
                            elif q == 0 and has(3):
                                pv((i - 3) % NG, g - 3, NT - 1)
                            elif q > 0 and has(2):
                                pv((i - 2) % NG, g - 2, q - 1)
                        bank7(b, i, g, q)
                run_groups(pe, step, TAIL)

            @block.scalar
            def _(act):
                def exps(g, n):
                    act.wait_ge(st_done, g * 16 + n + 1)
                    kt, h = n // HG, n % HG
                    if h == 0 and some(g * 4 + kt - 1):
                        act.wait_ge(pv_done, g * 4 + kt - 1)
                    act.activation(EX[:, kt % 2, h, :], PS[:, 4 + n % 2, :], ACT.Exp,
                                   scale=SCALE).then_inc(ex_set, 1)

                def copy_out(g):
                    act.wait_ge(pv_done, g * 4 + 4)
                    act.copy(OT[:], PS[:, 6, :]).then_inc(ot_set, 1)

                def correction(i, g):
                    act.wait_ge(m_split, g * M_SPLIT + 1)
                    if some(g - NG + 1):
                        act.wait_ge(nrm_steps, (g - NG + 1) * 3)
                    act.activation(corr[:, i, :], m_diff[:, i % 2, :], ACT.Exp, scale=SCALE).then_inc(corr_set, 1)

                def take(b, i, g, q):
                    k = kind(b, i, q)
                    if k is None or k == "project":
                        return
                    act.wait_ge(use_done, use(b, i, q) + 1)
                    bank = PS[:, 7, :]
                    if k == "turn":
                        act.copy(xTB[:], bank).then_inc(use_read, 1)
                    elif k == "query" or k == "key":
                        w = 0 if k == "query" else 1
                        n = b * 2 + w
                        if some(b):
                            act.wait_ge((q_out, k_out)[w], b * (16 * (5, 3)[w]))
                        act.copy(partsB[:, w, 0, :], bank).then_inc(part1_B, 1)
                        if some(n):
                            act.wait_ge(split_B, n * 3)
                        act.copy(qkf[:], bank).then_inc(use_read, 1)
                    elif k == "value":
                        act.copy(chunk_of(V, b + 1), bank).then_inc(use_read, 1)
                    elif k == "maxima":
                        if some((g - 1) - (i - 1) % 2):
                            act.wait_ge(mrow_in[(i - 1) % 2], ((g - 1) - (i - 1) % 2) * 8)
                        act.copy(m_row[:, (i - 1) % 2, :],
                                 PS[0:NPART * NT * HG, 7, 0:P // 2].bitcast(BF16)).then_inc(mrow_set, 1)
                    elif k == "outputs":
                        if some(g - 3):
                            act.wait_ge(nrm_steps, (g - 3) * 3)
                        act.copy(OTT[:], bank).then_inc(use_read, 1)
                    elif k == "rows":
                        act.copy(aT[:], bank).then_inc(use_read, 1)
                    elif k == "norm":
                        act.copy(chunk_of(XT, b - 2), bank).then_inc(use_read, 1)
                    if k == "maxima":
                        act.wait_ge(mrow_set, g)
                        act.sem_inc(use_read, 1)

                def step(b, i, g, has):
                    for n in range(NT * HG):
                        if has(2):
                            exps(g - 2, n)
                        if n == 0 and not (isinstance(g, int) and g == 0):
                            take(*behind(b, i, 1), g - 1, 3)
                        if n == 4 and has(3):
                            copy_out(g - 3)
                        if n == 5:
                            take(b, i, g, 0)
                        if n == 8:
                            take(b, i, g, 1)
                        if n == 9 and has(1):
                            correction((i - 1) % NG, g - 1)
                        if n == 12:
                            take(b, i, g, 2)
                run_groups(act, step, TAIL + 1)

            @block.gpsimd
            def _(pool):
                pool.wait_ge(vs_preset, 2)

                def stage_values(b, i, g):
                    if i == 0 and some(b - AHEAD + 1):
                        pool.wait_ge(use_read, use(b - 1, 0, 0) + 1)
                    if some(g - NG + 1):
                        pool.wait_ge(pv_done, (g - NG + 1) * 4)
                    settled(pool)
                    src = chunk_of(V, b).rearrange("p (t x) -> p t x", t=NT)[:, :, i * HG * HD:(i + 1) * HG * HD]
                    pool.tensor_copy(VS[:, i, :, :, 0:HD],
                                     src.rearrange("p t (h d) -> p t h d", d=HD)).then_inc(vs_set, 1)

                def split_max(i, g):
                    base, s = g * M_SPLIT, i % 2
                    pool.wait_ge(max_all, g + 1)
                    if some(g - 1):
                        pool.wait_ge(corr_set, g - 1)
                        pool.wait_ge(mrow_set, g - 1)
                    pool.tensor_tensor(m_diff[:, s, :], m_prev[:], m_all[:], ALU.subtract).then_inc(m_split, 1)
                    pool.tensor_copy(m_part[:, s, 0, :], m_all[:]).then_inc(m_split, 1)
                    pool.wait_ge(m_split, base + 2)
                    pool.tensor_tensor(m_res[:], m_all[:], m_part[:, s, 0, :], ALU.subtract).then_inc(m_split, 1)
                    pool.wait_ge(m_split, base + 3)
                    settled(pool)
                    pool.tensor_copy(m_part[:, s, 1, :], m_res[:]).then_inc(m_split, 1)
                    pool.wait_ge(m_split, base + 4)
                    pool.tensor_tensor(m_part[:, s, 2, :], m_res[:], m_part[:, s, 1, :],
                                       ALU.subtract).then_inc(m_split, 1)

                def split(b, w):
                    base = (b * 2 + w) * 3
                    pool.wait_ge(part1_B, b * 2 + w + 1)
                    pool.wait_ge(use_read, use(b, 2 + w, 0) + 1)
                    pool.tensor_tensor(residB[:], qkf[:], partsB[:, w, 0, :], ALU.subtract).then_inc(split_B, 1)
                    pool.wait_ge(split_B, base + 1)
                    settled(pool)
                    pool.tensor_copy(partsB[:, w, 1, :], residB[:]).then_inc(split_B, 1)
                    pool.wait_ge(split_B, base + 2)
                    pool.tensor_tensor(partsB[:, w, 2, :], residB[:], partsB[:, w, 1, :],
                                       ALU.subtract).then_inc(split_B, 1)

                def add_residual(c):
                    pool.wait_ge(lnA["steps"], c * LN_STEPS + LN_STEPS)
                    pool.tensor_tensor(chunk_of(X, c), chunk_of(X, c), y3[:], ALU.add).then_inc(x3_set, 1)

                def step(b, i, g, has):
                    if has(1):
                        split_max((i - 1) % NG, g - 1)
                    if has(0):
                        stage_values(b, i, g)
                    if i == 0 and exists(b + 2):
                        rstd(ln1b)(pool, b)
                    if i == 1 and exists(b - 2):
                        rstd(lnA)(pool, b - 2)
                        add_residual(b - 2)
                    if i == 2 and exists(b - 2):
                        rstd(ln2)(pool, b - 2)
                    if i >= 2 and exists(b + 2):
                        split(b, i - 2)
                run_groups(pool, step, TAIL)

            @block.vector
            def _(dve):
                dve.memset(KR[BLK:KROWS], -1.0).then_inc(kones, 1)
                dve.memset(VS[:], 0.0).then_inc(vs_preset, 1)
                dve.wait_ge(vs_preset, 1)
                dve.memset(VS[BLK:P, :, NT - 1, :, HD], 1.0).then_inc(vs_preset, 1)
                dve.wait_ge(w3_in, 32)

                def pair_reduce(i, g, u):
                    t, v = u // 2, u % 2
                    dve.wait_ge(pair_done, g * 8 + u + 1)
                    rows = bmax[:, i % 2].rearrange("p (h t) b -> p h t b", t=NT)
                    dve.tensor_reduce(rows[:, 2 * v:2 * v + 2, t, :],
                                      PS[:, 2 * (u % 2):2 * (u % 2) + 2, :].rearrange("p h (b k) -> p h b k", k=BLK),
                                      AX_X, ALU.max).then_inc(pair_max, 1)

                def previous_max(i, g):
                    dve.wait_ge(pair_max, g * 8 + 8)
                    if some(g):
                        dve.wait_ge(m_split, g * M_SPLIT)
                    dve.tensor_reduce(m_prev[:], bmax[:, i % 2, :, 0:NB - 1], AX_X, ALU.max).then_inc(max_prev, 1)

                def whole_max(i, g):
                    dve.wait_ge(max_prev, g + 1)
                    dve.tensor_tensor(m_all[:], m_prev[:], bmax[:, i % 2, :, NB - 1], ALU.max).then_inc(max_all, 1)

                def denominators(b, i, g):
                    G = g - NG
                    dve.wait_ge(use_read, use(*behind(b, i, 1), 2) + 1)
                    dve.wait_ge(corr_set, G + 1)
                    sums = OTT[:].rearrange("p (k d) -> p k d", d=32)[:, :, HD].rearrange("p (t h) -> p h t", t=NT)
                    dve.scalar_tensor_tensor(den[:].rearrange("p (h t) -> p h t", t=NT),
                                             corr[:, i, :].rearrange("p (h t) -> p h t", t=NT), 1.0, sums,
                                             ALU.add, ALU.mult).then_inc(nrm_steps, 1)

                def inverses(g):
                    dve.wait_ge(nrm_steps, (g - NG) * 3 + 1)
                    dve.reciprocal(rden[:], den[:]).then_inc(nrm_steps, 1)

                def normalise(b, i, g):
                    dve.wait_ge(nrm_steps, (g - NG) * 3 + 2)
                    if i == 0 and some(b - 1):
                        dve.wait_ge(use_done, use(b - 1, NG - 1, 3) + 1)
                    o = OTT[:].rearrange("p (k d) -> p k d", d=32)
                    dst = AOs[:].rearrange("p (t x) -> p t x", t=NT)[:, :, i * HG * HD:(i + 1) * HG * HD]
                    dve.tensor_tensor(dst.rearrange("p t (h d) -> p t h d", d=HD),
                                      o[:, :, 0:HD].rearrange("p (t h) d -> p t h d", t=NT),
                                      rden[:].rearrange("p (h t) -> p t h", t=NT).unsqueeze(3)
                                      .broadcast_to([P, NT, HG, HD]), ALU.mult).then_inc(nrm_steps, 1)

                def add_bias(b):
                    dve.wait_ge(use_done, use(b, 0, 3) + 1)
                    if some(b - 2):
                        dve.wait_ge(x3_set, b - 2)
                    dve.tensor_tensor(y3[:].rearrange("p (t e) -> p t e", t=NT),
                                      PS[:, 7, :].rearrange("p (t e) -> p t e", t=NT),
                                      bias[:].unsqueeze(1).broadcast_to([P, NT, E]), ALU.add).then_inc(use_read, 1)

                def tiles(buf):
                    return lambda t: buf[:, t * P:(t + 1) * P]

                def step(b, i, g, has):
                    ahead = i == 0 and exists(b + 2)
                    behind1 = i == 1 and exists(b - 2)
                    behind2 = i == 2 and exists(b - 2)
                    for u in range(8):
                        if has(0):
                            pair_reduce(i, g, u)
                        if u == 0:
                            if has(1):
                                whole_max((i - 1) % NG, g - 1)
                            if behind1:
                                add_bias(b)
                            if behind2:
                                dve.wait_ge(x3_set, b - 1)
                                ln_stats(dve, b - 2, ln2, lambda t: tile_of(X, b - 2, t))
                        if u == 1:
                            if has(4):
                                denominators(b, i, g)
                            if behind1:
                                dve.wait_ge(use_read, use(b, 0, 3) + 1)
                                ln_stats(dve, b - 2, lnA, tiles(y3))
                            if behind2:
                                ln_aggregate(dve, b - 2, ln2)
                        if u == 2:
                            if has(4):
                                inverses(g)
                            if ahead:
                                dve.wait_ge(xB_in, b * 16 + 16)
                                ln_stats(dve, b, ln1b, lambda t: tile_of(X, b + 2, t))
                            if behind1:
                                ln_aggregate(dve, b - 2, lnA)
                        if u == 3:
                            if has(4):
                                normalise(b, i, g)
                            if ahead:
                                ln_aggregate(dve, b, ln1b)
                            if behind2:
                                if some(b - 2):
                                    dve.wait_ge(use_done, use(b - 1, 2, 3) + 1)
                                ln_rows(dve, b - 2, ln2, lambda t: tile_of(X, b - 2, t), tiles(xn2))
                        if u == 4 and behind1:
                            ln_rows(dve, b - 2, lnA, tiles(y3), tiles(y3))
                        if u == 5 and ahead:
                            if some(b):
                                dve.wait_ge(use_done, use(b - 1, 1, 0) + 1)
                            ln_rows(dve, b, ln1b, lambda t: tile_of(X, b + 2, t), tiles(xnB))
                    if has(0):
                        previous_max(i, g)
                run_groups(dve, step, TAIL)
        p2.close()
        att.close()

        def tiles4(buf, s):
            return lambda t: buf[:, s, t * P:(t + 1) * P]

        AO = sb("AO", [P, TILES * E])

        p4 = ExitStack()
        w1 = sb("w1", [P, DH], F32, p4)
        w2 = sb("w2", [P, DH], F32, p4)
        hw = [sb("h1w", [P, FB, DH], F32, p4), sb("h2w", [P, FB, DH], F32, p4)]
        w3 = sb("w3", [P, FB, P], F32, p4)
        scales = sb("scales", [P, 4, FB], F32, p4)
        w3s = sb("w3s", [P, P], F32, p4)
        sil = sb("sil", [P, 2, S], F32, p4)
        hA = sb("hA", [P, 2, FB, S], F32, p4)
        hB = sb("hB", [P, 2, FB, S], F32, p4)
        y4 = sb("y4", [P, 2, S], F32, p4)
        xn3 = sb("xn3", [P, 2, S], F32, p4)
        lnB = ln_bufs("lnB", p4)
        ln3 = ln_bufs("ln3", p4)
        w4_in = sem("w4_in")
        in_done = sem("in_done")
        hid_done = sem("hid_done")
        mlp_done = sem("mlp_done")
        act_out = sem("act_out")
        h_set = sem("h_set")
        y4_set = sem("y4_set")
        x4_set = sem("x4_set")
        turned3 = sem("turned3")
        xT3_set = sem("xT3_set")
        PAIRS = NCH // 2

        def run_pairs(eng, step):
            step(0, True, False)
            step(1, True, True)
            with eng.Fori(2, PAIRS) as p:
                step(p, True, True)
            step(PAIRS, False, True)

        with nc.Block() as block:
            @block.sync
            def _(sp):
                sp.dma_start(w1[:], io["L0_ffn_w1_w"]).then_inc(w4_in, 16)
                sp.dma_start(w2[:], io["L0_ffn_w2_w"]).then_inc(w4_in, 16)
                for n, name in enumerate(("L0_ffn_w1_s", "L0_ffn_w2_s", "L0_ffn_h1_s", "L0_ffn_h2_s")):
                    sp.dma_start(scales[:, n, :], io[name]).then_inc(w4_in, 16)
                sp.dma_start(hw[0][:], io["L0_ffn_h1_w"].rearrange("(k p) o -> p k o", p=P)).then_inc(w4_in, 16)
                sp.dma_start(hw[1][:], io["L0_ffn_h2_w"].rearrange("(k p) o -> p k o", p=P)).then_inc(w4_in, 16)
                sp.dma_start(w3[:], io["L0_ffn_w3_w"].rearrange("(k p) o -> p k o", p=P)).then_inc(w4_in, 16)
                sp.dma_start(w3s[:], io["L0_ffn_w3_s"].to_broadcast([P, P])).then_inc(w4_in, 16)

            @block.tensor
            def _(pe):
                pe.wait_ge(w4_in, 160)

                def first(p):
                    return isinstance(p, int) and p == 0

                def layer_in(p, s):
                    xT = chunk_of(XT, 2 * p + s)
                    for f in range(FB):
                        n = 4 * s + f
                        if n >= 2:
                            pe.wait_ge(act_out, 24 * p + n - 1)
                            pe.wait_ge(h_set, 8 * p + n - 1)
                        elif not first(p):
                            pe.wait_ge(act_out, 24 * p - 2 + 2 * n)
                        for k, w in enumerate((w1, w2)):
                            pe.matmul(PS[:, 2 * (n % 2) + k, :], w[:, f * P:(f + 1) * P], xT,
                                      start=True, stop=True).then_inc(in_done, 1)

                def layer_hid(p, s, layer):
                    src = (hA, hB)[layer]
                    n = 2 * layer + s
                    pe.wait_ge(act_out, 24 * p + (4 * s + 4 if layer == 0 else 8 + 4 * s + 4))
                    if layer == 0:
                        pe.wait_ge(h_set, 8 * p + 4 * s + 4)
                    for f in range(FB):
                        if n == 0:
                            pe.wait_ge((act_out, h_set)[f % 2], (24 if f % 2 == 0 else 8) * p + 7 + f // 2)
                        else:
                            pe.wait_ge(act_out, 24 * p + 8 + 4 * (n - 1) + f + 1)
                        for k in range(FB):
                            mm = pe.matmul(PS[:, f, :], hw[layer][:, k, f * P:(f + 1) * P], src[:, s, k, :],
                                           start=(k == 0), stop=(k == FB - 1))
                        mm.then_inc(hid_done, 1)

                def layer_out(p, s):
                    pe.wait_ge(act_out, 24 * p + 16 + 4 * s + 4)
                    if not first(p):
                        pe.wait_ge(y4_set, 2 * p - 1 + s)
                    for t in range(NT):
                        for k in range(FB):
                            mm = pe.matmul(PS[:, 4 + s, t * P:(t + 1) * P], hA[:, s, k, t * P:(t + 1) * P],
                                           w3[:, k, :], start=(k == 0), stop=(k == FB - 1))
                    mm.then_inc(mlp_done, 1)

                def turn(p, s):
                    pe.wait_ge(ln3["steps"], (2 * p + s + 1) * LN_STEPS)
                    if not first(p):
                        pe.wait_ge(xT3_set, 2 * p - 1 + s)
                    for t in range(NT):
                        mm = pe.transpose(PS[:, 6 + s, t * P:(t + 1) * P], xn3[:, s, t * P:(t + 1) * P], idf[:])
                    mm.then_inc(turned3, 1)

                def step(p, now, before):
                    if now:
                        layer_in(p, 0)
                        layer_in(p, 1)
                        layer_hid(p, 0, 0)
                        layer_hid(p, 1, 0)
                        layer_hid(p, 0, 1)
                    if before:
                        turn(p - 1, 0)
                        turn(p - 1, 1)
                    if now:
                        layer_hid(p, 1, 1)
                        layer_out(p, 0)
                        layer_out(p, 1)
                run_pairs(pe, step)

            @block.gpsimd
            def _(pool):
                def step(p, now, before):
                    if before:
                        for s in range(2):
                            rstd(lnB)(pool, (p - 1) * 2 + s)
                            rstd(ln3)(pool, (p - 1) * 2 + s)
                run_pairs(pool, step)

            @block.scalar
            def _(act):
                act.wait_ge(w4_in, 160)

                def silus(p, s):
                    for f in range(FB):
                        n = 4 * s + f
                        act.wait_ge(in_done, 16 * p + 2 * n + 1)
                        if not (isinstance(p, int) and p == 0 and n < 2):
                            act.wait_ge(h_set, 8 * p + n - 1)
                        act.activation(sil[:, n % 2, :], PS[:, 2 * (n % 2), :], ACT.Silu,
                                       scale=scales[:, 0, f:f + 1]).then_inc(act_out, 1)

                def gelus(p, s, layer):
                    dst = (hB, hA)[layer]
                    for f in range(FB):
                        act.wait_ge(hid_done, 16 * p + 8 * layer + 4 * s + f + 1)
                        if f == 0 and not (isinstance(p, int) and p == 0 and layer == 0):
                            act.wait_ge(hid_done, 16 * p + 4 * s + (4 if layer else -4))
                        act.activation(dst[:, s, f, :], PS[:, f, :], ACT.Gelu,
                                       scale=scales[:, 2 + layer, f:f + 1]).then_inc(act_out, 1)

                def copy_xT(p, s):
                    act.wait_ge(turned3, 2 * p + s + 1)
                    act.copy(chunk_of(XT, 2 * p + s), PS[:, 6 + s, :]).then_inc(xT3_set, 1)

                def step(p, now, before):
                    if now:
                        silus(p, 0)
                        silus(p, 1)
                        gelus(p, 0, 0)
                        gelus(p, 1, 0)
                        gelus(p, 0, 1)
                    if before:
                        copy_xT(p - 1, 0)
                        copy_xT(p - 1, 1)
                    if now:
                        gelus(p, 1, 1)
                run_pairs(act, step)

            @block.vector
            def _(dve):
                dve.wait_ge(w4_in, 160)

                def gate(p, s):
                    if not (isinstance(p, int) and p == 0):
                        dve.wait_ge(mlp_done, 2 * p - 1 + s)
                    for f in range(FB):
                        n = 4 * s + f
                        dve.wait_ge(in_done, 16 * p + 2 * n + 2)
                        dve.wait_ge(act_out, 24 * p + n + 1)
                        dve.scalar_tensor_tensor(hA[:, s, f, :], PS[:, 2 * (n % 2) + 1, :], scales[:, 1, f:f + 1],
                                                 sil[:, n % 2, :], ALU.mult, ALU.mult).then_inc(h_set, 1)

                def residual(p, s):
                    c = 2 * p + s
                    dve.wait_ge(mlp_done, c + 1)
                    dve.tensor_tensor(y4[:, s, :].rearrange("p (t e) -> p t e", t=NT),
                                      PS[:, 4 + s, :].rearrange("p (t e) -> p t e", t=NT),
                                      w3s[:].unsqueeze(1).broadcast_to([P, NT, E]), ALU.mult).then_inc(y4_set, 1)
                    dve.wait_ge(y4_set, c + 1)
                    layernorm(dve, c, lnB, tiles4(y4, s), tiles4(y4, s))
                    dve.wait_ge(lnB["steps"], c * LN_STEPS + LN_STEPS)
                    dve.tensor_tensor(chunk_of(X, c), chunk_of(X, c), y4[:, s, :], ALU.add).then_inc(x4_set, 1)
                    dve.wait_ge(x4_set, c + 1)
                    if not (isinstance(p, int) and p == 0):
                        dve.wait_ge(turned3, c - 1)
                    layernorm(dve, c, ln3, lambda t: tile_of(X, c, t), tiles4(xn3, s))

                def step(p, now, before):
                    if now:
                        gate(p, 0)
                        gate(p, 1)
                    if before:
                        residual(p - 1, 0)
                        residual(p - 1, 1)
                run_pairs(dve, step)
        p4.close()

        p5 = ExitStack()
        wqkvT = sb("wqkvT", [P, 3, P], F32, p5)
        wout1 = sb("wout1", [P, P], F32, p5)
        dft = sb("dft", [P, 6, P], F32, p5)
        fold = sb("fold", [P, 8, P], F32, p5)
        gate_w = sb("gate_w", [P, NE], F32, p5)
        ones5 = sb("ones5", [P, S], F32, p5)
        kA = sb("kA", [P, 2, S], F32, p5)
        qq = sb("qq", [P, 2, 2, S], F32, p5)
        p12 = sb("p12", [P, 2, 2, S], F32, p5)
        csum = sb("csum", [P, 2, S], F32, p5)
        p34 = sb("p34", [P, 2, 2, S], F32, p5)
        y5 = sb("y5", [P, 2, S], F32, p5)
        xn4 = sb("xn4", [P, 2, S], F32, p5)
        xT4 = sb("xT4", [P, 2, S], F32, p5)
        lnC = ln_bufs("lnC", p5)
        ln4 = ln_bufs("ln4", p5)
        w5_in = sem("w5_in")
        folds_done = sem("folds_done")
        fold_set = sem("fold_set")
        ones5_set = sem("ones5_set")
        k_done = sem("k_done")
        q_done = sem("q_done")
        v5_done = sem("v5_done")
        kv_done = sem("kv_done")
        out5_done = sem("out5_done")
        turned4 = sem("turned4")
        logits_done = sem("logits_done")
        kA_set = sem("kA_set")
        qq_set = sem("qq_set")
        xT4_set = sem("xT4_set")
        p12_set = sem("p12_set")
        scan_set = sem("scan_set")
        p34_set = sem("p34_set")
        x5_set = sem("x5_set")
        xn4_kept = sem("xn4_kept")
        LB = 7

        with nc.Block() as block:
            @block.sync
            def _(sp):
                sp.dma_start(wqkvT[:], io["L1_attn_w_qkv"].rearrange("(k p) i -> p k i", p=P)).then_inc(w5_in, 16)
                sp.dma_start(wout1[:], io["L1_attn_w_out"]).then_inc(w5_in, 16)
                sp.dma_start(dft[:], io["dft"].rearrange("k p i -> p k i")).then_inc(w5_in, 16)
                sp.dma_start(gate_w[:], io["L1_ffn_gate_w"]).then_inc(w5_in, 16)

            @block.tensor
            def _(pe):
                pe.wait_ge(w5_in, 64)
                for n, (w, d) in enumerate(((1, 0), (2, 0), (2, 1), (0, 0), (0, 1))):
                    pe.matmul(PS[:, n // 4, (n % 4) * P:(n % 4 + 1) * P], wqkvT[:, w, :], dft[:, d, :],
                              start=True, stop=True)
                for n in (5, 6):
                    mm = pe.matmul(PS[:, n // 4, (n % 4) * P:(n % 4 + 1) * P], dft[:, n - 1, :], wout1[:],
                                   start=True, stop=True)
                mm.then_inc(folds_done, 1)
                pe.wait_ge(fold_set, 1)

                def project(c, s):
                    xT = chunk_of(XT, c)
                    if late(c, 1):
                        pe.wait_ge(kA_set, c)
                    if late(c, 4):
                        pe.wait_ge(xT4_set, 2 * c - 6)
                    pe.matmul(PS[:, 0, :], fold[:, 0, :], xT, start=True, stop=True).then_inc(k_done, 1)
                    if late(c, 1):
                        pe.wait_ge(qq_set, c)
                    pe.matmul(PS[:, 3, :], fold[:, 3, :], xT, start=True, stop=True)
                    pe.matmul(PS[:, 4, :], fold[:, 4, :], xT, start=True, stop=True).then_inc(q_done, 1)
                    if late(c, 1):
                        pe.wait_ge(p12_set, 2 * c)
                    pe.matmul(PS[:, 1, :], fold[:, 1, :], xT, start=True, stop=True)
                    pe.matmul(PS[:, 2, :], fold[:, 2, :], xT, start=True, stop=True).then_inc(v5_done, 1)

                def combine(c, s):
                    pe.wait_ge(p12_set, 2 * c + 2)
                    if late(c, 1):
                        pe.wait_ge(scan_set, c)
                    pe.matmul(PS[:, 5, :], dft[:, 2, :], p12[:, s, 0, :], start=True, stop=False)
                    pe.matmul(PS[:, 5, :], dft[:, 3, :], p12[:, s, 1, :], start=False, stop=True).then_inc(kv_done, 1)

                def output(c, s):
                    pe.wait_ge(p34_set, 2 * c + 2)
                    if late(c, 1):
                        pe.wait_ge(lnC["steps"], c * LN_STEPS)
                    for t in range(NT):
                        for k in range(2):
                            mm = pe.matmul(PS[:, 6, t * P:(t + 1) * P], p34[:, s, k, t * P:(t + 1) * P],
                                           fold[:, 5 + k, :], start=(k == 0), stop=(k == 1))
                    mm.then_inc(out5_done, 1)

                def turn(c, s):
                    pe.wait_ge(ln4["steps"], c * LN_STEPS + LN_STEPS)
                    pe.wait_ge(kA_set, min(c + 4, NCH) if isinstance(c, int) else c + 4)
                    if isinstance(c, int) and c + 4 > NCH:
                        pe.wait_ge(xT4_set, 2 * c)
                    for t in range(NT):
                        mm = pe.transpose(PS[:, 0, t * P:(t + 1) * P], xn4[:, s, t * P:(t + 1) * P], idf[:])
                    mm.then_inc(turned4, 1)

                def logits(c, s):
                    pe.wait_ge(xT4_set, 2 * c + 2)
                    for t in range(NT):
                        mm = pe.matmul(PS[:, LB, ds(c * (NT * NE) + t * NE, NE)], xT4[:, s, t * P:(t + 1) * P],
                                       gate_w[:], start=True, stop=True)
                    mm.then_inc(logits_done, 1)
                run_stages(pe, NCH, [(0, project), (1, combine), (2, output), (3, turn), (4, logits)])

            @block.scalar
            def _(act):
                act.wait_ge(folds_done, 1)
                act.copy(fold[:, 0:7, :], PS[:, 0:2, :].rearrange("p a (b e) -> p (a b) e", e=P)[:, 0:7, :])\
                   .then_inc(fold_set, 1)

                def copies(c, s):
                    act.wait_ge(k_done, c + 1)
                    if late(c, 2):
                        act.wait_ge(p12_set, 2 * c - 2)
                    act.copy(kA[:, s, :], PS[:, 0, :]).then_inc(kA_set, 1)
                    act.wait_ge(q_done, c + 1)
                    if late(c, 2):
                        act.wait_ge(p34_set, 2 * c - 2)
                    act.copy(qq[:, s], PS[:, 3:5, :]).then_inc(qq_set, 1)

                def copy_xT(c, s):
                    act.wait_ge(turned4, c + 1)
                    if late(c, 2):
                        act.wait_ge(logits_done, c - 1)
                    act.copy(xT4[:, s, :], PS[:, 0, :]).then_inc(xT4_set, 1)
                    act.copy(chunk_of(XT, c), PS[:, 0, :]).then_inc(xT4_set, 1)
                run_stages(act, NCH, [(0, copies), (3, copy_xT)])

            @block.gpsimd
            def _(pool):
                def spectra(c, s):
                    pool.wait_ge(scan_set, c + 1)
                    pool.wait_ge(qq_set, c + 1)
                    if late(c, 2):
                        pool.wait_ge(out5_done, c - 1)
                    for k in range(2):
                        pool.tensor_tensor(p34[:, s, k, :], qq[:, s, k, :], csum[:, s, :],
                                           ALU.mult).then_inc(p34_set, 1)

                def keep(c, s):
                    pool.wait_ge(ln4["steps"], c * LN_STEPS + LN_STEPS)
                    pool.tensor_copy(chunk_of(AO, c), xn4[:, s, :]).then_inc(xn4_kept, 1)
                run_stages(pool, NCH, [(3, keep), (1, spectra), (2, lambda c, s: rstd(lnC)(pool, c)),
                                       (2, lambda c, s: rstd(ln4)(pool, c))])

            @block.vector
            def _(dve):
                dve.memset(ones5[:], 1.0).then_inc(ones5_set, 1)
                dve.wait_ge(ones5_set, 1)

                def products(c, s):
                    dve.wait_ge(kA_set, c + 1)
                    dve.wait_ge(v5_done, c + 1)
                    if late(c, 2):
                        dve.wait_ge(kv_done, c - 1)
                    for k in range(2):
                        dve.tensor_tensor(p12[:, s, k, :], PS[:, 1 + k, :], kA[:, s, :], ALU.mult).then_inc(p12_set, 1)

                def scan(c, s):
                    dve.wait_ge(kv_done, c + 1)
                    if late(c, 2):
                        dve.wait_ge(p34_set, 2 * c - 2)
                    dve.tensor_tensor_scan(csum[:, s, :], ones5[:], PS[:, 5, :], 0.0, ALU.mult,
                                           ALU.add).then_inc(scan_set, 1)

                def residual(c, s):
                    dve.wait_ge(out5_done, c + 1)
                    layernorm(dve, c, lnC, lambda t: PS[:, 6, t * P:(t + 1) * P], tiles4(y5, s))
                    dve.wait_ge(lnC["steps"], c * LN_STEPS + LN_STEPS)
                    dve.tensor_tensor(chunk_of(X, c), chunk_of(X, c), y5[:, s, :], ALU.add).then_inc(x5_set, 1)
                    dve.wait_ge(x5_set, c + 1)
                    if late(c, 2):
                        dve.wait_ge(turned4, c - 1)
                        dve.wait_ge(xn4_kept, c - 1)
                    layernorm(dve, c, ln4, lambda t: tile_of(X, c, t), tiles4(xn4, s))
                run_stages(dve, NCH, [(0, products), (1, scan), (2, residual)])
        p5.close()

        SH = sb("SH", [P, TILES * E])
        TE = TILES * NE
        pos_u = sb("pos_u", [P, TILES], U32)
        score = sb("score", [P, TILES])
        tile_e = sb("tile_e", [P, ST_TILES], I32)
        p6 = ExitStack()
        lg = sb("lg", [P, TILES, NE], F32, p6)
        mx = sb("mx", [P, TILES], F32, p6)
        cand = sb("cand", [P, TILES, NE], F32, p6)
        best = sb("best", [P, TILES], F32, p6)
        oh = sb("oh", [P, NE, TILES], F32, p6)
        ohb = sb("ohb", [P, NE * TILES], BF16, p6)
        tri = sb("tri", [P, P], F32, p6)
        trib = sb("trib", [P, P], BF16, p6)
        onesb = sb("onesb", [P, P], BF16, p6)
        onesr = sb("onesr", [P, TE], F32, p6)
        cls = sb("cls", [P, NE], F32, p6)
        starts = sb("starts", [P, ST_TILES], F32, p6)
        incl = sb("incl", [P, TE], F32, p6)
        where = sb("where", [P, TE], F32, p6)
        cnt = sb("cnt", [P, 6, NE], F32, p6)
        cnti = sb("cnti", [P, 2, NE], I32, p6)
        posf = sb("posf", [P, TILES], F32, p6)
        texp = sb("texp", [P, ST_TILES], F32, p6)
        w6_in = sem("w6_in")
        r6 = sem("route_steps")
        mx_set = sem("mx_set")
        score_set = sem("score_set")
        ranks_done = sem("ranks_done")

        with nc.Block() as block:
            @block.sync
            def _(sp):
                sp.dma_start(tri[:], io["tri"]).then_inc(w6_in, 16)
                sp.dma_start(cls[:], io["cls"].to_broadcast([P, NE])).then_inc(w6_in, 16)
                sp.dma_start(starts[:], io["starts"].to_broadcast([P, ST_TILES])).then_inc(w6_in, 16)

            @block.scalar
            def _(act):
                act.wait_ge(mx_set, 1)
                act.activation(score[:], mx[:], ACT.Sigmoid).then_inc(score_set, 1)

            @block.tensor
            def _(pe):
                pe.wait_ge(r6, 9)
                pe.matmul(PS[:, 0, :], trib[:], ohb[:], start=True, stop=True)
                pe.matmul(PS[:, 1, :], onesb[:], ohb[:], start=True, stop=True).then_inc(ranks_done, 1)

            @block.vector
            def _(dve):
                n = [0]

                def then(ins):
                    n[0] += 1
                    ins.then_inc(r6, 1)
                    dve.wait_ge(r6, n[0])

                def b_te(col):
                    return col.unsqueeze(2).broadcast_to([P, TILES, NE])

                cls_te = cls[:].unsqueeze(1).broadcast_to([P, TILES, NE])
                oh_te = oh[:].rearrange("p e t -> p t e")
                dve.wait_ge(w6_in, 48)
                then(dve.tensor_copy(lg[:], PS[:, LB, :].rearrange("p (t e) -> p t e", e=NE)))
                dve.tensor_reduce(mx[:], lg[:], AX_X, ALU.max).then_inc(mx_set, 1)
                dve.wait_ge(mx_set, 1)
                then(dve.tensor_tensor(cand[:], lg[:], b_te(mx[:]), ALU.is_equal))
                then(dve.tensor_tensor(cand[:], cand[:], cls_te, ALU.mult))
                then(dve.tensor_reduce(best[:], cand[:], AX_X, ALU.max))
                then(dve.tensor_tensor(oh_te, b_te(best[:]), cls_te, ALU.is_equal))
                then(dve.tensor_copy(ohb[:], oh[:].rearrange("p e t -> p (e t)")))
                then(dve.tensor_copy(trib[:], tri[:]))
                then(dve.memset(onesb[:], 1.0))
                then(dve.memset(onesr[:], 1.0))
                dve.wait_ge(ranks_done, 1)
                then(dve.tensor_tensor_scan(incl[:], onesr[:], PS[:, 1, :], 0.0, ALU.mult, ALU.add))
                then(dve.tensor_tensor(where[:], incl[:], PS[:, 1, :], ALU.subtract))
                then(dve.tensor_tensor(where[:], where[:], PS[:, 0, :], ALU.add))
                ends = incl[:].rearrange("p (e t) -> p e t", e=NE)[:, :, TILES - 1]
                count, padded, pad_ends, shift, pad_ceil = (cnt[:, k, :] for k in range(5))
                then(dve.tensor_copy(count, ends))
                then(dve.tensor_tensor(count[:, 1:NE], ends[:, 1:NE], ends[:, 0:NE - 1], ALU.subtract))
                then(dve.tensor_scalar(pad_ceil, count, float(P - 1), None, ALU.add))
                then(dve.tensor_copy(cnti[:, 0, :], pad_ceil))
                then(dve.tensor_scalar(cnti[:, 1, :], cnti[:, 0, :], 7, 7, ALU.arith_shift_right,
                                       ALU.logical_shift_left))
                then(dve.tensor_copy(padded, cnti[:, 1, :]))
                then(dve.tensor_tensor_scan(pad_ends, onesr[:, 0:NE], padded, 0.0, ALU.mult, ALU.add))
                then(dve.tensor_tensor(shift, pad_ends, padded, ALU.subtract))
                then(dve.tensor_tensor(shift, shift, ends, ALU.subtract))
                then(dve.tensor_tensor(shift, shift, count, ALU.add))
                w_et = where[:].rearrange("p (e t) -> p e t", e=NE)
                then(dve.tensor_tensor(w_et, w_et, shift.unsqueeze(2).broadcast_to([P, NE, TILES]), ALU.add))
                then(dve.tensor_tensor(w_et, w_et, oh[:], ALU.mult))
                then(dve.tensor_reduce(posf[:], where[:].rearrange("p (e t) -> p t e", e=NE), AX_X, ALU.add))
                then(dve.tensor_copy(pos_u[:], posf[:]))
                then(dve.memset(texp[:], 0.0))
                for e in range(NE - 1):
                    then(dve.scalar_tensor_tensor(texp[:], starts[:], pad_ends[:, e:e + 1], texp[:],
                                                  ALU.is_ge, ALU.add))
                then(dve.tensor_copy(tile_e[:], texp[:]))
        p6.close()

        wgu = sb("wgu", [P, NE * 2 * F1])
        wdn = sb("wdn", [P, NE * FB1 * E])
        w8_in = sem("w8_in")
        p7 = ExitStack()
        sgu = sb("sgu", [P, 2, F1], F32, p7)
        sdn = sb("sdn", [P, FB1, P], F32, p7)
        sg = sb("sg", [P, 2, FB1, S], F32, p7)
        sh = sb("sh", [P, 2, FB1, S], F32, p7)
        xs = sb("xs", [P, 2, NT, E], F32, p7)
        idx = sb("idx", [P, 2, NT], U32, p7)
        w7_in = sem("w7_in")
        gu_done = sem("gu_done")
        sg_set = sem("sg_set")
        sh_set = sem("sh_set")
        dn_done = sem("dn_done")
        SH_set = sem("SH_set")
        xs_set = sem("xs_set")
        xs_out = [sem("xs_out0"), sem("xs_out1")]

        with nc.Block() as block:
            @block.sync
            def _(sp):
                sp.dma_start(sgu[:, 0, :], io["L1_ffn_shared_gate"]).then_inc(w7_in, 16)
                sp.dma_start(sgu[:, 1, :], io["L1_ffn_shared_up"]).then_inc(w7_in, 16)
                sp.dma_start(sdn[:], io["L1_ffn_shared_down"].rearrange("(k p) o -> p k o", p=P)).then_inc(w7_in, 16)
                g = wgu[:].rearrange("p (e u f) -> p e u f", e=NE, u=2)
                sp.dma_start(g[:, :, 0, :], io["L1_ffn_r_gate"].rearrange("e p f -> p e f")).then_inc(w8_in, 16)
                sp.dma_start(g[:, :, 1, :], io["L1_ffn_r_up"].rearrange("e p f -> p e f")).then_inc(w8_in, 16)
                sp.dma_start(wdn[:].rearrange("p (e k o) -> p e k o", e=NE, k=FB1),
                             io["L1_ffn_r_down"].rearrange("e (k p) o -> p e k o", p=P)).then_inc(w8_in, 16)

            @block.tensor
            def _(pe):
                pe.wait_ge(w7_in, 48)

                def expand(c, s):
                    for f in range(FB1):
                        if late(c, 1):
                            pe.wait_ge(sh_set, 2 * c + f - 1)
                        for u in range(2):
                            mm = pe.matmul(PS[:, 2 * f + u, :], sgu[:, u, f * P:(f + 1) * P], chunk_of(XT, c),
                                           start=True, stop=True)
                        mm.then_inc(gu_done, 1)

                def reduce(c, s):
                    pe.wait_ge(sh_set, 2 * c + 2)
                    if late(c, 2):
                        pe.wait_ge(SH_set, c - 1)
                    for t in range(NT):
                        for f in range(FB1):
                            mm = pe.matmul(PS[:, 4 + s, t * P:(t + 1) * P], sh[:, s, f, t * P:(t + 1) * P],
                                           sdn[:, f, :], start=(f == 0), stop=(f == FB1 - 1))
                    mm.then_inc(dn_done, 1)
                run_stages(pe, NCH, [(0, expand), (1, reduce)])

            @block.scalar
            def _(act):
                def silus(c, s):
                    for f in range(FB1):
                        act.wait_ge(gu_done, 2 * c + f + 1)
                        if late(c, 2):
                            act.wait_ge(sh_set, 2 * c - 2)
                        act.activation(sg[:, s, f, :], PS[:, 2 * f, :], ACT.Silu).then_inc(sg_set, 1)

                def keep(c, s):
                    act.wait_ge(dn_done, c + 1)
                    act.copy(chunk_of(SH, c), PS[:, 4 + s, :]).then_inc(SH_set, 1)
                run_stages(act, NCH, [(0, silus), (1, keep)])

            @block.gpsimd
            def _(pool):
                def scatter(c, s):
                    pool.wait_ge(xs_set, 5 * c + 5)
                    settled(pool)
                    if isinstance(c, int) and c == 0:
                        pool.wait_ge(zero_out, 16 * (ST_TILES // 8))
                    for t in range(NT):
                        pool.indirect_dma_start(out=xs_scr, out_offset=bass.IndirectOffsetOnAxis(idx[:, s, t:t + 1], 0),
                                                in_=xs[:, s, t, :], in_offset=None).then_inc(xs_out[s], 16)
                run_stages(pool, NCH, [(0, scatter)])
                for s in range(2):
                    pool.wait_ge(xs_out[s], NCH // 2 * NT * 16)

            @block.vector
            def _(dve):
                def scale(c, s):
                    if late(c, 2):
                        dve.wait_ge(xs_out[s], (c - s) * 32)
                    for t in range(NT):
                        dve.tensor_scalar(xs[:, s, t, :], tile_of(AO, c, t), score[:, ds(c * NT + t, 1)], None,
                                          ALU.mult).then_inc(xs_set, 1)
                    dve.tensor_copy(idx[:, s, :], pos_u[:, ds(c * NT, NT)]).then_inc(xs_set, 1)

                def gate(c, s):
                    if late(c, 2):
                        dve.wait_ge(dn_done, c - 1)
                    for f in range(FB1):
                        dve.wait_ge(gu_done, 2 * c + f + 1)
                        dve.wait_ge(sg_set, 2 * c + f + 1)
                        dve.tensor_tensor(sh[:, s, f, :], PS[:, 2 * f + 1, :], sg[:, s, f, :],
                                          ALU.mult).then_inc(sh_set, 1)
                run_stages(dve, NCH, [(0, scale), (0, gate)])
        p7.close()

        p8 = ExitStack()
        xt = sb("xt", [P, 2, E], F32, p8)
        xtT = sb("xtT", [P, 2, P], F32, p8)
        g8 = sb("g8", [P, 2, F1], F32, p8)
        h8 = sb("h8", [P, 2, F1], F32, p8)
        h8T = sb("h8T", [P, 2, FB1 * P], F32, p8)
        y8 = sb("y8", [P, 2, E], F32, p8)
        xt_in = [sem("xt_in0"), sem("xt_in1")]
        xt_turned = sem("xt_turned")
        xtT_set = sem("xtT_set")
        gu8_done = sem("gu8_done")
        g8_set = sem("g8_set")
        h8_set = sem("h8_set")
        h8_turned = sem("h8_turned")
        h8T_set = sem("h8T_set")
        y8_done = sem("y8_done")
        y8_set = sem("y8_set")
        y8_out = [sem("y8_out0"), sem("y8_out1")]
        xs_tiles = xs_scr.rearrange("(n p) e -> n p e", p=P)
        y_tiles = y_scr.rearrange("(n p) e -> n p e", p=P)

        with nc.Block() as block:
            @block.sync
            def _(sp):
                def load(j, s):
                    if late(j, 2):
                        sp.wait_ge(xt_turned, j - 1)
                    sp.dma_start(xt[:, s, :], xs_tiles[ds(j, 1)].rearrange("n p e -> p (n e)")).then_inc(xt_in[s], 16)

                def store(j, s):
                    sp.wait_ge(y8_set, j + 1)
                    sp.dma_start(y_tiles[ds(j, 1)].rearrange("n p e -> p (n e)"), y8[:, s, :]).then_inc(y8_out[s], 16)
                run_stages(sp, ST_TILES, [(0, load), (4, store)])
                for s in range(2):
                    sp.wait_ge(y8_out[s], 16 * (ST_TILES // 2))

            @block.tensor
            def _(pe):
                pe.wait_ge(w8_in, 48)

                def turn_x(j, s):
                    pe.wait_ge(xt_in[s], (j - s) * 8 + 16)
                    if late(j, 2):
                        pe.wait_ge(xtT_set, j - 1)
                    pe.transpose(PS[:, s, 0:P], xt[:, s, :], idf[:]).then_inc(xt_turned, 1)

                def expand(j, s):
                    e = pe.value_load(tile_e[0:1, ds(j, 1)], min_val=0, max_val=NE - 1)
                    pe.wait_ge(xtT_set, j + 1)
                    if late(j, 2):
                        pe.wait_ge(h8_set, j - 1)
                    pe.matmul(PS[:, 2 + s, :], xtT[:, s, :], wgu[:, ds(e * (2 * F1), 2 * F1)],
                              start=True, stop=True).then_inc(gu8_done, 1)

                def turn_h(j, s):
                    pe.wait_ge(h8_set, j + 1)
                    if late(j, 2):
                        pe.wait_ge(h8T_set, j - 1)
                    for f in range(FB1):
                        mm = pe.transpose(PS[:, 4 + s, f * P:(f + 1) * P], h8[:, s, f * P:(f + 1) * P], idf[:])
                    mm.then_inc(h8_turned, 1)

                def reduce(j, s):
                    e = pe.value_load(tile_e[0:1, ds(j, 1)], min_val=0, max_val=NE - 1)
                    pe.wait_ge(h8T_set, j + 1)
                    if late(j, 2):
                        pe.wait_ge(y8_set, j - 1)
                    for f in range(FB1):
                        mm = pe.matmul(PS[:, 6 + s, 0:E], h8T[:, s, f * P:(f + 1) * P],
                                       wdn[:, ds(e * (FB1 * E) + f * E, E)], start=(f == 0), stop=(f == FB1 - 1))
                    mm.then_inc(y8_done, 1)
                run_stages(pe, ST_TILES, [(0, turn_x), (1, expand), (2, turn_h), (3, reduce)])

            @block.scalar
            def _(act):
                def copy_xT(j, s):
                    act.wait_ge(xt_turned, j + 1)
                    if late(j, 2):
                        act.wait_ge(gu8_done, j - 1)
                    act.copy(xtT[:, s, :], PS[:, s, 0:P]).then_inc(xtT_set, 1)

                def silu(j, s):
                    act.wait_ge(gu8_done, j + 1)
                    if late(j, 2):
                        act.wait_ge(h8_set, j - 1)
                    act.activation(g8[:, s, :], PS[:, 2 + s, 0:F1], ACT.Silu).then_inc(g8_set, 1)

                def copy_y(j, s):
                    act.wait_ge(y8_done, j + 1)
                    if late(j, 2):
                        act.wait_ge(y8_out[s], (j - s) * 8)
                    act.copy(y8[:, s, :], PS[:, 6 + s, 0:E]).then_inc(y8_set, 1)
                run_stages(act, ST_TILES, [(0, copy_xT), (1, silu), (3, copy_y)])

            @block.vector
            def _(dve):
                def gate(j, s):
                    dve.wait_ge(g8_set, j + 1)
                    if late(j, 2):
                        dve.wait_ge(h8_turned, j - 1)
                    dve.tensor_tensor(h8[:, s, :], PS[:, 2 + s, F1:2 * F1], g8[:, s, :], ALU.mult).then_inc(h8_set, 1)

                def copy_hT(j, s):
                    dve.wait_ge(h8_turned, j + 1)
                    if late(j, 2):
                        dve.wait_ge(y8_done, j - 1)
                    dve.tensor_copy(h8T[:, s, :], PS[:, 4 + s, 0:FB1 * P]).then_inc(h8T_set, 1)
                run_stages(dve, ST_TILES, [(1, gate), (2, copy_hT)])
        p8.close()

        p9 = ExitStack()
        idx9 = sb("idx9", [P, 2, NT], U32, p9)
        y9 = sb("y9", [P, 2, S], F32, p9)
        o9 = sb("o9", [P, 2, S], F32, p9)
        ln9 = ln_bufs("ln9", p9)
        idx9_set = sem("idx9_set")
        y9_in = [sem("y9_in0"), sem("y9_in1")]
        sum_set = sem("sum_set")
        o9_set = sem("o9_set")
        o9_out = [sem("o9_out0"), sem("o9_out1")]

        with nc.Block() as block:
            @block.gpsimd
            def _(pool):
                def gather(c, s):
                    if late(c, 2):
                        pool.wait_ge(o9_set, c - 1)
                    pool.tensor_copy(idx9[:, s, :], pos_u[:, ds(c * NT, NT)]).then_inc(idx9_set, 1)
                    pool.wait_ge(idx9_set, c + 1)
                    settled(pool)
                    for t in range(NT):
                        pool.indirect_dma_start(out=y9[:, s, t * P:(t + 1) * P], out_offset=None, in_=y_scr,
                                                in_offset=bass.IndirectOffsetOnAxis(idx9[:, s, t:t + 1], 0))\
                            .then_inc(y9_in[s], 16)
                run_stages(pool, NCH, [(0, gather), (1, lambda c, s: rstd(ln9)(pool, c))])

            @block.vector
            def _(dve):
                def finish(c, s):
                    dve.wait_ge(y9_in[s], (c - s) * 32 + 64)
                    dve.tensor_tensor(y9[:, s, :], y9[:, s, :], chunk_of(SH, c), ALU.add).then_inc(sum_set, 1)
                    dve.wait_ge(sum_set, c + 1)
                    layernorm(dve, c, ln9, tiles4(y9, s), tiles4(y9, s))
                    dve.wait_ge(ln9["steps"], c * LN_STEPS + LN_STEPS)
                    if late(c, 2):
                        dve.wait_ge(o9_out[s], (c - s) * 8)
                    dve.tensor_tensor(o9[:, s, :], chunk_of(X, c), y9[:, s, :], ALU.add).then_inc(o9_set, 1)
                run_stages(dve, NCH, [(0, finish)])

            @block.sync
            def _(sp):
                def store(c, s):
                    sp.wait_ge(o9_set, c + 1)
                    sp.dma_start(out[ds(c, 1)].rearrange("b (t p) e -> p (b t) e", p=P),
                                 o9[:, s, :].rearrange("p (t e) -> p t e", t=NT)).then_inc(o9_out[s], 16)
                run_stages(sp, NCH, [(0, store)])
                for s in range(2):
                    sp.wait_ge(o9_out[s], 8 * NCH)
        p9.close()


def _constants():
    import numpy as np

    n, f = np.arange(16), np.arange(9)
    ang = 2 * np.pi * np.outer(n, f) / 16
    fwd = np.zeros((16, 16))
    fwd[:, :9] = np.cos(ang)
    fwd[:, 9:] = -np.sin(ang)[:, 1:8]
    swp = np.zeros((16, 16))
    swp[:, 1:8] = fwd[:, 9:]
    swp[:, 9:] = fwd[:, 1:8]
    c1, c2 = np.zeros((16, 16)), np.zeros((16, 16))
    g1, g2 = np.zeros((16, 16)), np.zeros((16, 16))
    for k in range(9):
        w = 1.0 if k in (0, 8) else 2.0
        c1[k, k] = 1
        g1[k] = w * np.cos(ang[:, k]) / 16
        if w == 2:
            c1[8 + k, k] = -1
            c2[k, 8 + k] = c2[8 + k, 8 + k] = 1
            g1[8 + k] = g1[k]
            g2[k] = 2 * np.sin(ang[:, k]) / 16
            g2[8 + k] = -g2[k]
    heads = np.eye(8)
    mats = [fwd, swp, c1, c2, g1.T, g2.T]
    return {
        "ident": np.eye(128, dtype=np.float32),
        "tri": np.triu(np.ones((128, 128), np.float32), 1),
        "dft": np.stack([np.kron(heads, m) for m in mats]).astype(np.float32),
        "cls": (8 - np.arange(8, dtype=np.float32)).reshape(1, 8),
        "starts": (128 * np.arange(72, dtype=np.float32)).reshape(1, 72),
    }


def _layout(inputs):
    import numpy as np

    a = {k: np.asarray(v) for k, v in inputs.items()}
    turned = ["L0_attn_q_w", "L0_attn_k_w", "L0_attn_v_w", "L0_attn_out_w", "L0_ffn_w1_w", "L0_ffn_w2_w",
              "L0_ffn_h1_w", "L0_ffn_h2_w", "L0_ffn_w3_w", "L1_attn_w_qkv", "L1_ffn_gate_w",
              "L1_ffn_shared_gate", "L1_ffn_shared_up", "L1_ffn_shared_down"]
    for k in turned:
        a[k] = a[k].T
    for k in ("L1_ffn_r_gate", "L1_ffn_r_up", "L1_ffn_r_down"):
        a[k] = a[k].transpose(0, 2, 1)
    for k in ("L0_ffn_w1_s", "L0_ffn_w2_s", "L0_ffn_h1_s", "L0_ffn_h2_s"):
        a[k] = a[k].reshape(-1, 128).T
    for k in ("L0_attn_out_b", "L0_ffn_w3_s"):
        a[k] = a[k].reshape(1, -1)
    return a


def kernel(**inputs):
    import numpy as _np
    import concourse.bacc as _bacc
    from concourse import mybir as _mybir
    from concourse.bass_utils import run_bass_kernel_spmd as _run

    nc = _bacc.Bacc("TRN2", target_bir_lowering=False, num_devices=1)
    arrays, aps = {}, {}
    for name, a in {**_layout(inputs), **_constants()}.items():
        a = _np.ascontiguousarray(a)
        arrays[f"in_{name}"] = a
        aps[name] = nc.dram_tensor(f"in_{name}", a.shape, _mybir.dt.from_np(a.dtype), kind="ExternalInput").ap()
    out = nc.dram_tensor("out_0", aps["L0_attn_x"].shape, _mybir.dt.from_np(_np.dtype("float32")),
                         kind="ExternalOutput").ap()
    block_kernel(nc, aps, out)
    r = _run(nc, [arrays], core_ids=[0])
    return r.results[0]["out_0"]
```

```python
from contextlib import ExitStack

import concourse.bass as bass
from concourse import mybir

P = 128
F32 = mybir.dt.float32
BF16 = mybir.dt.bfloat16
I32 = mybir.dt.int32
U32 = mybir.dt.uint32
ALU = mybir.AluOpType
ACT = mybir.ActivationFunctionType
AX_X = mybir.AxisListType.X
ds = bass.ds

EPS = 1e-5
HD = 8
NPART = 3
ROWS = NPART * NPART * HD
KROWS = ROWS + NPART
BLK = 64
LN_STEPS = 13
LN_SCALED = 10
NE = 8


def late(c, k):
    return not isinstance(c, int) or c >= k


def run_stages(eng, n, stages, ring=2):
    most = max(lag for lag, _ in stages)
    peel = -(-(most + ring) // ring) * ring
    for c in range(peel):
        for lag, stage in stages:
            if 0 <= c - lag < n:
                stage(c - lag, (c - lag) % ring)
    if n > peel:
        with eng.Fori(peel // ring, n // ring) as u:
            r = u * ring
            for s in range(ring):
                for lag, stage in stages:
                    k = s - lag
                    stage(r + k if k > 0 else r - (-k) if k < 0 else r, k % ring)
    for c in range(max(n, peel), n + most):
        for lag, stage in stages:
            if c - lag < n:
                stage(c - lag, (c - lag) % ring)


def block_kernel(nc, io, out):
    B, S, E = io["L0_attn_x"].shape
    NCH = B
    NT = S // P
    TILES = NCH * NT
    H0 = E // HD
    HG = 4
    NG = H0 // HG
    SCALE = 1.0 / float(HD) ** 0.5
    NB = S // BLK
    DH = io["L0_ffn_h1_w"].shape[0]
    FB = DH // P
    F1 = io["L1_ffn_shared_gate"].shape[1]
    FB1 = F1 // P
    ST_TILES = TILES + NE
    assert (E, S, NT, FB, FB1) == (P, 512, 4, 4, 2)

    q_scr = nc.dram_tensor("q_scr", (B, H0, 5, HD, S), BF16).ap()
    k_scr = nc.dram_tensor("k_scr", (B, H0, NPART, HD, S), BF16).ap()
    REGION = TILES * P + P
    ROW = 2 * E + 2
    row_scr = nc.dram_tensor("row_scr", (NE * REGION + P, ROW), F32).ap()
    x_dram = io["L0_attn_x"]

    top = ExitStack()
    with top:
        def sem(name):
            return top.enter_context(nc.semaphore(name))

        def sb(name, shape, dt=F32, ctx=top):
            return ctx.enter_context(nc.sbuf_tensor(name, shape, dt))

        PS = top.enter_context(nc.psum_tensor("PS", [P, 8, 512], F32))
        X = sb("X", [P, TILES * E])
        XT = sb("XT", [P, TILES * E])
        idf = sb("idf", [P, P])
        idb = sb("idb", [P, P], BF16)
        neg_half = sb("neg_half", [P, NT])
        const_in = sem("const_in")
        held = sem("held")
        ones_set = sem("ones_set")

        def settled(eng):
            eng.sem_inc(held, 1)

        def ln_bufs(name, ctx, steps=LN_STEPS):
            return dict(n=steps, nb=sb(name + "_nb", [P, NT], F32, ctx), st=sb(name + "_st", [P, NT, 6], F32, ctx), mv=sb(name + "_mv", [P, NT, 2], F32, ctx),
                        ve=sb(name + "_ve", [P, NT], F32, ctx), rs=sb(name + "_rs", [P, NT], F32, ctx),
                        steps=sem(name + "_steps"), rstd=sem(name + "_rstd"))

        def layernorm(dve, c, ln, src, dst):
            ln_stats(dve, c, ln, src)
            ln_aggregate(dve, c, ln)
            ln_rows(dve, c, ln, src, dst)

        def ln_stats(dve, c, ln, src):
            settled(dve)
            for t in range(NT):
                dve.bn_stats(ln["st"][:, t, :], src(t)).then_inc(ln["steps"], 1)

        def ln_aggregate(dve, c, ln):
            steps, base = ln["steps"], c * ln["n"]
            dve.wait_ge(steps, base + 4)
            settled(dve)
            for t in range(NT):
                dve.bn_aggr(ln["mv"][:, t, :], ln["st"][:, t, :]).then_inc(steps, 1)
            dve.wait_ge(steps, base + 8)
            dve.tensor_scalar(ln["ve"][:], ln["mv"][:, :, 1], EPS, None, ALU.add).then_inc(steps, 1)

        def ln_rows(dve, c, ln, src, dst):
            steps = ln["steps"]
            dve.wait_ge(ln["rstd"], c + 1)
            for t in range(NT):
                dve.tensor_scalar(dst(t), src(t), ln["mv"][:, t, 0:1], ln["rs"][:, t:t + 1],
                                  ALU.subtract, ALU.mult).then_inc(steps, 1)

        def ln_bias(dve, c, ln):
            dve.wait_ge(ln["rstd"], c + 1)
            dve.scalar_tensor_tensor(ln["nb"][:], ln["mv"][:, :, 0], -1.0, ln["rs"][:],
                                     ALU.mult, ALU.mult).then_inc(ln["steps"], 1)

        def rstd(ln):
            def stage(pool, c):
                pool.wait_ge(ln["steps"], c * ln["n"] + 9)
                pool.tensor_tensor(ln["rs"][:], ln["ve"][:], neg_half[:], ALU.pow).then_inc(ln["rstd"], 1)
            return stage

        def tile_of(buf, c, t):
            return buf[:, ds(c * (NT * E) + t * E, E)]

        def chunk_of(buf, c):
            return buf[:, ds(c * (NT * E), NT * E)]

        mlp = ExitStack()
        NWB = 3 + 2 * (io["L0_ffn_h1_w"].shape[0] // P)
        wb = sb("wb", [P, NWB, S], BF16, mlp)
        rounded = sb("rounded", [P, S], F32, mlp)
        att = ExitStack()
        V = sb("V", [P, TILES * E], F32, att)
        wq = sb("wq", [P, P], F32, att)
        wk = sb("wk", [P, P], F32, att)
        wv = sb("wv", [P, P], F32, att)
        KR = sb("KR", [KROWS, NG, HG, S], BF16, att)
        VS = sb("VS", [P, NG, NT, HG, HD + 1], F32, att)
        kones = sem("kones")
        vs_preset = sem("vs_preset")
        p1 = ExitStack()
        xn1 = sb("xn1", [P, 2, S], F32, p1)
        xT1 = sb("xT1", [P, 2, S], F32, p1)
        parts = sb("parts", [P, 2, NPART, 2 * S], BF16, p1)
        resid = sb("resid", [P, 2, 2 * S], F32, p1)
        ln1 = ln_bufs("ln1", p1)
        x_in = [sem("x_in0"), sem("x_in1")]
        turned1 = sem("turned1")
        xT1_set = sem("xT1_set")
        qk_done = sem("qk_done")
        v_done = sem("v_done")
        part1_set = sem("part1_set")
        v_set = sem("v_set")
        split_steps = sem("split_steps")
        part3_set = sem("part3_set")
        parts_out = [sem("parts_out0"), sem("parts_out1")]
        PARTS_DMA = 8 * 16
        AHEAD = 2

        with nc.Block() as block:
            @block.sync
            def _(sp):
                def load(c, s):
                    if late(c, 2):
                        sp.wait_ge(x_in[s], (c - s) * 8)
                    sp.dma_start(chunk_of(X, c).rearrange("p (t e) -> p t e", t=NT),
                                 x_dram[ds(c, 1)].rearrange("b (t p) e -> p (b t) e", p=P)).then_inc(x_in[s], 16)

                def store_parts(c, s):
                    sp.wait_ge(part3_set, c + 1)
                    sp.wait_ge(split_steps, 2 * c + 2)
                    for j in range(5):
                        sp.dma_start(q_scr[ds(c, 1), :, j].rearrange("b h d t -> (b h) d t"),
                                     parts[:, s, j % NPART, 0:S]).then_inc(parts_out[s], 16)
                    for j in range(NPART):
                        sp.dma_start(k_scr[ds(c, 1), :, j].rearrange("b h d t -> (b h) d t"),
                                     parts[:, s, j, S:2 * S]).then_inc(parts_out[s], 16)
                load(0, 0)
                sp.dma_start(idf[:], io["ident"]).then_inc(const_in, 16)
                sp.dma_start(wq[:], io["L0_attn_q_w"]).then_inc(const_in, 16)
                sp.dma_start(wk[:], io["L0_attn_k_w"]).then_inc(const_in, 16)
                sp.dma_start(wv[:], io["L0_attn_v_w"]).then_inc(const_in, 16)
                load(1, 1)
                for c in range(AHEAD):
                    store_parts(c, c)
                for s in range(2):
                    sp.wait_ge(parts_out[s], PARTS_DMA)

            @block.tensor
            def _(pe):
                pe.wait_ge(const_in, 64)

                def turn(c, s):
                    pe.wait_ge(ln1["steps"], c * LN_STEPS + LN_STEPS)
                    if late(c, 2):
                        pe.wait_ge(xT1_set, c - 1)
                    for t in range(NT):
                        mm = pe.transpose(PS[:, s, t * P:(t + 1) * P], xn1[:, s, t * P:(t + 1) * P], idf[:])
                    mm.then_inc(turned1, 1)

                def project(c, s):
                    pe.wait_ge(xT1_set, c + 1)
                    if late(c, 1):
                        pe.wait_ge(split_steps, 2 * c)
                    pe.matmul(PS[:, 2, :], wq[:], xT1[:, s, :], start=True, stop=True)
                    pe.matmul(PS[:, 3, :], wk[:], xT1[:, s, :], start=True, stop=True).then_inc(qk_done, 1)
                    if late(c, 2):
                        pe.wait_ge(v_set, c - 1)
                    for t in range(NT):
                        mm = pe.matmul(PS[:, 4 + s, t * P:(t + 1) * P], xT1[:, s, t * P:(t + 1) * P], wv[:],
                                       start=True, stop=True)
                    mm.then_inc(v_done, 1)

                run_stages(pe, AHEAD, [(0, turn), (1, project)])

            @block.scalar
            def _(act):
                def copy_xT(c, s):
                    act.wait_ge(turned1, c + 1)
                    if late(c, 2):
                        act.wait_ge(v_done, c - 1)
                    act.copy(xT1[:, s, :], PS[:, s, :]).then_inc(xT1_set, 1)

                def cast(c, s):
                    act.wait_ge(qk_done, c + 1)
                    if late(c, 2):
                        act.wait_ge(parts_out[s], (c - s) * (PARTS_DMA // 2))
                        act.wait_ge(part3_set, c - 1)
                    act.copy(parts[:, s, 0, :], PS[:, 2:4, :].rearrange("p a b -> p (a b)")).then_inc(part1_set, 1)
                    act.wait_ge(v_done, c + 1)
                    act.copy(chunk_of(V, c), PS[:, 4 + s, :]).then_inc(v_set, 1)

                run_stages(act, AHEAD, [(0, copy_xT), (1, cast)])

            @block.gpsimd
            def _(pool):
                pool.wait_ge(ones_set, 3)

                def third(c, s):
                    pool.wait_ge(split_steps, 2 * c + 2)
                    if late(c, 2):
                        pool.wait_ge(parts_out[s], (c - s) * (PARTS_DMA // 2))
                    pool.tensor_tensor(parts[:, s, 2, :], resid[:, s, :], parts[:, s, 1, :],
                                       ALU.subtract).then_inc(part3_set, 1)
                run_stages(pool, AHEAD, [(0, lambda c, s: rstd(ln1)(pool, c)), (1, third)])

            @block.vector
            def _(dve):
                dve.memset(neg_half[:], -0.5).then_inc(ones_set, 1)
                dve.memset(PS[:, 6:8, :], 0.0).then_inc(ones_set, 1)
                dve.wait_ge(const_in, 64)
                dve.tensor_copy(idb[:], idf[:]).then_inc(ones_set, 1)

                def norm(c, s):
                    dve.wait_ge(x_in[s], (c - s) * 8 + 16)
                    if late(c, 2):
                        dve.wait_ge(turned1, c - 1)
                    layernorm(dve, c, ln1, lambda t: tile_of(X, c, t), lambda t: xn1[:, s, t * P:(t + 1) * P])

                def split(c, s):
                    dve.wait_ge(part1_set, c + 1)
                    if late(c, 2):
                        dve.wait_ge(part3_set, c - 1)
                        dve.wait_ge(parts_out[s], (c - s) * (PARTS_DMA // 2))
                    dve.tensor_tensor(resid[:, s, :], PS[:, 2:4, :].rearrange("p a b -> p (a b)"),
                                      parts[:, s, 0, :], ALU.subtract).then_inc(split_steps, 1)
                    dve.wait_ge(split_steps, 2 * c + 1)
                    dve.tensor_copy(parts[:, s, 1, :], resid[:, s, :]).then_inc(split_steps, 1)

                def ones_rows(i):
                    dve.memset(KR[BLK:KROWS, i], -1.0).then_inc(kones, 1)

                norm(0, 0)
                norm(1, 1)
                ones_rows(0)
                ones_rows(1)
                split(0, 0)
                ones_rows(2)
                ones_rows(3)
                dve.memset(VS[:], 0.0).then_inc(vs_preset, 1)
                dve.memset(rounded[:], 0.0).then_inc(vs_preset, 1)
                dve.wait_ge(vs_preset, 2)
                dve.memset(VS[BLK:P, :, NT - 1, :, HD], 1.0).then_inc(vs_preset, 1)
                split(1, 1)
        p1.close()

        p2 = ExitStack()
        QR = sb("QR", [KROWS, NG, HG, S], BF16, p2)
        EX = sb("EX", [P, 2, HG, S], F32, p2)
        OT = sb("OT", [P, S], F32, p2)
        OTT = sb("OTT", [P, S], F32, p2)
        bmax = sb("bmax", [P, 2, NT * HG, NB], F32, p2)
        m_prev = sb("m_prev", [P, NT * HG], F32, p2)
        m_all = sb("m_all", [P, NT * HG], F32, p2)
        m_res = sb("m_res", [P, NT * HG], F32, p2)
        m_diff = sb("m_diff", [P, 2, NT * HG], F32, p2)
        m_part = sb("m_part", [P, 2, NPART, NT * HG], BF16, p2)
        m_row = sb("m_row", [NPART * NT * HG, 2, P], BF16, p2)
        corr = sb("corr", [P, NG, NT * HG], F32, p2)
        den = sb("den", [P, NT * HG], F32, p2)
        rden = sb("rden", [P, NT * HG], F32, p2)
        xnB = sb("xnB", [P, S], F32, p2)
        xTB = sb("xTB", [P, S], F32, p2)
        qkf = sb("qkf", [P, S], F32, p2)
        residB = sb("residB", [P, S], F32, p2)
        partsB = sb("partsB", [P, 2, NPART, S], BF16, p2)
        wo = sb("wo", [P, P], F32, p2)
        bias = sb("bias", [P, P], F32, p2)
        AOs = sb("AOs", [P, S], F32, p2)
        aT = sb("aT", [P, S], F32, p2)
        y3 = sb("y3", [P, S], F32, p2)
        xn2 = sb("xn2", [P, S], F32, p2)
        ln1b = ln_bufs("ln1b", p2)
        lnA = ln_bufs("lnA", p2)
        ln2 = ln_bufs("ln2", p2)
        w_raw = sb("w_raw", [P, 3, S], F32, p2)
        w_diff = sb("w_diff", [P, S], F32, p2)
        w_raw_in = [sem(f"w_raw_in{k}") for k in range(3)]
        w_cast = sem("w_cast")
        w_checked = sem("w_checked")
        load_in = [sem(f"load_in{i}") for i in range(NG)]
        mrow_in = [sem("mrow_in0"), sem("mrow_in1")]
        xB_in = sem("xB_in")
        w3_in = sem("w3_in")
        q_out = sem("q_out")
        k_out = sem("k_out")
        vs_set = sem("vs_set")
        pair_done = sem("pair_done")
        pair_max = sem("pair_max")
        st_done = sem("st_done")
        ex_set = sem("ex_set")
        pv_done = sem("pv_done")
        max_prev = sem("max_prev")
        max_all = sem("max_all")
        m_split = sem("m_split")
        mrow_set = sem("mrow_set")
        corr_set = sem("corr_set")
        ot_set = sem("ot_set")
        nrm_steps = sem("nrm_steps")
        split_B = sem("split_B")
        part1_B = sem("part1_B")
        y3_set = sem("y3_set")
        x3_set = sem("x3_set")
        use_done = sem("use_done")
        use_read = sem("use_read")
        M_SPLIT = 5
        GROUPS = NCH * NG
        TAIL = 7

        def kind_of(b, i, q):
            g = b * NG + i
            if q == 0:
                if i == 0:
                    return "value" if AHEAD <= b + 1 < NCH else None
                return ("turn", "query", "key")[i - 1] if b + 2 < NCH else None
            if q == 1:
                return "maxima" if 0 <= g - 1 < GROUPS else None
            if q == 2:
                return "outputs" if 0 <= g - 3 < GROUPS else None
            if i == 3:
                return "rows" if 0 <= b - 1 < NCH else None
            if i == 1:
                return None
            return ("project", "", "norm")[i] if 0 <= b - 2 < NCH else None

        uses = [(b, i, q) for b in range(NCH + 2) for i in range(NG) for q in range(NT) if kind_of(b, i, q)]
        PER_CHUNK = 4 * NG - 1
        STEADY = 3
        ENDING = NCH - 2

        def use(b, i, q):
            if isinstance(b, int):
                return uses.index((b, i, q))
            return b * PER_CHUNK + (uses.index((STEADY, i, q)) - STEADY * PER_CHUNK)

        def kind(b, i, q):
            return kind_of(b if isinstance(b, int) else STEADY, i, q)

        def run_groups(eng, step, tail):
            def at(b, i):
                g = b * NG + i
                step(b, i, g, lambda k: 0 <= g - k < GROUPS)
            for b in range(STEADY):
                for i in range(NG):
                    at(b, i)
            with eng.Fori(STEADY, ENDING) as b:
                for i in range(NG):
                    step(b, i, b * NG + i, lambda k: True)
            for g in range(ENDING * NG, GROUPS + tail):
                at(g // NG, g % NG)

        def behind(b, i, k):
            return (b - 1 if i - k < 0 else b), (i - k) % NG

        def some(n):
            return not (isinstance(n, int) and n <= 0)

        def exists(b):
            return not isinstance(b, int) or 0 <= b < NCH

        with nc.Block() as block:
            @block.sync
            def _(sp):
                sp.dma_start(wo[:], io["L0_attn_out_w"]).then_inc(w3_in, 16)
                sp.dma_start(bias[:], io["L0_attn_out_b"].to_broadcast([P, P])).then_inc(w3_in, 16)
                sp.wait_ge(kones, NG)

                def load(b, i):
                    for a in range(NPART):
                        rows = slice(a * NPART * HD, (a + 1) * NPART * HD)
                        sp.dma_start(QR[rows, i, :, :],
                                     q_scr[ds(b, 1), i * HG:(i + 1) * HG, a:a + NPART]
                                     .rearrange("b h j d t -> (j d) (b h) t")).then_inc(load_in[i], 16)
                        sp.dma_start(KR[rows, i, :, :],
                                     k_scr[ds(b, 1), i * HG:(i + 1) * HG]
                                     .rearrange("b h j d t -> (j d) (b h) t")).then_inc(load_in[i], 16)

                def load_max(i, g):
                    sp.wait_ge(mrow_set, g + 1)
                    sp.dma_start(QR[ROWS:KROWS, i].rearrange("r h q -> r (h q)"),
                                 m_row[:, i % 2, :]).then_inc(mrow_in[i % 2], 16)

                def load_x(b):
                    if some(b):
                        sp.wait_ge(xB_in, b * 16)
                        settled(sp)
                    sp.dma_start(chunk_of(X, b + 2).rearrange("p (t e) -> p t e", t=NT),
                                 x_dram[ds(b + 2, 1)].rearrange("b (t p) e -> p (b t) e", p=P)).then_inc(xB_in, 16)

                def store_q(d):
                    sp.wait_ge(split_B, (d - AHEAD) * 6 + 3)
                    settled(sp)
                    for j in range(5):
                        sp.dma_start(q_scr[ds(d, 1), :, j].rearrange("b h d t -> (b h) d t"),
                                     partsB[:, 0, j % NPART, :]).then_inc(q_out, 16)

                def store_k(d):
                    sp.wait_ge(split_B, (d - AHEAD) * 6 + 6)
                    settled(sp)
                    for j in range(NPART):
                        sp.dma_start(k_scr[ds(d, 1), :, j].rearrange("b h d t -> (b h) d t"),
                                     partsB[:, 1, j, :]).then_inc(k_out, 16)

                def load_weights(n):
                    if n >= 3:
                        sp.wait_ge(w_checked, 2 * n - 4)
                    dst = w_raw[:, n % 3, :]
                    if n < 2:
                        src = io[("L0_ffn_w1_w", "L0_ffn_w2_w")[n]]
                    elif n < NWB - 1:
                        k = (n - 2) % FB
                        src = io[("L0_ffn_h1_w", "L0_ffn_h2_w")[(n - 2) // FB]][k * P:(k + 1) * P]
                    else:
                        src = io["L0_ffn_w3_w"].rearrange("(k p) o -> p k o", p=P)
                        dst = dst.rearrange("p (k o) -> p k o", k=FB)
                    sp.dma_start(dst, src).then_inc(w_raw_in[n % 3], 16)

                def step(b, i, g, has):
                    if i == 0 and exists(b + 2):
                        load_x(b)
                    if has(0):
                        if has(4):
                            sp.wait_ge(st_done, (g - 3) * 16)
                            settled(sp)
                        if i == 0 and some(b - 1):
                            sp.wait_ge(q_out, (b - 1) * (5 * 16))
                            settled(sp)
                            sp.wait_ge(k_out, (b - 1) * (3 * 16))
                            settled(sp)
                        load(b, i)
                    if has(2):
                        load_max((i - 2) % NG, g - 2)
                    if i < 2 and some(b) and exists(b + 1):
                        (store_q, store_k)[i](b + 1)
                    if isinstance(g, int) and g < NWB:
                        load_weights(g)
                run_groups(sp, step, 2)

            @block.tensor
            def _(pe):
                pe.wait_ge(w3_in, 32)

                def score_half(b, i, g, n):
                    t, h = n // HG, n % HG
                    pair = n // 2
                    if n == 0:
                        pe.wait_ge(load_in[i], b * 96 + 96)
                    if n % 2 == 0 and some(g * 8 + pair - 1):
                        pe.wait_ge(pair_max, g * 8 + pair - 1)
                    mm = pe.matmul(PS[:, 2 * (pair % 2) + n % 2, :], QR[0:ROWS, i, h, t * P:(t + 1) * P],
                                   KR[0:ROWS, i, h, :], start=True, stop=True)
                    if n % 2 == 1:
                        mm.then_inc(pair_done, 1)

                def score_T(j, g, n):
                    kt, h = n // HG, n % HG
                    if n == 0:
                        pe.wait_ge(mrow_in[j % 2], (g - j % 2) * 8 + 16)
                    if some(g * 16 + n - 1):
                        pe.wait_ge(ex_set, g * 16 + n - 1)
                    pe.matmul(PS[:, 4 + n % 2, :], KR[:, j, h, kt * P:(kt + 1) * P], QR[:, j, h, :],
                              start=True, stop=True).then_inc(st_done, 1)

                def pv(j, g, kt):
                    pe.wait_ge(ex_set, g * 16 + 4 * kt + 4)
                    if kt == 0:
                        pe.wait_ge(vs_set, g + 1)
                    if kt == 0 and some(g):
                        pe.wait_ge(ot_set, g)
                    for h in range(HG):
                        mm = pe.matmul(PS[32 * h:32 * h + HD + 1, 6, :], VS[:, j, kt, h, :],
                                       EX[:, kt % 2, h, :], start=(kt == 0), stop=(kt == NT - 1))
                    mm.then_inc(pv_done, 1)

                def free_bank(b, i, q):
                    if some(use(b, i, q)):
                        pe.wait_ge(use_read, use(b, i, q))

                def turn(src):
                    for t in range(NT):
                        mm = pe.transpose(PS[:, 7, t * P:(t + 1) * P], src[:, t * P:(t + 1) * P], idf[:])
                    mm.then_inc(use_done, 1)

                def by_rows(src, w):
                    for t in range(NT):
                        mm = pe.matmul(PS[:, 7, t * P:(t + 1) * P], src[:, t * P:(t + 1) * P], w[:],
                                       start=True, stop=True)
                    mm.then_inc(use_done, 1)

                def bank7(b, i, g, q):
                    k = kind(b, i, q)
                    if k is None:
                        return
                    if k == "turn":
                        pe.wait_ge(ln1b["steps"], b * LN_STEPS + LN_STEPS)
                    if k == "maxima":
                        pe.wait_ge(m_split, g * M_SPLIT)
                    if k == "outputs":
                        pe.wait_ge(ot_set, g - 2)
                    if k == "rows":
                        pe.wait_ge(nrm_steps, b * (3 * NG))
                    if k == "norm":
                        pe.wait_ge(ln2["steps"], (b - 2) * LN_STEPS + LN_STEPS)
                    free_bank(b, i, q)
                    if k == "turn":
                        turn(xnB)
                    elif k == "query":
                        pe.matmul(PS[:, 7, :], wq[:], xTB[:], start=True, stop=True).then_inc(use_done, 1)
                    elif k == "key":
                        pe.matmul(PS[:, 7, :], wk[:], xTB[:], start=True, stop=True).then_inc(use_done, 1)
                    elif k == "value":
                        by_rows(xTB, wv)
                    elif k == "maxima":
                        settled(pe)
                        pe.transpose(PS[0:NPART * NT * HG, 7, 0:P // 2].bitcast(BF16),
                                     m_part[:, (i - 1) % 2].rearrange("p a b -> p (a b)"),
                                     idb[:]).then_inc(use_done, 1)
                    elif k == "outputs":
                        turn(OT)
                    elif k == "rows":
                        turn(AOs)
                    elif k == "project":
                        by_rows(aT, wo)
                    elif k == "norm":
                        turn(xn2)

                ORDER = "TssTvTssT"

                def step(b, i, g, has):
                    for q in range(NT):
                        n_half = n_T = 4 * q
                        for what in ORDER:
                            if what == "s":
                                if has(0):
                                    score_half(b, i, g, n_half)
                                n_half += 1
                            elif what == "T":
                                if has(2):
                                    score_T((i - 2) % NG, g - 2, n_T)
                                n_T += 1
                            elif q == 0 and has(3):
                                pv((i - 3) % NG, g - 3, NT - 1)
                            elif q > 0 and has(2):
                                pv((i - 2) % NG, g - 2, q - 1)
                        bank7(b, i, g, q)
                run_groups(pe, step, TAIL)

            @block.scalar
            def _(act):
                def exps(g, n):
                    act.wait_ge(st_done, g * 16 + n + 1)
                    kt, h = n // HG, n % HG
                    if h == 0 and some(g * 4 + kt - 1):
                        act.wait_ge(pv_done, g * 4 + kt - 1)
                    act.activation(EX[:, kt % 2, h, :], PS[:, 4 + n % 2, :], ACT.Exp,
                                   scale=SCALE).then_inc(ex_set, 1)

                def copy_out(g):
                    act.wait_ge(pv_done, g * 4 + 4)
                    act.copy(OT[:], PS[:, 6, :]).then_inc(ot_set, 1)

                def correction(i, g):
                    act.wait_ge(m_split, g * M_SPLIT + 1)
                    if some(g - NG + 1):
                        act.wait_ge(nrm_steps, (g - NG + 1) * 3)
                    act.activation(corr[:, i, :], m_diff[:, i % 2, :], ACT.Exp, scale=SCALE).then_inc(corr_set, 1)

                def take(b, i, g, q):
                    k = kind(b, i, q)
                    if k is None or k == "project":
                        return
                    act.wait_ge(use_done, use(b, i, q) + 1)
                    bank = PS[:, 7, :]
                    if k == "turn":
                        act.copy(xTB[:], bank).then_inc(use_read, 1)
                    elif k == "query" or k == "key":
                        w = 0 if k == "query" else 1
                        n = b * 2 + w
                        if some(b):
                            act.wait_ge((q_out, k_out)[w], b * (16 * (5, 3)[w]))
                        act.copy(partsB[:, w, 0, :], bank).then_inc(part1_B, 1)
                        if some(n):
                            act.wait_ge(split_B, n * 3)
                        act.copy(qkf[:], bank).then_inc(use_read, 1)
                    elif k == "value":
                        act.copy(chunk_of(V, b + 1), bank).then_inc(use_read, 1)
                    elif k == "maxima":
                        if some((g - 1) - (i - 1) % 2):
                            act.wait_ge(mrow_in[(i - 1) % 2], ((g - 1) - (i - 1) % 2) * 8)
                        act.copy(m_row[:, (i - 1) % 2, :],
                                 PS[0:NPART * NT * HG, 7, 0:P // 2].bitcast(BF16)).then_inc(mrow_set, 1)
                    elif k == "outputs":
                        if some(g - 3):
                            act.wait_ge(nrm_steps, (g - 3) * 3)
                        act.copy(OTT[:], bank).then_inc(use_read, 1)
                    elif k == "rows":
                        act.copy(aT[:], bank).then_inc(use_read, 1)
                    elif k == "norm":
                        act.copy(chunk_of(XT, b - 2), bank).then_inc(use_read, 1)
                    if k == "maxima":
                        act.wait_ge(mrow_set, g)
                        act.sem_inc(use_read, 1)

                def step(b, i, g, has):
                    for n in range(NT * HG):
                        if has(2):
                            exps(g - 2, n)
                        if n == 0 and not (isinstance(g, int) and g == 0):
                            take(*behind(b, i, 1), g - 1, 3)
                        if n == 3 and has(3):
                            copy_out(g - 3)
                        if n == 4:
                            take(b, i, g, 0)
                        if n == 8:
                            take(b, i, g, 1)
                        if n == 9 and has(1):
                            correction((i - 1) % NG, g - 1)
                        if n == 12:
                            take(b, i, g, 2)
                run_groups(act, step, TAIL + 1)

            @block.gpsimd
            def _(pool):
                pool.wait_ge(vs_preset, 3)

                def stage_values(b, i, g):
                    if i == 0 and some(b - AHEAD + 1):
                        pool.wait_ge(use_read, use(b - 1, 0, 0) + 1)
                    if some(g - NG + 1):
                        pool.wait_ge(pv_done, (g - NG + 1) * 4)
                    settled(pool)
                    src = chunk_of(V, b).rearrange("p (t x) -> p t x", t=NT)[:, :, i * HG * HD:(i + 1) * HG * HD]
                    pool.tensor_copy(VS[:, i, :, :, 0:HD],
                                     src.rearrange("p t (h d) -> p t h d", d=HD)).then_inc(vs_set, 1)

                def split_max(i, g):
                    base, s = g * M_SPLIT, i % 2
                    pool.wait_ge(max_all, g + 1)
                    if some(g - 1):
                        pool.wait_ge(corr_set, g - 1)
                        pool.wait_ge(mrow_set, g - 1)
                    pool.tensor_tensor(m_diff[:, s, :], m_prev[:], m_all[:], ALU.subtract).then_inc(m_split, 1)
                    pool.tensor_copy(m_part[:, s, 0, :], m_all[:]).then_inc(m_split, 1)
                    pool.wait_ge(m_split, base + 2)
                    pool.tensor_tensor(m_res[:], m_all[:], m_part[:, s, 0, :], ALU.subtract).then_inc(m_split, 1)
                    pool.wait_ge(m_split, base + 3)
                    settled(pool)
                    pool.tensor_copy(m_part[:, s, 1, :], m_res[:]).then_inc(m_split, 1)
                    pool.wait_ge(m_split, base + 4)
                    pool.tensor_tensor(m_part[:, s, 2, :], m_res[:], m_part[:, s, 1, :],
                                       ALU.subtract).then_inc(m_split, 1)

                def split(b, w):
                    base = (b * 2 + w) * 3
                    pool.wait_ge(part1_B, b * 2 + w + 1)
                    pool.wait_ge(use_read, use(b, 2 + w, 0) + 1)
                    pool.tensor_tensor(residB[:], qkf[:], partsB[:, w, 0, :], ALU.subtract).then_inc(split_B, 1)
                    pool.wait_ge(split_B, base + 1)
                    settled(pool)
                    pool.tensor_copy(partsB[:, w, 1, :], residB[:]).then_inc(split_B, 1)
                    pool.wait_ge(split_B, base + 2)
                    pool.tensor_tensor(partsB[:, w, 2, :], residB[:], partsB[:, w, 1, :],
                                       ALU.subtract).then_inc(split_B, 1)

                def add_residual(c):
                    pool.wait_ge(lnA["steps"], c * LN_STEPS + LN_STEPS)
                    pool.tensor_tensor(chunk_of(X, c), chunk_of(X, c), y3[:], ALU.add).then_inc(x3_set, 1)

                def cast_weights(n):
                    pool.wait_ge(w_raw_in[n % 3], (n // 3) * 16 + 16)
                    pool.tensor_copy(wb[:, n, :], w_raw[:, n % 3, :]).then_inc(w_cast, 1)

                def step(b, i, g, has):
                    if has(1):
                        split_max((i - 1) % NG, g - 1)
                    if isinstance(g, int) and g < NWB:
                        cast_weights(g)
                    if has(0):
                        stage_values(b, i, g)
                    if i == 0 and exists(b + 2):
                        rstd(ln1b)(pool, b)
                    if i == 1 and exists(b - 2):
                        rstd(lnA)(pool, b - 2)
                        add_residual(b - 2)
                    if i == 2 and exists(b - 2):
                        rstd(ln2)(pool, b - 2)
                    if i >= 2 and exists(b + 2):
                        split(b, i - 2)
                run_groups(pool, step, TAIL)

            @block.vector
            def _(dve):
                dve.wait_ge(w3_in, 32)

                def pair_reduce(i, g, u):
                    t, v = u // 2, u % 2
                    dve.wait_ge(pair_done, g * 8 + u + 1)
                    rows = bmax[:, i % 2].rearrange("p (h t) b -> p h t b", t=NT)
                    dve.tensor_reduce(rows[:, 2 * v:2 * v + 2, t, :],
                                      PS[:, 2 * (u % 2):2 * (u % 2) + 2, :].rearrange("p h (b k) -> p h b k", k=BLK),
                                      AX_X, ALU.max).then_inc(pair_max, 1)

                def previous_max(i, g):
                    dve.wait_ge(pair_max, g * 8 + 8)
                    if some(g):
                        dve.wait_ge(m_split, g * M_SPLIT)
                    dve.tensor_reduce(m_prev[:], bmax[:, i % 2, :, 0:NB - 1], AX_X, ALU.max).then_inc(max_prev, 1)

                def whole_max(i, g):
                    dve.wait_ge(max_prev, g + 1)
                    dve.tensor_tensor(m_all[:], m_prev[:], bmax[:, i % 2, :, NB - 1], ALU.max).then_inc(max_all, 1)

                def denominators(b, i, g):
                    G = g - NG
                    dve.wait_ge(use_read, use(*behind(b, i, 1), 2) + 1)
                    dve.wait_ge(corr_set, G + 1)
                    sums = OTT[:].rearrange("p (k d) -> p k d", d=32)[:, :, HD].rearrange("p (t h) -> p h t", t=NT)
                    dve.scalar_tensor_tensor(den[:].rearrange("p (h t) -> p h t", t=NT),
                                             corr[:, i, :].rearrange("p (h t) -> p h t", t=NT), 1.0, sums,
                                             ALU.add, ALU.mult).then_inc(nrm_steps, 1)

                def inverses(g):
                    dve.wait_ge(nrm_steps, (g - NG) * 3 + 1)
                    dve.reciprocal(rden[:], den[:]).then_inc(nrm_steps, 1)

                def normalise(b, i, g):
                    dve.wait_ge(nrm_steps, (g - NG) * 3 + 2)
                    if i == 0 and some(b - 1):
                        dve.wait_ge(use_done, use(b - 1, NG - 1, 3) + 1)
                    o = OTT[:].rearrange("p (k d) -> p k d", d=32)
                    dst = AOs[:].rearrange("p (t x) -> p t x", t=NT)[:, :, i * HG * HD:(i + 1) * HG * HD]
                    dve.tensor_tensor(dst.rearrange("p t (h d) -> p t h d", d=HD),
                                      o[:, :, 0:HD].rearrange("p (t h) d -> p t h d", t=NT),
                                      rden[:].rearrange("p (h t) -> p t h", t=NT).unsqueeze(3)
                                      .broadcast_to([P, NT, HG, HD]), ALU.mult).then_inc(nrm_steps, 1)

                def add_bias(b):
                    dve.wait_ge(use_done, use(b, 0, 3) + 1)
                    if some(b - 2):
                        dve.wait_ge(x3_set, b - 2)
                    dve.tensor_tensor(y3[:].rearrange("p (t e) -> p t e", t=NT),
                                      PS[:, 7, :].rearrange("p (t e) -> p t e", t=NT),
                                      bias[:].unsqueeze(1).broadcast_to([P, NT, E]), ALU.add).then_inc(use_read, 1)

                def tiles(buf):
                    return lambda t: buf[:, t * P:(t + 1) * P]

                def check_weights(n):
                    dve.wait_ge(w_cast, n + 1)
                    dve.tensor_tensor(w_diff[:], w_raw[:, n % 3, :], wb[:, n, :],
                                      ALU.not_equal).then_inc(w_checked, 1)
                    dve.wait_ge(w_checked, 2 * n + 1)
                    dve.tensor_tensor(rounded[:], rounded[:], w_diff[:], ALU.max).then_inc(w_checked, 1)

                def step(b, i, g, has):
                    ahead = i == 0 and exists(b + 2)
                    behind1 = i == 1 and exists(b - 2)
                    behind2 = i == 2 and exists(b - 2)
                    for u in range(8):
                        if has(0):
                            pair_reduce(i, g, u)
                        if u == 0:
                            if has(1):
                                whole_max((i - 1) % NG, g - 1)
                            if behind1:
                                add_bias(b)
                            if behind2:
                                dve.wait_ge(x3_set, b - 1)
                                ln_stats(dve, b - 2, ln2, lambda t: tile_of(X, b - 2, t))
                        if u == 1:
                            if has(4):
                                denominators(b, i, g)
                            if behind1:
                                dve.wait_ge(use_read, use(b, 0, 3) + 1)
                                ln_stats(dve, b - 2, lnA, tiles(y3))
                            if behind2:
                                ln_aggregate(dve, b - 2, ln2)
                        if u == 2:
                            if has(4):
                                inverses(g)
                            if ahead:
                                dve.wait_ge(xB_in, b * 16 + 16)
                                ln_stats(dve, b, ln1b, lambda t: tile_of(X, b + 2, t))
                            if behind1:
                                ln_aggregate(dve, b - 2, lnA)
                        if u == 3:
                            if has(4):
                                normalise(b, i, g)
                            if ahead:
                                ln_aggregate(dve, b, ln1b)
                            if behind2:
                                if some(b - 2):
                                    dve.wait_ge(use_done, use(b - 1, 2, 3) + 1)
                                ln_rows(dve, b - 2, ln2, lambda t: tile_of(X, b - 2, t), tiles(xn2))
                        if u == 4 and behind1:
                            ln_rows(dve, b - 2, lnA, tiles(y3), tiles(y3))
                        if u == 5 and ahead:
                            if some(b):
                                dve.wait_ge(use_done, use(b - 1, 1, 0) + 1)
                            ln_rows(dve, b, ln1b, lambda t: tile_of(X, b + 2, t), tiles(xnB))
                    if has(0):
                        previous_max(i, g)
                    if isinstance(g, int) and 1 <= g <= NWB:
                        check_weights(g - 1)
                run_groups(dve, step, TAIL)
        p2.close()
        att.close()

        def tiles4(buf, s):
            return lambda t: buf[:, s, t * P:(t + 1) * P]

        p4 = ExitStack()
        w1 = sb("w1", [P, DH], F32, p4)
        w2 = sb("w2", [P, DH], F32, p4)
        hw = [sb("h1w", [P, FB, DH], F32, p4), sb("h2w", [P, FB, DH], F32, p4)]
        w3 = sb("w3", [P, FB, P], F32, p4)
        scales = sb("scales", [P, 4, FB], F32, p4)
        w3s = sb("w3s", [P, P], F32, p4)
        sil = sb("sil", [P, 2, S], F32, p4)
        hA = sb("hA", [P, 2, FB, S], F32, p4)
        hB = sb("hB", [P, 2, FB, S], F32, p4)
        pX = sb("pX", [P, 2, NPART, S], BF16, p4)
        pA = sb("pA", [P, 2, FB, NPART, S], BF16, p4)
        pB = sb("pB", [P, 2, FB, NPART, S], BF16, p4)
        RRES = 4
        res4 = sb("res4", [P, RRES, S], F32, p4)
        y4 = sb("y4", [P, 2, S], F32, p4)
        xn3 = sb("xn3", [P, 2, S], F32, p4)
        any_rounded = sb("any_rounded", [P, 1], F32, p4)
        exact_w = sb("exact_w", [P, 1], I32, p4)
        lnB = ln_bufs("lnB", p4)
        ln3 = ln_bufs("ln3", p4)
        w4_in = sem("w4_in")
        s4_in = sem("s4_in")
        exact_steps = sem("exact_steps")
        in_done = sem("in_done")
        hid_done = sem("hid_done")
        mlp_done = sem("mlp_done")
        act_out = sem("act_out")
        gelu_set = sem("gelu_set")
        h_set = sem("h_set")
        first_set = sem("first_set")
        res_set = sem("res_set")
        second_act = sem("second_act")
        second_set = sem("second_set")
        third_set = sem("third_set")
        y4_set = sem("y4_set")
        x4_set = sem("x4_set")
        turned3 = sem("turned3")
        xT3_set = sem("xT3_set")
        PAIRS = NCH // 2
        SPLITS = 6 * FB + 2
        FIRSTS = 2 * FB + 2

        def run_pairs(eng, step):
            step(0, True, False)
            step(1, True, True)
            with eng.Fori(2, PAIRS - 1) as p:
                step(p, True, True)
            step(PAIRS - 1, True, True)
            step(PAIRS, False, True)

        def last(p):
            return isinstance(p, int) and p == PAIRS - 1

        def place_of(p, kind, s, f=0):
            if kind == "x":
                return 5 * FB + s
            return (2 * kind + s) * FB + f + (2 if (kind, s) == (2, 1) and not last(p) else 0)

        def splits(p, kind, s, f=0):
            return p * SPLITS + 2 + place_of(p, kind, s, f) + 1

        def seconds(p, kind, s, f=0):
            return p * (SPLITS - 2 * FB) + 2 + place_of(p, kind, s, f) - 2 * FB + 1

        with nc.Block() as block:
            @block.sync
            def _(sp):
                for n, name in enumerate(("L0_ffn_w1_s", "L0_ffn_w2_s", "L0_ffn_h1_s", "L0_ffn_h2_s")):
                    sp.dma_start(scales[:, n, :], io[name]).then_inc(s4_in, 16)
                sp.dma_start(w3s[:], io["L0_ffn_w3_s"].to_broadcast([P, P])).then_inc(s4_in, 16)
                sp.dma_start(w1[:], io["L0_ffn_w1_w"]).then_inc(w4_in, 16)
                sp.dma_start(w2[:], io["L0_ffn_w2_w"]).then_inc(w4_in, 16)
                sp.dma_start(hw[0][:], io["L0_ffn_h1_w"].rearrange("(k p) o -> p k o", p=P)).then_inc(w4_in, 16)
                sp.dma_start(hw[1][:], io["L0_ffn_h2_w"].rearrange("(k p) o -> p k o", p=P)).then_inc(w4_in, 16)
                sp.dma_start(w3[:], io["L0_ffn_w3_w"].rearrange("(k p) o -> p k o", p=P)).then_inc(w4_in, 16)
                sp.wait_ge(w4_in, 80)

            @block.tensor
            def _(pe):
                def first(p):
                    return isinstance(p, int) and p == 0

                def times(bank, terms, parts):
                    n = 0
                    todo = [(wl, x) if not turned else (x, wl)
                            for w32, w16, x32, xp, turned in terms
                            for wl, x in ([(w16, xp[j]) for j in range(NPART)] if parts else [(w32, x32)])]
                    for lhs, rhs in todo:
                        mm = pe.matmul(bank, lhs, rhs, start=(n == 0), stop=(n == len(todo) - 1))
                        n += 1
                    return mm

                def wb_of(n, f):
                    return wb[:, n, f * P:(f + 1) * P]

                def layer_in(p, s, parts):
                    pe.wait_ge(third_set, s + 1 if first(p) else splits(p - 1, "x", s))
                    xT = chunk_of(XT, 2 * p + s)
                    for f in range(FB):
                        n = 4 * s + f
                        if n >= 2:
                            pe.wait_ge(act_out, 24 * p + n - 1)
                            pe.wait_ge(h_set, 8 * p + n - 1)
                        elif not first(p):
                            pe.wait_ge(act_out, 24 * p - 2 + 2 * n)
                        for k, w in enumerate((w1, w2)):
                            times(PS[:, 2 * (n % 2) + k, :],
                                  [(w[:, f * P:(f + 1) * P], wb_of(k, f), xT, [pX[:, s, j, :] for j in range(NPART)],
                                    False)], parts).then_inc(in_done, 1)

                def layer_hid(p, s, layer, parts):
                    src = (hA, hB)[layer]
                    srcp = (pA, pB)[layer]
                    n = 2 * layer + s
                    pe.wait_ge(third_set, splits(p, layer, s, FB - 1))
                    for f in range(FB):
                        if n == 0:
                            pe.wait_ge((act_out, h_set)[f % 2], (24 if f % 2 == 0 else 8) * p + 7 + f // 2)
                        else:
                            pe.wait_ge(act_out, 24 * p + 8 + 4 * (n - 1) + f + 1)
                        times(PS[:, f, :],
                              [(hw[layer][:, k, f * P:(f + 1) * P], wb_of(2 + layer * FB + k, f), src[:, s, k, :],
                                [srcp[:, s, k, j, :] for j in range(NPART)], False) for k in range(FB)],
                              parts).then_inc(hid_done, 1)

                def layer_out(p, s, parts):
                    pe.wait_ge(third_set, splits(p, 2, s, FB - 1))
                    if not first(p):
                        pe.wait_ge(y4_set, 2 * p - 1 + s)
                    for t in range(NT):
                        tok = slice(t * P, (t + 1) * P)
                        mm = times(PS[:, 4 + s, tok],
                                   [(w3[:, k, :], wb_of(NWB - 1, k), hA[:, s, k, tok],
                                     [pA[:, s, k, j, tok] for j in range(NPART)], True) for k in range(FB)], parts)
                    mm.then_inc(mlp_done, 1)

                def turn(p, s):
                    pe.wait_ge(ln3["steps"], (2 * p + s + 1) * LN_STEPS)
                    if not first(p):
                        pe.wait_ge(xT3_set, 2 * p - 1 + s)
                    for t in range(NT):
                        mm = pe.transpose(PS[:, 6 + s, t * P:(t + 1) * P], xn3[:, s, t * P:(t + 1) * P], idf[:])
                    mm.then_inc(turned3, 1)

                def step_of(parts):
                    def step(p, now, before):
                        if now:
                            layer_in(p, 0, parts)
                        if before:
                            layer_out(p - 1, 1, parts)
                        if now:
                            layer_in(p, 1, parts)
                            layer_hid(p, 0, 0, parts)
                            layer_hid(p, 1, 0, parts)
                            layer_hid(p, 0, 1, parts)
                            layer_hid(p, 1, 1, parts)
                        if before:
                            turn(p - 1, 0)
                            turn(p - 1, 1)
                        if now:
                            layer_out(p, 0, parts)
                    return step

                pe.wait_ge(exact_steps, 1)
                pe.matmul(PS[0:1, 4, 0:1], any_rounded[:], any_rounded[:], start=True, stop=True)\
                    .then_inc(exact_steps, 1)
                pe.wait_ge(exact_steps, 3)
                exact = pe.value_load(exact_w[0:1, 0:1], min_val=0, max_val=1)
                with pe.If(exact == 1):
                    run_pairs(pe, step_of(True))
                with pe.Else():
                    pe.wait_ge(w4_in, 80)
                    run_pairs(pe, step_of(False))

            @block.gpsimd
            def _(pool):
                def third(dst, i):
                    pool.tensor_tensor(dst[:, 2, :], res4[:, i % RRES, :], dst[:, 1, :],
                                       ALU.subtract).then_inc(third_set, 1)

                def thirds(p, kind, s):
                    for f in range(FB):
                        if kind == 0:
                            pool.wait_ge(second_act, p * (2 * FB) + s * FB + f + 1)
                        else:
                            pool.wait_ge(second_set, seconds(p, kind, s, f))
                        third((pA, pB, pA)[kind][:, s, f], place_of(p, kind, s, f))

                def step(p, now, before):
                    if now:
                        thirds(p, 0, 0)
                        thirds(p, 0, 1)
                    if before:
                        rstd(lnB)(pool, (p - 1) * 2)
                        rstd(ln3)(pool, (p - 1) * 2)
                    if now:
                        thirds(p, 1, 0)
                    if before:
                        rstd(lnB)(pool, (p - 1) * 2 + 1)
                        rstd(ln3)(pool, (p - 1) * 2 + 1)
                    if now:
                        thirds(p, 1, 1)
                        thirds(p, 2, 0)
                        if not last(p):
                            for s in range(2):
                                pool.wait_ge(second_set, seconds(p, "x", s))
                                third(pX[:, s], place_of(p, "x", s))
                        thirds(p, 2, 1)
                for s in range(2):
                    pool.wait_ge(second_set, s + 1)
                    third(pX[:, s], s)
                run_pairs(pool, step)

            @block.scalar
            def _(act):

                def silu(p, n):
                    f = n % FB
                    act.wait_ge(in_done, 16 * p + 2 * n + 1)
                    if not (isinstance(p, int) and p == 0 and n < 2):
                        act.wait_ge(h_set, 8 * p + n - 1)
                    act.activation(sil[:, n % 2, :], PS[:, 2 * (n % 2), :], ACT.Silu,
                                   scale=scales[:, 0, f:f + 1]).then_inc(act_out, 1)

                def first_part(p, n):
                    act.wait_ge(h_set, 8 * p + n + 1)
                    act.copy(pA[:, n // FB, n % FB, 0, :], hA[:, n // FB, n % FB, :]).then_inc(first_set, 1)

                def second_part(p, n):
                    act.wait_ge(res_set, splits(p, 0, n // FB, n % FB))
                    act.copy(pA[:, n // FB, n % FB, 1, :], res4[:, n % RRES, :]).then_inc(second_act, 1)

                def first_x(c, s):
                    act.copy(pX[:, s, 0, :], chunk_of(XT, c)).then_inc(first_set, 1)

                def gelus(p, s, layer):
                    dst, dstp = (hB, hA)[layer], (pB, pA)[layer]
                    for f in range(FB):
                        act.wait_ge(hid_done, 16 * p + 8 * layer + 4 * s + f + 1)
                        if f == 0 and not (isinstance(p, int) and p == 0 and layer == 0):
                            act.wait_ge(hid_done, 16 * p + 4 * s + (4 if layer else -4))
                        act.activation(dst[:, s, f, :], PS[:, f, :], ACT.Gelu,
                                       scale=scales[:, 2 + layer, f:f + 1]).then_inc(gelu_set, 1)
                        act.activation(dstp[:, s, f, 0, :], PS[:, f, :], ACT.Gelu,
                                       scale=scales[:, 2 + layer, f:f + 1]).then_inc(act_out, 1)

                def copy_xT(p, s):
                    act.wait_ge(turned3, 2 * p + s + 1)
                    act.copy(chunk_of(XT, 2 * p + s), PS[:, 6 + s, :]).then_inc(xT3_set, 1)

                def step(p, now, before):
                    if now:
                        for n in range(2 * FB + 2):
                            if n < 2 * FB:
                                silu(p, n)
                            if 0 < n <= 2 * FB:
                                first_part(p, n - 1)
                            if n > 1:
                                second_part(p, n - 2)
                        gelus(p, 0, 0)
                        gelus(p, 1, 0)
                        gelus(p, 0, 1)
                    if now and not last(p):
                        for s in range(2):
                            act.wait_ge(in_done, 16 * p + 8 + 8 * s)
                            first_x(2 * p + 2 + s, s)
                    if now:
                        gelus(p, 1, 1)
                    if before:
                        copy_xT(p - 1, 0)
                        copy_xT(p - 1, 1)
                for s in range(2):
                    first_x(s, s)
                act.wait_ge(s4_in, 80)
                run_pairs(act, step)

            @block.vector
            def _(dve):
                dve.tensor_reduce(any_rounded[:], rounded[:], AX_X, ALU.max).then_inc(exact_steps, 1)
                dve.wait_ge(exact_steps, 2)
                dve.tensor_scalar(exact_w[0:1, :], PS[0:1, 4, 0:1], 0.0, None, ALU.is_equal).then_inc(exact_steps, 1)

                def gate(p, n):
                    s, f = n // FB, n % FB
                    if f == 0 and not (isinstance(p, int) and p == 0):
                        dve.wait_ge(mlp_done, 2 * p - 1 + s)
                    dve.wait_ge(in_done, 16 * p + 2 * n + 2)
                    dve.wait_ge(act_out, 24 * p + n + 1)
                    dve.scalar_tensor_tensor(hA[:, s, f, :], PS[:, 2 * (n % 2) + 1, :], scales[:, 1, f:f + 1],
                                             sil[:, n % 2, :], ALU.mult, ALU.mult).then_inc(h_set, 1)

                def residue(src, dst, k, i):
                    done = k - (2 if i < 2 else 6 if i < 4 else 4)
                    if not (isinstance(done, int) and done <= 0):
                        dve.wait_ge(third_set, done)
                    dve.tensor_tensor(res4[:, i % RRES, :], src, dst[:, 0, :], ALU.subtract).then_inc(res_set, 1)

                def second(dst, k, i):
                    dve.wait_ge(res_set, k)
                    dve.tensor_copy(dst[:, 1, :], res4[:, i % RRES, :]).then_inc(second_set, 1)

                def split_gelus(p, kind, s):
                    src, dst = (hA, hB, hA)[kind], (pA, pB, pA)[kind]
                    for f in range(FB + 1):
                        if f < FB:
                            dve.wait_ge(gelu_set, 16 * p + 8 * (kind - 1) + 4 * s + f + 1)
                            dve.wait_ge(act_out, 24 * p + 8 + 8 * (kind - 1) + 4 * s + f + 1)
                            residue(src[:, s, f, :], dst[:, s, f], splits(p, kind, s, f), place_of(p, kind, s, f))
                        if f > 0:
                            second(dst[:, s, f - 1], splits(p, kind, s, f - 1), place_of(p, kind, s, f - 1))

                def split_x(c, s, firsts, k, i):
                    dve.wait_ge(first_set, firsts)
                    residue(chunk_of(XT, c), pX[:, s], k, i)
                    second(pX[:, s], k, i)

                def residual(p, s):
                    c = 2 * p + s
                    dve.wait_ge(mlp_done, c + 1)
                    dve.tensor_tensor(y4[:, s, :].rearrange("p (t e) -> p t e", t=NT),
                                      PS[:, 4 + s, :].rearrange("p (t e) -> p t e", t=NT),
                                      w3s[:].unsqueeze(1).broadcast_to([P, NT, E]), ALU.mult).then_inc(y4_set, 1)
                    dve.wait_ge(y4_set, c + 1)
                    layernorm(dve, c, lnB, tiles4(y4, s), tiles4(y4, s))
                    dve.wait_ge(lnB["steps"], c * LN_STEPS + LN_STEPS)
                    dve.tensor_tensor(chunk_of(X, c), chunk_of(X, c), y4[:, s, :], ALU.add).then_inc(x4_set, 1)
                    dve.wait_ge(x4_set, c + 1)
                    if not (isinstance(p, int) and p == 0):
                        dve.wait_ge(turned3, c - 1)
                    layernorm(dve, c, ln3, lambda t: tile_of(X, c, t), tiles4(xn3, s))

                def step(p, now, before):
                    if now:
                        for n in range(2 * FB + 1):
                            if n < 2 * FB:
                                gate(p, n)
                            if n > 0:
                                m = n - 1
                                dve.wait_ge(first_set, p * FIRSTS + 2 + m + 1)
                                residue(hA[:, m // FB, m % FB, :], pA[:, m // FB, m % FB],
                                        splits(p, 0, m // FB, m % FB), m)
                    if before:
                        residual(p - 1, 0)
                    if now:
                        split_gelus(p, 1, 0)
                    if before:
                        residual(p - 1, 1)
                    if now:
                        split_gelus(p, 1, 1)
                        split_gelus(p, 2, 0)
                        if not last(p):
                            for s in range(2):
                                split_x(2 * p + 2 + s, s, p * FIRSTS + 2 + 2 * FB + s + 1, splits(p, "x", s),
                                        place_of(p, "x", s))
                        split_gelus(p, 2, 1)
                for s in range(2):
                    split_x(s, s, s + 1, s + 1, s)
                dve.wait_ge(s4_in, 80)
                run_pairs(dve, step)
        p4.close()
        mlp.close()

        AO = sb("AO", [P, TILES * E])
        tri = sb("tri", [P, P])
        cls = sb("cls", [P, NE])
        starts = sb("starts", [P, ST_TILES])
        firsts = sb("firsts", [P, NE])
        filled = sb("filled", [P, NE])
        sgu = sb("sgu", [P, 2 * F1])
        sdn = sb("sdn", [P, FB1, P])
        wgu = sb("wgu", [P, NE * 2 * F1])
        wdn = sb("wdn", [P, NE * FB1 * E])
        tile_e = sb("tile_e", [P, ST_TILES], I32)
        tile_row = sb("tile_row", [P, ST_TILES], I32)
        p5 = ExitStack()
        wqkvT = sb("wqkvT", [P, 3, P], F32, p5)
        wout1 = sb("wout1", [P, P], F32, p5)
        dft = sb("dft", [P, 6, P], F32, p5)
        fold = sb("fold", [P, 8, P], F32, p5)
        gate_w = sb("gate_w", [P, NE], F32, p5)
        ids = sb("ids", [P, TILES], F32, p5)
        trib = sb("trib", [P, P], BF16, p5)
        onesb = sb("onesb", [P, P], BF16, p5)
        ones5 = sb("ones5", [P, S], F32, p5)
        kA = sb("kA", [P, 2, S], F32, p5)
        qq = sb("qq", [P, 2, 2, S], F32, p5)
        p12 = sb("p12", [P, 2, 2, S], F32, p5)
        csum = sb("csum", [P, 2, S], F32, p5)
        p34 = sb("p34", [P, 2, 2, S], F32, p5)
        y5 = sb("y5", [P, S], F32, p5)
        xn4 = sb("xn4", [P, 2, S], F32, p5)
        xT4 = sb("xT4", [P, 2, S], F32, p5)
        lg = sb("lg", [P, 2, NT, NE], F32, p5)
        mx = sb("mx", [P, 2, NT], F32, p5)
        cand = sb("cand", [P, NT, NE], F32, p5)
        best = sb("best", [P, NT], F32, p5)
        ohb = sb("ohb", [P, 2, NT, NE], BF16, p5)
        rk = sb("rk", [P, 2, (NT + 1) * NE], F32, p5)
        where = sb("where", [P, NT, NE], F32, p5)
        posf = sb("posf", [P, NT], F32, p5)
        idx = sb("idx", [P, 2, NT], U32, p5)
        row = sb("row", [P, 2, NT, ROW], F32, p5)
        lnC = ln_bufs("lnC", p5, LN_SCALED)
        ln4 = ln_bufs("ln4", p5, LN_SCALED)
        pad = sb("pad", [P, ROW], F32, p5)
        count = sb("count", [P, NE], F32, p5)
        cnti = sb("cnti", [P, 2, NE], I32, p5)
        end_i = sb("end_i", [P, NE], I32, p5)
        padded = sb("padded", [P, NE], F32, p5)
        pad_ends = sb("pad_ends", [P, NE], F32, p5)
        skip = sb("skip", [P, NE], F32, p5)
        ones6 = sb("ones6", [P, NE], F32, p5)
        past = sb("past", [P, ST_TILES, NE], F32, p5)
        skips = sb("skips", [P, ST_TILES, NE], F32, p5)
        texp = sb("texp", [P, ST_TILES], F32, p5)
        trow = sb("trow", [P, ST_TILES], F32, p5)
        route = sem("route")
        pad_set = sem("pad_set")
        pad_out = sem("pad_out")
        w5_in = sem("w5_in")
        w6_in = sem("w6_in")
        w8_in = sem("w8_in")
        folds_done = sem("folds_done")
        fold_set = sem("fold_set")
        const5_set = sem("const5_set")
        k_done = sem("k_done")
        q_done = sem("q_done")
        v5_done = sem("v5_done")
        kv_done = sem("kv_done")
        out5_done = sem("out5_done")
        turned4 = sem("turned4")
        logits_done = sem("logits_done")
        ranks_done = sem("ranks_done")
        kA_set = sem("kA_set")
        qq_set = sem("qq_set")
        xT4_set = sem("xT4_set")
        xn4_kept = sem("xn4_kept")
        lg_set = sem("lg_set")
        rk_set = sem("rk_set")
        row_set = sem("row_set")
        p12_set = sem("p12_set")
        scan_set = sem("scan_set")
        p34_set = sem("p34_set")
        y5_set = sem("y5_set")
        x5_set = sem("x5_set")
        xn4_set = sem("xn4_set")
        choose = sem("choose")
        place = sem("place")
        row_out = [sem("row_out0"), sem("row_out1")]
        ROW_STEPS = 4
        CHOOSE = 5
        PLACE = 5
        RB = 7

        with nc.Block() as block:
            @block.sync
            def _(sp):
                sp.dma_start(wqkvT[:], io["L1_attn_w_qkv"].rearrange("(k p) i -> p k i", p=P)).then_inc(w5_in, 16)
                sp.dma_start(wout1[:], io["L1_attn_w_out"]).then_inc(w5_in, 16)
                sp.dma_start(dft[:], io["dft"].rearrange("k p i -> p k i")).then_inc(w5_in, 16)
                sp.dma_start(gate_w[:], io["L1_ffn_gate_w"]).then_inc(w5_in, 16)
                sp.dma_start(tri[:], io["tri"]).then_inc(w6_in, 16)
                sp.dma_start(cls[:], io["cls"].to_broadcast([P, NE])).then_inc(w6_in, 16)
                sp.dma_start(starts[:], io["starts"].to_broadcast([P, ST_TILES])).then_inc(w6_in, 16)
                sp.dma_start(firsts[:], io["firsts"].to_broadcast([P, NE])).then_inc(w6_in, 16)
                sp.dma_start(ids[:], io["ids"]).then_inc(w6_in, 16)
                sp.dma_start(sgu[:, 0:F1], io["L1_ffn_shared_gate"]).then_inc(w8_in, 16)
                sp.dma_start(sgu[:, F1:2 * F1], io["L1_ffn_shared_up"]).then_inc(w8_in, 16)
                sp.dma_start(sdn[:], io["L1_ffn_shared_down"].rearrange("(k p) o -> p k o", p=P)).then_inc(w8_in, 16)
                g = wgu[:].rearrange("p (e u f) -> p e u f", e=NE, u=2)
                sp.dma_start(g[:, :, 0, :], io["L1_ffn_r_gate"].rearrange("e p f -> p e f")).then_inc(w8_in, 16)
                sp.dma_start(g[:, :, 1, :], io["L1_ffn_r_up"].rearrange("e p f -> p e f")).then_inc(w8_in, 16)
                sp.dma_start(wdn[:].rearrange("p (e k o) -> p e k o", e=NE, k=FB1),
                             io["L1_ffn_r_down"].rearrange("e (k p) o -> p e k o", p=P)).then_inc(w8_in, 16)
                sp.wait_ge(pad_set, 3)
                sp.dma_start(row_scr[NE * REGION:NE * REGION + P], pad[:]).then_inc(pad_out, 16)
                for e in range(NE):
                    end = sp.value_load(end_i[0:1, e:e + 1], min_val=0, max_val=NE * REGION)
                    sp.dma_start(row_scr[ds(end, P)], pad[:]).then_inc(pad_out, 16)
                sp.wait_ge(pad_out, (NE + 1) * 16)

            @block.tensor
            def _(pe):
                pe.wait_ge(w5_in, 64)
                for n, (w, d) in enumerate(((1, 0), (2, 0), (2, 1), (0, 0), (0, 1))):
                    pe.matmul(PS[:, n // 4, (n % 4) * P:(n % 4 + 1) * P], wqkvT[:, w, :], dft[:, d, :],
                              start=True, stop=True)
                for n in (5, 6):
                    mm = pe.matmul(PS[:, n // 4, (n % 4) * P:(n % 4 + 1) * P], dft[:, n - 1, :], wout1[:],
                                   start=True, stop=True)
                mm.then_inc(folds_done, 1)
                pe.wait_ge(fold_set, 1)

                def project(c, s):
                    xT = chunk_of(XT, c)
                    if late(c, 1):
                        pe.wait_ge(kA_set, c)
                    if late(c, 5):
                        pe.wait_ge(xT4_set, c - 4)
                    pe.matmul(PS[:, 0, :], fold[:, 0, :], xT, start=True, stop=True).then_inc(k_done, 1)
                    if late(c, 1):
                        pe.wait_ge(qq_set, c)
                    pe.matmul(PS[:, 3, :], fold[:, 3, :], xT, start=True, stop=True)
                    pe.matmul(PS[:, 4, :], fold[:, 4, :], xT, start=True, stop=True).then_inc(q_done, 1)
                    if late(c, 1):
                        pe.wait_ge(p12_set, 2 * c)
                    pe.matmul(PS[:, 1, :], fold[:, 1, :], xT, start=True, stop=True)
                    pe.matmul(PS[:, 2, :], fold[:, 2, :], xT, start=True, stop=True).then_inc(v5_done, 1)

                def combine(c, s):
                    pe.wait_ge(p12_set, 2 * c + 2)
                    if late(c, 1):
                        pe.wait_ge(scan_set, c)
                    pe.matmul(PS[:, 5, :], dft[:, 2, :], p12[:, s, 0, :], start=True, stop=False)
                    pe.matmul(PS[:, 5, :], dft[:, 3, :], p12[:, s, 1, :], start=False, stop=True).then_inc(kv_done, 1)

                def output(c, s):
                    pe.wait_ge(p34_set, 2 * c + 2)
                    if late(c, 1):
                        pe.wait_ge(y5_set, c)
                    for t in range(NT):
                        for k in range(2):
                            mm = pe.matmul(PS[:, 6, t * P:(t + 1) * P], p34[:, s, k, t * P:(t + 1) * P],
                                           fold[:, 5 + k, :], start=(k == 0), stop=(k == 1))
                    mm.then_inc(out5_done, 1)

                def turn(c, s):
                    pe.wait_ge(xn4_set, c + 1)
                    pe.wait_ge(kA_set, min(c + 5, NCH) if isinstance(c, int) else c + 5)
                    if isinstance(c, int) and c + 5 > NCH:
                        pe.wait_ge(xT4_set, c)
                    for t in range(NT):
                        mm = pe.transpose(PS[:, 0, t * P:(t + 1) * P], xn4[:, s, t * P:(t + 1) * P], idf[:])
                    mm.then_inc(turned4, 1)

                def logits(c, s):
                    pe.wait_ge(xT4_set, c + 1)
                    if late(c, 1):
                        pe.wait_ge(rk_set, c)
                    for t in range(NT):
                        mm = pe.matmul(PS[:, RB, t * NE:(t + 1) * NE], xT4[:, s, t * P:(t + 1) * P],
                                       gate_w[:], start=True, stop=True)
                    mm.then_inc(logits_done, 1)

                def ranks(c, s):
                    pe.wait_ge(choose, c * CHOOSE + CHOOSE)
                    if isinstance(c, int) and c == 0:
                        pe.wait_ge(const5_set, 4)
                    oh = ohb[:, s].rearrange("p t e -> p (t e)")
                    pe.matmul(PS[:, RB, 0:NT * NE], trib[:], oh, start=True, stop=False)
                    for t in range(1, NT):
                        pe.matmul(PS[:, RB, t * NE:NT * NE], onesb[:], oh[:, 0:(NT - t) * NE],
                                  start=False, stop=(t == NT - 1))
                    for t in range(NT):
                        mm = pe.matmul(PS[:, RB, NT * NE:(NT + 1) * NE], onesb[:], oh[:, t * NE:(t + 1) * NE],
                                       start=(t == 0), stop=(t == NT - 1))
                    mm.then_inc(ranks_done, 1)
                run_stages(pe, NCH, [(0, project), (6, ranks), (4, turn), (1, combine), (2, output), (5, logits)])

            @block.scalar
            def _(act):
                act.wait_ge(folds_done, 1)
                act.copy(fold[:, 0:7, :], PS[:, 0:2, :].rearrange("p a (b e) -> p (a b) e", e=P)[:, 0:7, :])\
                   .then_inc(fold_set, 1)
                act.wait_ge(w6_in, 80)

                def copy_k(c, s):
                    act.wait_ge(k_done, c + 1)
                    if late(c, 2):
                        act.wait_ge(p12_set, 2 * c - 2)
                    act.copy(kA[:, s, :], PS[:, 0, :]).then_inc(kA_set, 1)

                def copy_q(c, s):
                    act.wait_ge(q_done, c + 1)
                    if late(c, 2):
                        act.wait_ge(p34_set, 2 * c - 2)
                    act.copy(qq[:, s], PS[:, 3:5, :]).then_inc(qq_set, 1)

                def copy_xT(c, s):
                    act.wait_ge(turned4, c + 1)
                    if late(c, 2):
                        act.wait_ge(logits_done, c - 1)
                    act.copy(xT4[:, s, :], PS[:, 0, :]).then_inc(xT4_set, 1)
                    act.wait_ge(xn4_set, c + 1)
                    act.copy(chunk_of(AO, c), xn4[:, s, :]).then_inc(xn4_kept, 1)

                def out_rows(c, s):
                    act.wait_ge(lnC["steps"], (c + 1) * LN_SCALED)
                    if late(c, 1):
                        act.wait_ge(x5_set, c)
                    for t in range(NT):
                        ins = act.activation(y5[:, t * P:(t + 1) * P], PS[:, 6, t * P:(t + 1) * P], ACT.Identity,
                                             bias=lnC["nb"][:, t:t + 1], scale=lnC["rs"][:, t:t + 1])
                    ins.then_inc(y5_set, 1)

                def moe_rows(c, s):
                    act.wait_ge(ln4["steps"], (c + 1) * LN_SCALED)
                    if late(c, 2):
                        act.wait_ge(turned4, c - 1)
                        act.wait_ge(xn4_kept, c - 1)
                    for t in range(NT):
                        ins = act.activation(xn4[:, s, t * P:(t + 1) * P], tile_of(X, c, t), ACT.Identity,
                                             bias=ln4["nb"][:, t:t + 1], scale=ln4["rs"][:, t:t + 1])
                    ins.then_inc(xn4_set, 1)

                def copy_logits(c, s):
                    act.wait_ge(logits_done, c + 1)
                    if late(c, 2):
                        act.wait_ge(choose, (c - 1) * CHOOSE)
                    act.copy(lg[:, s].rearrange("p t e -> p (t e)"), PS[:, RB, 0:NT * NE]).then_inc(lg_set, 1)

                def copy_ranks(c, s):
                    act.wait_ge(ranks_done, c + 1)
                    if late(c, 2):
                        act.wait_ge(place, (c - 1) * PLACE)
                    act.copy(rk[:, s, :], PS[:, RB, 0:(NT + 1) * NE]).then_inc(rk_set, 1)

                def assemble(c, s):
                    act.wait_ge(x5_set, c + 1)
                    act.wait_ge(xn4_kept, c + 1)
                    if late(c, 2):
                        act.wait_ge(row_out[s], (c - s) * 32)
                    act.copy(row[:, s, :, 0:E],
                             chunk_of(AO, c).rearrange("p (t e) -> p t e", t=NT)).then_inc(row_set, 1)
                    act.copy(row[:, s, :, E:2 * E],
                             chunk_of(X, c).rearrange("p (t e) -> p t e", t=NT)).then_inc(row_set, 1)
                    act.copy(row[:, s, :, 2 * E + 1], ids[:, ds(c * NT, NT)]).then_inc(row_set, 1)
                    act.wait_ge(choose, c * CHOOSE + 1)
                    act.activation(row[:, s, :, 2 * E], mx[:, s, :], ACT.Sigmoid).then_inc(row_set, 1)
                run_stages(act, NCH, [(0, copy_k), (3, out_rows), (0, copy_q), (6, copy_ranks), (4, copy_xT),
                                      (5, copy_logits), (3, moe_rows), (6, assemble)])

            @block.gpsimd
            def _(pool):
                def scatter(c, s):
                    pool.wait_ge(row_set, c * ROW_STEPS + ROW_STEPS)
                    settled(pool)
                    pool.wait_ge(place, c * PLACE + PLACE)
                    settled(pool)
                    for t in range(NT):
                        pool.indirect_dma_start(out=row_scr,
                                                out_offset=bass.IndirectOffsetOnAxis(idx[:, s, t:t + 1], 0),
                                                in_=row[:, s, t, :], in_offset=None).then_inc(row_out[s], 16)

                def spectra(c, s):
                    pool.wait_ge(scan_set, c + 1)
                    pool.wait_ge(qq_set, c + 1)
                    if late(c, 2):
                        pool.wait_ge(out5_done, c - 1)
                    for k in range(2):
                        pool.tensor_tensor(p34[:, s, k, :], qq[:, s, k, :], csum[:, s, :],
                                           ALU.mult).then_inc(p34_set, 1)
                run_stages(pool, NCH, [(3, lambda c, s: rstd(ln4)(pool, c)), (1, spectra),
                                       (2, lambda c, s: rstd(lnC)(pool, c)), (7, scatter)])
                for s in range(2):
                    pool.wait_ge(row_out[s], NCH // 2 * NT * 16)

            @block.vector
            def _(dve):
                dve.memset(ones5[:], 1.0).then_inc(const5_set, 1)
                dve.memset(onesb[:], 1.0).then_inc(const5_set, 1)
                dve.wait_ge(w6_in, 80)
                dve.tensor_copy(trib[:], tri[:]).then_inc(const5_set, 1)
                dve.tensor_copy(filled[:], firsts[:]).then_inc(const5_set, 1)
                dve.wait_ge(const5_set, 4)

                def products(c, s):
                    dve.wait_ge(kA_set, c + 1)
                    dve.wait_ge(v5_done, c + 1)
                    if late(c, 2):
                        dve.wait_ge(kv_done, c - 1)
                    for k in range(2):
                        dve.tensor_tensor(p12[:, s, k, :], PS[:, 1 + k, :], kA[:, s, :], ALU.mult).then_inc(p12_set, 1)

                def scan(c, s):
                    dve.wait_ge(kv_done, c + 1)
                    if late(c, 2):
                        dve.wait_ge(p34_set, 2 * c - 2)
                    dve.tensor_tensor_scan(csum[:, s, :], ones5[:], PS[:, 5, :], 0.0, ALU.mult,
                                           ALU.add).then_inc(scan_set, 1)

                def out_stats(c, s):
                    dve.wait_ge(out5_done, c + 1)
                    ln_stats(dve, c, lnC, lambda t: PS[:, 6, t * P:(t + 1) * P])
                    ln_aggregate(dve, c, lnC)

                def residual(c, s):
                    dve.wait_ge(y5_set, c + 1)
                    dve.tensor_tensor(chunk_of(X, c), chunk_of(X, c), y5[:], ALU.add).then_inc(x5_set, 1)

                def moe_stats(c, s):
                    dve.wait_ge(x5_set, c + 1)
                    ln_stats(dve, c, ln4, lambda t: tile_of(X, c, t))
                    ln_aggregate(dve, c, ln4)

                cls_te = cls[:].unsqueeze(1).broadcast_to([P, NT, NE])

                def choose_step(k):
                    def stage(c, s):
                        if k == 0:
                            dve.wait_ge(lg_set, c + 1)
                            if late(c, 2):
                                dve.wait_ge(row_set, (c - 1) * ROW_STEPS)
                            ins = dve.tensor_reduce(mx[:, s, :], lg[:, s], AX_X, ALU.max)
                        else:
                            dve.wait_ge(choose, c * CHOOSE + k)
                        if k == 1:
                            ins = dve.tensor_tensor(cand[:], lg[:, s], mx[:, s, :].unsqueeze(2)
                                                    .broadcast_to([P, NT, NE]), ALU.is_equal)
                        if k == 2:
                            ins = dve.tensor_tensor(cand[:], cand[:], cls_te, ALU.mult)
                        if k == 3:
                            ins = dve.tensor_reduce(best[:], cand[:], AX_X, ALU.max)
                        if k == 4:
                            if late(c, 2):
                                dve.wait_ge(ranks_done, c - 1)
                            ins = dve.tensor_tensor(ohb[:, s], best[:].unsqueeze(2).broadcast_to([P, NT, NE]),
                                                    cls_te, ALU.is_equal)
                        ins.then_inc(choose, 1)
                    return stage

                def place_step(k):
                    def stage(c, s):
                        rank = rk[:, s, 0:NT * NE].rearrange("p (t e) -> p t e", t=NT)
                        if k == 0:
                            dve.wait_ge(rk_set, c + 1)
                            if late(c, 1):
                                dve.wait_ge(place, c * PLACE)
                            ins = dve.tensor_tensor(where[:], rank, filled[:].unsqueeze(1)
                                                    .broadcast_to([P, NT, NE]), ALU.add)
                        else:
                            dve.wait_ge(place, c * PLACE + k)
                        if k == 1:
                            ins = dve.tensor_tensor(where[:], where[:], ohb[:, s], ALU.mult)
                        if k == 2:
                            ins = dve.tensor_reduce(posf[:], where[:], AX_X, ALU.add)
                        if k == 3:
                            if late(c, 2):
                                dve.wait_ge(row_out[s], (c - s) * 32)
                            ins = dve.tensor_copy(idx[:, s, :], posf[:])
                        if k == 4:
                            ins = dve.tensor_tensor(filled[:], filled[:], rk[:, s, NT * NE:(NT + 1) * NE], ALU.add)
                        ins.then_inc(place, 1)
                    return stage
                routing = [pair for k in range(CHOOSE) for pair in ((6, place_step(k)), (5, choose_step(k)))]
                run_stages(dve, NCH, [(0, products), (3, residual), (3, moe_stats), (1, scan), (2, out_stats),
                                      (3, lambda c, s: ln_bias(dve, c, ln4))]
                           + routing + [(2, lambda c, s: ln_bias(dve, c, lnC))])

                dve.wait_ge(place, NCH * PLACE)
                n = [0]

                def then(ins):
                    n[0] += 1
                    ins.then_inc(route, 1)
                    dve.wait_ge(route, n[0])

                def over(col):
                    return col.unsqueeze(1).broadcast_to([P, ST_TILES, NE])

                dve.tensor_copy(end_i[:], filled[:]).then_inc(pad_set, 1)
                dve.memset(pad[:], 0.0).then_inc(pad_set, 1)
                dve.wait_ge(pad_set, 2)
                dve.memset(pad[:, 2 * E + 1:], float(TILES * P)).then_inc(pad_set, 1)
                then(dve.memset(ones6[:], 1.0))
                then(dve.tensor_tensor(count[:], filled[:], firsts[:], ALU.subtract))
                then(dve.tensor_scalar(count[:], count[:], float(P - 1), None, ALU.add))
                then(dve.tensor_copy(cnti[:, 0, :], count[:]))
                then(dve.tensor_scalar(cnti[:, 1, :], cnti[:, 0, :], 7, 7, ALU.arith_shift_right,
                                       ALU.logical_shift_left))
                then(dve.tensor_copy(padded[:], cnti[:, 1, :]))
                then(dve.tensor_tensor_scan(pad_ends[:], ones6[:], padded[:], 0.0, ALU.mult, ALU.add))
                then(dve.tensor_scalar(skip[:], padded[:], -1.0, float(REGION), ALU.mult, ALU.add))
                then(dve.memset(skip[:, NE - 1:NE], float(NE * REGION)))
                starts_te = starts[:].unsqueeze(2).broadcast_to([P, ST_TILES, NE])
                then(dve.tensor_tensor(past[:], starts_te, over(pad_ends[:]), ALU.is_ge))
                then(dve.tensor_tensor(skips[:], past[:], over(skip[:]), ALU.mult))
                then(dve.tensor_reduce(texp[:], past[:], AX_X, ALU.add))
                then(dve.tensor_reduce(trow[:], skips[:], AX_X, ALU.add))
                then(dve.tensor_scalar(tile_e[:], texp[:], float(NE - 1), None, ALU.min))
                then(dve.tensor_tensor(trow[:], trow[:], starts[:], ALU.add))
                then(dve.tensor_scalar(tile_row[:], trow[:], float(NE * REGION), None, ALU.min))
        p5.close()

        RING = 12
        p7 = ExitStack()
        rows7 = sb("rows7", [P, RING, ROW], F32, p7)
        xs7 = sb("xs7", [P, 2, E], F32, p7)
        idx7 = sb("idx7", [P, RING], U32, p7)
        xT7 = sb("xT7", [P, 2, 2, P], F32, p7)
        g7 = sb("g7", [P, 2, 2, F1], F32, p7)
        h7 = sb("h7", [P, 2, 2, F1], F32, p7)
        hT7 = sb("hT7", [P, 2, 2 * FB1, P], F32, p7)
        st7 = sb("st7", [P, 2, 6], F32, p7)
        mv7 = sb("mv7", [P, 2, 2], F32, p7)
        ve7 = sb("ve7", [P, 2], F32, p7)
        rs7 = sb("rs7", [P, 2], F32, p7)
        o7 = sb("o7", [P, 4, E], F32, p7)
        row_in = [sem(f"row_in{k}") for k in range(RING)]
        in7_set = sem("in7_set")
        turned7 = sem("turned7")
        xT7_set = sem("xT7_set")
        gu7_done = sem("gu7_done")
        g7_set = sem("g7_set")
        h7_set = sem("h7_set")
        h7_turned = sem("h7_turned")
        hT7_set = sem("hT7_set")
        y7_done = sem("y7_done")
        ln7 = sem("ln7")
        rs7_set = sem("rs7_set")
        n7_set = sem("n7_set")
        o7_set = sem("o7_set")
        o7_out = [sem(f"o7_out{k}") for k in range(4)]
        out_rows = out.rearrange("b s e -> (b s) e")
        Y_BANKS = (1, 7)

        with nc.Block() as block:
            @block.sync
            def _(sp):
                def load(j, k):
                    r = sp.value_load(tile_row[0:1, ds(j, 1)], min_val=0, max_val=NE * REGION)
                    if late(j, RING):
                        sp.wait_ge(o7_set, j - (RING - 1))
                    sp.dma_start(rows7[:, k, :], row_scr[ds(r, P)]).then_inc(row_in[k], 16)
                run_stages(sp, ST_TILES, [(0, load)], RING)

            @block.tensor
            def _(pe):
                pe.wait_ge(w8_in, 96)

                def turn_x(j, k):
                    pe.wait_ge(in7_set, 2 * j + 2)
                    if late(j, 1):
                        pe.wait_ge(xT7_set, j)
                    pe.transpose(PS[:, 0, 0:P], rows7[:, k, 0:E], idf[:])
                    pe.transpose(PS[:, 0, P:2 * P], xs7[:, k % 2, :], idf[:]).then_inc(turned7, 1)

                def expand(j, k):
                    s = k % 2
                    e = pe.value_load(tile_e[0:1, ds(j, 1)], min_val=0, max_val=NE - 1)
                    pe.wait_ge(xT7_set, j + 1)
                    if late(j, 2):
                        pe.wait_ge(h7_set, j - 1)
                    pe.matmul(PS[:, 2 + 2 * s, :], xT7[:, s, 0, :], sgu[:], start=True, stop=True)
                    pe.matmul(PS[:, 3 + 2 * s, :], xT7[:, s, 1, :], wgu[:, ds(e * (2 * F1), 2 * F1)],
                              start=True, stop=True).then_inc(gu7_done, 1)

                def turn_h(j, k):
                    pe.wait_ge(h7_set, j + 1)
                    if late(j, 1):
                        pe.wait_ge(hT7_set, j)
                    for u in range(2):
                        for f in range(FB1):
                            n = u * FB1 + f
                            mm = pe.transpose(PS[:, 6, n * P:(n + 1) * P], h7[:, k % 2, u, f * P:(f + 1) * P], idf[:])
                    mm.then_inc(h7_turned, 1)

                def reduce(j, k):
                    s = k % 2
                    e = pe.value_load(tile_e[0:1, ds(j, 1)], min_val=0, max_val=NE - 1)
                    pe.wait_ge(hT7_set, j + 1)
                    if late(j, 2):
                        pe.wait_ge(n7_set, j - 1)
                    for f in range(FB1):
                        pe.matmul(PS[:, Y_BANKS[s], 0:E], hT7[:, s, f, :], sdn[:, f, :], start=(f == 0), stop=False)
                    for f in range(FB1):
                        mm = pe.matmul(PS[:, Y_BANKS[s], 0:E], hT7[:, s, FB1 + f, :],
                                       wdn[:, ds(e * (FB1 * E) + f * E, E)], start=False, stop=(f == FB1 - 1))
                    mm.then_inc(y7_done, 1)
                run_stages(pe, ST_TILES, [(2, turn_x), (5, turn_h), (6, reduce), (3, expand)], RING)

            @block.scalar
            def _(act):
                def copy_xT(j, k):
                    act.wait_ge(turned7, j + 1)
                    if late(j, 2):
                        act.wait_ge(gu7_done, j - 1)
                    act.copy(xT7[:, k % 2].rearrange("p u t -> p (u t)"), PS[:, 0, 0:2 * P]).then_inc(xT7_set, 1)

                def silus(j, k):
                    s = k % 2
                    act.wait_ge(gu7_done, j + 1)
                    if late(j, 2):
                        act.wait_ge(h7_set, j - 1)
                    act.activation(g7[:, s], PS[:, 2 + 2 * s:4 + 2 * s, 0:F1], ACT.Silu).then_inc(g7_set, 1)

                def copy_hT(j, k):
                    act.wait_ge(h7_turned, j + 1)
                    if late(j, 2):
                        act.wait_ge(y7_done, j - 1)
                    act.copy(hT7[:, k % 2].rearrange("p n t -> p (n t)"), PS[:, 6, :]).then_inc(hT7_set, 1)
                run_stages(act, ST_TILES, [(4, silus), (2, copy_xT), (5, copy_hT)], RING)

            @block.gpsimd
            def _(pool):
                def inverse_std(j, k):
                    s = k % 2
                    pool.wait_ge(ln7, 3 * j + 3)
                    pool.tensor_tensor(rs7[:, s:s + 1], ve7[:, s:s + 1], neg_half[:, 0:1],
                                       ALU.pow).then_inc(rs7_set, 1)

                def scatter(j, k):
                    pool.wait_ge(o7_set, j + 1)
                    settled(pool)
                    pool.indirect_dma_start(out=out_rows, out_offset=bass.IndirectOffsetOnAxis(idx7[:, k:k + 1], 0),
                                            in_=o7[:, k % 4, :], in_offset=None, bounds_check=TILES * P - 1,
                                            oob_is_err=False).then_inc(o7_out[k % 4], 16)
                run_stages(pool, ST_TILES, [(7, inverse_std), (8, scatter)], RING)
                for k in range(4):
                    pool.wait_ge(o7_out[k], ST_TILES // 4 * 16)

            @block.vector
            def _(dve):
                def scale(j, k):
                    dve.wait_ge(row_in[k], (j - k) // RING * 16 + 16)
                    if late(j, 2):
                        dve.wait_ge(turned7, j - 1)
                    dve.tensor_scalar(xs7[:, k % 2, :], rows7[:, k, 0:E], rows7[:, k, 2 * E:2 * E + 1], None,
                                      ALU.mult).then_inc(in7_set, 1)
                    dve.tensor_copy(idx7[:, k:k + 1], rows7[:, k, 2 * E + 1:2 * E + 2]).then_inc(in7_set, 1)

                def gate(j, k):
                    s = k % 2
                    dve.wait_ge(g7_set, j + 1)
                    if late(j, 2):
                        dve.wait_ge(h7_turned, j - 1)
                    dve.tensor_tensor(h7[:, s], PS[:, 2 + 2 * s:4 + 2 * s, F1:2 * F1], g7[:, s],
                                      ALU.mult).then_inc(h7_set, 1)

                def stats(j, k):
                    s = k % 2
                    dve.wait_ge(y7_done, j + 1)
                    settled(dve)
                    dve.bn_stats(st7[:, s, :], PS[:, Y_BANKS[s], 0:E]).then_inc(ln7, 1)
                    dve.wait_ge(ln7, 3 * j + 1)
                    settled(dve)
                    dve.bn_aggr(mv7[:, s, :], st7[:, s, :]).then_inc(ln7, 1)
                    dve.wait_ge(ln7, 3 * j + 2)
                    dve.tensor_scalar(ve7[:, s:s + 1], mv7[:, s, 1:2], EPS, None, ALU.add).then_inc(ln7, 1)

                def finish(j, k):
                    s = k % 2
                    dve.wait_ge(rs7_set, j + 1)
                    if late(j, 4):
                        dve.wait_ge(o7_out[k % 4], (j - k % 4) * 4)
                    dve.tensor_scalar(o7[:, k % 4, :], PS[:, Y_BANKS[s], 0:E], mv7[:, s, 0:1], rs7[:, s:s + 1],
                                      ALU.subtract, ALU.mult).then_inc(n7_set, 1)
                    dve.wait_ge(n7_set, j + 1)
                    dve.tensor_tensor(o7[:, k % 4, :], o7[:, k % 4, :], rows7[:, k, E:2 * E],
                                      ALU.add).then_inc(o7_set, 1)
                run_stages(dve, ST_TILES, [(8, finish), (4, gate), (1, scale), (7, stats)], RING)
        p7.close()


def _constants():
    import numpy as np

    n, f = np.arange(16), np.arange(9)
    ang = 2 * np.pi * np.outer(n, f) / 16
    fwd = np.zeros((16, 16))
    fwd[:, :9] = np.cos(ang)
    fwd[:, 9:] = -np.sin(ang)[:, 1:8]
    swp = np.zeros((16, 16))
    swp[:, 1:8] = fwd[:, 9:]
    swp[:, 9:] = fwd[:, 1:8]
    c1, c2 = np.zeros((16, 16)), np.zeros((16, 16))
    g1, g2 = np.zeros((16, 16)), np.zeros((16, 16))
    for k in range(9):
        w = 1.0 if k in (0, 8) else 2.0
        c1[k, k] = 1
        g1[k] = w * np.cos(ang[:, k]) / 16
        if w == 2:
            c1[8 + k, k] = -1
            c2[k, 8 + k] = c2[8 + k, 8 + k] = 1
            g1[8 + k] = g1[k]
            g2[k] = 2 * np.sin(ang[:, k]) / 16
            g2[8 + k] = -g2[k]
    heads = np.eye(8)
    mats = [fwd, swp, c1, c2, g1.T, g2.T]
    return {
        "ident": np.eye(128, dtype=np.float32),
        "tri": np.triu(np.ones((128, 128), np.float32), 1),
        "dft": np.stack([np.kron(heads, m) for m in mats]).astype(np.float32),
        "cls": (8 - np.arange(8, dtype=np.float32)).reshape(1, 8),
        "firsts": (np.arange(8, dtype=np.float32) * (64 * 128 + 128)).reshape(1, 8),
        "ids": (np.arange(64)[None, :] * 128 + np.arange(128)[:, None]).astype(np.float32),
        "starts": (128 * np.arange(72, dtype=np.float32)).reshape(1, 72),
    }


def _layout(inputs):
    import numpy as np

    a = {k: np.asarray(v) for k, v in inputs.items()}
    turned = ["L0_attn_q_w", "L0_attn_k_w", "L0_attn_v_w", "L0_attn_out_w", "L0_ffn_w1_w", "L0_ffn_w2_w",
              "L0_ffn_h1_w", "L0_ffn_h2_w", "L0_ffn_w3_w", "L1_attn_w_qkv", "L1_ffn_gate_w",
              "L1_ffn_shared_gate", "L1_ffn_shared_up", "L1_ffn_shared_down"]
    for k in turned:
        a[k] = a[k].T
    for k in ("L1_ffn_r_gate", "L1_ffn_r_up", "L1_ffn_r_down"):
        a[k] = a[k].transpose(0, 2, 1)
    for k in ("L0_ffn_w1_s", "L0_ffn_w2_s", "L0_ffn_h1_s", "L0_ffn_h2_s"):
        a[k] = a[k].reshape(-1, 128).T
    for k in ("L0_attn_out_b", "L0_ffn_w3_s"):
        a[k] = a[k].reshape(1, -1)
    return a


def kernel(**inputs):
    import numpy as _np
    import concourse.bacc as _bacc
    from concourse import mybir as _mybir
    from concourse.bass_utils import run_bass_kernel_spmd as _run

    nc = _bacc.Bacc("TRN2", target_bir_lowering=False, num_devices=1)
    arrays, aps = {}, {}
    for name, a in {**_layout(inputs), **_constants()}.items():
        a = _np.ascontiguousarray(a)
        arrays[f"in_{name}"] = a
        aps[name] = nc.dram_tensor(f"in_{name}", a.shape, _mybir.dt.from_np(a.dtype), kind="ExternalInput").ap()
    out = nc.dram_tensor("out_0", aps["L0_attn_x"].shape, _mybir.dt.from_np(_np.dtype("float32")),
                         kind="ExternalOutput").ap()
    block_kernel(nc, aps, out)
    r = _run(nc, [arrays], core_ids=[0])
    return r.results[0]["out_0"]
```
